# Optimizing a Trainium2 kernel written in Bass

```python
import numpy as np
import jax
import jax.numpy as jnp

def _softmax(x, axis=-1):
    return jax.nn.softmax(x, axis=axis)

def _gelu(x):
    return jax.nn.gelu(x, approximate=True)

def _silu(x):
    return jax.nn.silu(x)

def _sigmoid(x):
    return jax.nn.sigmoid(x)

def _layernorm(x, axis=-1, eps=1e-05):
    m = jnp.mean(x, axis=axis, keepdims=True)
    v = jnp.var(x, axis=axis, keepdims=True)
    return (x - m) / jnp.sqrt(v + eps)

def _scatter_add(tgt, idx, src, axis=0):
    return tgt.at[idx].add(src)

def _segment_sum(src, seg, n):
    return jax.ops.segment_sum(src, seg, n)
kernel_name = 'mk_conv_preact_d4_conv_nchw384_r2_9b6290'

def setup_inputs(seed: int=0):
    np.random.seed(seed)
    _w = jnp.asarray

    def _rec_inputs():
        import jax
        import jax.numpy as jnp
        _gk = jax.random.key(seed)
        x = -0.0002221 + 1 * jax.random.normal(jax.random.fold_in(_gk, 1), (16, 192, 32, 32), jnp.float32)
        return x
    x = _rec_inputs()

    def _L0_conv_setup():
        import jax, jax.numpy as jnp
        import numpy as np
        EPS = 1e-05

        def _dwconv(x, w, pad):
            return jax.lax.conv_general_dilated(x, w, window_strides=(1, 1), padding=[(pad, pad), (pad, pad)], feature_group_count=w.shape[0], dimension_numbers=('NCHW', 'OIHW', 'NCHW'))

        def _bn(y, g, b, m, v):
            scale = (g / jnp.sqrt(v + EPS))[None, :, None, None]
            shift = (b - m * g / jnp.sqrt(v + EPS))[None, :, None, None]
            return y * scale + shift
        key = jax.random.key(seed)
        ks = jax.random.split(key, 16)
        C, KL, KS = (192, 13, 3)
        N, H, W = (16, 32, 32)
        inp = {'x': jax.random.normal(ks[0], (N, C, H, W), jnp.float32), 'w_large': jax.random.normal(ks[1], (C, 1, KL, KL), jnp.float32) * 0.05, 'w_small': jax.random.normal(ks[2], (C, 1, KS, KS), jnp.float32) * 0.2, 'g_l': jax.random.normal(ks[3], (C,), jnp.float32), 'b_l': jax.random.normal(ks[4], (C,), jnp.float32), 'm_l': jax.random.normal(ks[5], (C,), jnp.float32), 'v_l': jax.random.uniform(ks[6], (C,), jnp.float32, 0.5, 1.5), 'g_s': jax.random.normal(ks[7], (C,), jnp.float32), 'b_s': jax.random.normal(ks[8], (C,), jnp.float32), 'm_s': jax.random.normal(ks[9], (C,), jnp.float32), 'v_s': jax.random.uniform(ks[10], (C,), jnp.float32, 0.5, 1.5), 'g_i': jax.random.normal(ks[11], (C,), jnp.float32), 'b_i': jax.random.normal(ks[12], (C,), jnp.float32), 'm_i': jax.random.normal(ks[13], (C,), jnp.float32), 'v_i': jax.random.uniform(ks[14], (C,), jnp.float32, 0.5, 1.5)}
        return inp
    _L0_conv_all = _L0_conv_setup()
    _L0_conv_in = {k: v for k, v in _L0_conv_all.items() if k in ('w_large', 'w_small', 'g_l', 'b_l', 'm_l', 'v_l', 'g_s', 'b_s', 'm_s', 'v_s', 'g_i', 'b_i', 'm_i', 'v_i')}
    del _L0_conv_all

    def _L1_conv_setup():
        import jax, jax.numpy as jnp
        import numpy as np
        WIN = 7
        HEADS = 6
        key = jax.random.key(seed)
        k0, k1, k2, k3 = jax.random.split(key, 4)
        B, C, H, W = (8, 192, 56, 56)
        x = jax.random.normal(k0, (B, C, H, W), jnp.float32)
        w_qkv = jax.random.normal(k1, (3 * C, C), jnp.float32) * 0.02
        b_qkv = jnp.zeros((3 * C,), jnp.float32)
        w_proj = jax.random.normal(k2, (C, C), jnp.float32) * 0.02
        b_proj = jnp.zeros((C,), jnp.float32)
        bias_table = jax.random.normal(k3, (WIN * WIN, HEADS), jnp.float32) * 0.02
        return {'x': x, 'w_qkv': w_qkv, 'b_qkv': b_qkv, 'w_proj': w_proj, 'b_proj': b_proj, 'bias_table': bias_table}
    _L1_conv_all = _L1_conv_setup()
    _L1_conv_in = {k: v for k, v in _L1_conv_all.items() if k in ('w_qkv', 'b_qkv', 'w_proj', 'b_proj', 'bias_table')}
    del _L1_conv_all

    def _L2_conv_setup():
        import jax, jax.numpy as jnp
        import numpy as np
        DIM = 192
        D_STATE = 16

        def _selective_scan(x_in, delta, A, Bm, Cm, D):
            Bsz, L, dim = x_in.shape
            n = A.shape[1]

            def step(h, inp):
                d_t, x_t, b_t, c_t = inp
                h = jnp.exp(d_t[..., None] * A) * h + (d_t * x_t)[..., None] * b_t[:, None, :]
                y_t = jnp.einsum('bdn,bn->bd', h, c_t)
                return (h, y_t)
            h0 = jnp.zeros((Bsz, dim, n), dtype=x_in.dtype)
            xs = (jnp.swapaxes(delta, 0, 1), jnp.swapaxes(x_in, 0, 1), jnp.swapaxes(Bm, 0, 1), jnp.swapaxes(Cm, 0, 1))
            _, ys = jax.lax.scan(step, h0, xs)
            y = jnp.swapaxes(ys, 0, 1)
            return y + x_in * D
        key = jax.random.key(seed)
        ks = jax.random.split(key, 8)
        B, C, H, W = (4, DIM, 32, 32)
        x = jax.random.normal(ks[0], (B, C, H, W), dtype=jnp.float32)
        P = 2 * DIM + 2 * D_STATE
        W_proj = jax.random.normal(ks[1], (P, DIM), dtype=jnp.float32) * 0.02
        b_proj = jnp.zeros((P,), dtype=jnp.float32)
        A_log = jnp.log(jax.random.uniform(ks[2], (DIM, D_STATE), dtype=jnp.float32) + 0.0001)
        D = jnp.ones((DIM,), dtype=jnp.float32)
        dt_bias = jnp.zeros((DIM,), dtype=jnp.float32)
        W_out = jax.random.normal(ks[3], (DIM, DIM), dtype=jnp.float32) * 0.02
        b_out = jnp.zeros((DIM,), dtype=jnp.float32)
        return {'x': x, 'W_proj': W_proj, 'b_proj': b_proj, 'A_log': A_log, 'D': D, 'dt_bias': dt_bias, 'W_out': W_out, 'b_out': b_out}
    _L2_conv_all = _L2_conv_setup()
    _L2_conv_in = {k: v for k, v in _L2_conv_all.items() if k in ('W_proj', 'b_proj', 'A_log', 'D', 'dt_bias', 'W_out', 'b_out')}
    del _L2_conv_all

    def _L3_conv_setup():
        import jax, jax.numpy as jnp
        import numpy as np
        DIM = 192
        D_STATE = 16

        def _selective_scan(x_in, delta, A, Bm, Cm, D):
            Bsz, L, dim = x_in.shape
            n = A.shape[1]

            def step(h, inp):
                d_t, x_t, b_t, c_t = inp
                h = jnp.exp(d_t[..., None] * A) * h + (d_t * x_t)[..., None] * b_t[:, None, :]
                y_t = jnp.einsum('bdn,bn->bd', h, c_t)
                return (h, y_t)
            h0 = jnp.zeros((Bsz, dim, n), dtype=x_in.dtype)
            xs = (jnp.swapaxes(delta, 0, 1), jnp.swapaxes(x_in, 0, 1), jnp.swapaxes(Bm, 0, 1), jnp.swapaxes(Cm, 0, 1))
            _, ys = jax.lax.scan(step, h0, xs)
            y = jnp.swapaxes(ys, 0, 1)
            return y + x_in * D
        key = jax.random.key(seed)
        ks = jax.random.split(key, 8)
        B, C, H, W = (4, DIM, 32, 32)
        x = jax.random.normal(ks[0], (B, C, H, W), dtype=jnp.float32)
        P = 2 * DIM + 2 * D_STATE
        W_proj = jax.random.normal(ks[1], (P, DIM), dtype=jnp.float32) * 0.02
        b_proj = jnp.zeros((P,), dtype=jnp.float32)
        A_log = jnp.log(jax.random.uniform(ks[2], (DIM, D_STATE), dtype=jnp.float32) + 0.0001)
        D = jnp.ones((DIM,), dtype=jnp.float32)
        dt_bias = jnp.zeros((DIM,), dtype=jnp.float32)
        W_out = jax.random.normal(ks[3], (DIM, DIM), dtype=jnp.float32) * 0.02
        b_out = jnp.zeros((DIM,), dtype=jnp.float32)
        return {'x': x, 'W_proj': W_proj, 'b_proj': b_proj, 'A_log': A_log, 'D': D, 'dt_bias': dt_bias, 'W_out': W_out, 'b_out': b_out}
    _L3_conv_all = _L3_conv_setup()
    _L3_conv_in = {k: v for k, v in _L3_conv_all.items() if k in ('W_proj', 'b_proj', 'A_log', 'D', 'dt_bias', 'W_out', 'b_out')}
    del _L3_conv_all
    return {'x': x, 'L0_conv_w_large': _L0_conv_in['w_large'], 'L0_conv_w_small': _L0_conv_in['w_small'], 'L0_conv_g_l': _L0_conv_in['g_l'], 'L0_conv_b_l': _L0_conv_in['b_l'], 'L0_conv_m_l': _L0_conv_in['m_l'], 'L0_conv_v_l': _L0_conv_in['v_l'], 'L0_conv_g_s': _L0_conv_in['g_s'], 'L0_conv_b_s': _L0_conv_in['b_s'], 'L0_conv_m_s': _L0_conv_in['m_s'], 'L0_conv_v_s': _L0_conv_in['v_s'], 'L0_conv_g_i': _L0_conv_in['g_i'], 'L0_conv_b_i': _L0_conv_in['b_i'], 'L0_conv_m_i': _L0_conv_in['m_i'], 'L0_conv_v_i': _L0_conv_in['v_i'], 'L1_conv_w_qkv': _L1_conv_in['w_qkv'], 'L1_conv_b_qkv': _L1_conv_in['b_qkv'], 'L1_conv_w_proj': _L1_conv_in['w_proj'], 'L1_conv_b_proj': _L1_conv_in['b_proj'], 'L1_conv_bias_table': _L1_conv_in['bias_table'], 'L2_conv_W_proj': _L2_conv_in['W_proj'], 'L2_conv_b_proj': _L2_conv_in['b_proj'], 'L2_conv_A_log': _L2_conv_in['A_log'], 'L2_conv_D': _L2_conv_in['D'], 'L2_conv_dt_bias': _L2_conv_in['dt_bias'], 'L2_conv_W_out': _L2_conv_in['W_out'], 'L2_conv_b_out': _L2_conv_in['b_out'], 'L3_conv_W_proj': _L3_conv_in['W_proj'], 'L3_conv_b_proj': _L3_conv_in['b_proj'], 'L3_conv_A_log': _L3_conv_in['A_log'], 'L3_conv_D': _L3_conv_in['D'], 'L3_conv_dt_bias': _L3_conv_in['dt_bias'], 'L3_conv_W_out': _L3_conv_in['W_out'], 'L3_conv_b_out': _L3_conv_in['b_out']}

def reference(x, L0_conv_w_large, L0_conv_w_small, L0_conv_g_l, L0_conv_b_l, L0_conv_m_l, L0_conv_v_l, L0_conv_g_s, L0_conv_b_s, L0_conv_m_s, L0_conv_v_s, L0_conv_g_i, L0_conv_b_i, L0_conv_m_i, L0_conv_v_i, L1_conv_w_qkv, L1_conv_b_qkv, L1_conv_w_proj, L1_conv_b_proj, L1_conv_bias_table, L2_conv_W_proj, L2_conv_b_proj, L2_conv_A_log, L2_conv_D, L2_conv_dt_bias, L2_conv_W_out, L2_conv_b_out, L3_conv_W_proj, L3_conv_b_proj, L3_conv_A_log, L3_conv_D, L3_conv_dt_bias, L3_conv_W_out, L3_conv_b_out):
    import jax
    import jax.numpy as jnp

    def _L0_conv_ref(x, w_large, w_small, g_l, b_l, m_l, v_l, g_s, b_s, m_s, v_s, g_i, b_i, m_i, v_i):
        import jax, jax.numpy as jnp
        import numpy as np
        EPS = 1e-05

        def _dwconv(x, w, pad):
            return jax.lax.conv_general_dilated(x, w, window_strides=(1, 1), padding=[(pad, pad), (pad, pad)], feature_group_count=w.shape[0], dimension_numbers=('NCHW', 'OIHW', 'NCHW'))

        def _bn(y, g, b, m, v):
            scale = (g / jnp.sqrt(v + EPS))[None, :, None, None]
            shift = (b - m * g / jnp.sqrt(v + EPS))[None, :, None, None]
            return y * scale + shift
        kl = w_large.shape[-1]
        ks = w_small.shape[-1]
        out = _bn(_dwconv(x, w_large, kl // 2), g_l, b_l, m_l, v_l) + _bn(_dwconv(x, w_small, ks // 2), g_s, b_s, m_s, v_s) + _bn(x, g_i, b_i, m_i, v_i)
        return out

    def _L1_conv_ref(x, w_qkv, b_qkv, w_proj, b_proj, bias_table):
        import jax, jax.numpy as jnp
        import numpy as np
        WIN = 7
        HEADS = 6
        B, C, H, W = x.shape
        heads, win = (HEADS, WIN)
        dph = C // heads
        scale = dph ** (-0.5)
        qkv = jnp.einsum('bcij,oc->boij', x, w_qkv) + b_qkv[None, :, None, None]
        q = qkv[:, :C] * scale
        k = qkv[:, C:2 * C]
        v = qkv[:, 2 * C:]
        p = win // 2
        kp = jnp.pad(k, ((0, 0), (0, 0), (p, p), (p, p)))
        vp = jnp.pad(v, ((0, 0), (0, 0), (p, p), (p, p)))
        qh = q.reshape(B, heads, dph, H, W)
        scores = []
        for idx in range(win * win):
            dy, dx = (idx // win, idx % win)
            ks = kp[:, :, dy:dy + H, dx:dx + W].reshape(B, heads, dph, H, W)
            scores.append(jnp.einsum('bhdij,bhdij->bhij', qh, ks))
        attn = jnp.stack(scores, axis=2)
        attn = attn + bias_table.T.reshape(1, heads, win * win, 1, 1) * 0.0
        attn = jax.nn.softmax(attn, axis=2)
        out = jnp.zeros((B, heads, dph, H, W), x.dtype)
        for idx in range(win * win):
            dy, dx = (idx // win, idx % win)
            vs = vp[:, :, dy:dy + H, dx:dx + W].reshape(B, heads, dph, H, W)
            out = out + attn[:, :, idx][:, :, None] * vs
        out = out.reshape(B, C, H, W)
        out = jnp.einsum('bcij,oc->boij', out, w_proj) + b_proj[None, :, None, None]
        return out

    def _L2_conv_ref(x, W_proj, b_proj, A_log, D, dt_bias, W_out, b_out):
        import jax, jax.numpy as jnp
        import numpy as np
        DIM = 192
        D_STATE = 16

        def _selective_scan(x_in, delta, A, Bm, Cm, D):
            Bsz, L, dim = x_in.shape
            n = A.shape[1]

            def step(h, inp):
                d_t, x_t, b_t, c_t = inp
                h = jnp.exp(d_t[..., None] * A) * h + (d_t * x_t)[..., None] * b_t[:, None, :]
                y_t = jnp.einsum('bdn,bn->bd', h, c_t)
                return (h, y_t)
            h0 = jnp.zeros((Bsz, dim, n), dtype=x_in.dtype)
            xs = (jnp.swapaxes(delta, 0, 1), jnp.swapaxes(x_in, 0, 1), jnp.swapaxes(Bm, 0, 1), jnp.swapaxes(Cm, 0, 1))
            _, ys = jax.lax.scan(step, h0, xs)
            y = jnp.swapaxes(ys, 0, 1)
            return y + x_in * D
        B, C, H, W = x.shape
        L = H * W
        seq = x.reshape(B, C, L).transpose(0, 2, 1)
        proj = seq @ W_proj.T + b_proj
        x_in = proj[..., :DIM]
        delta = proj[..., DIM:2 * DIM]
        Bm = proj[..., 2 * DIM:2 * DIM + D_STATE]
        Cm = proj[..., 2 * DIM + D_STATE:]
        A = -jnp.exp(A_log)
        delta = jax.nn.softplus(delta + dt_bias)
        y = _selective_scan(x_in, delta, A, Bm, Cm, D)
        out = y @ W_out.T + b_out
        return out.transpose(0, 2, 1).reshape(B, C, H, W)

    def _L3_conv_ref(x, W_proj, b_proj, A_log, D, dt_bias, W_out, b_out):
        import jax, jax.numpy as jnp
        import numpy as np
        DIM = 192
        D_STATE = 16

        def _selective_scan(x_in, delta, A, Bm, Cm, D):
            Bsz, L, dim = x_in.shape
            n = A.shape[1]

            def step(h, inp):
                d_t, x_t, b_t, c_t = inp
                h = jnp.exp(d_t[..., None] * A) * h + (d_t * x_t)[..., None] * b_t[:, None, :]
                y_t = jnp.einsum('bdn,bn->bd', h, c_t)
                return (h, y_t)
            h0 = jnp.zeros((Bsz, dim, n), dtype=x_in.dtype)
            xs = (jnp.swapaxes(delta, 0, 1), jnp.swapaxes(x_in, 0, 1), jnp.swapaxes(Bm, 0, 1), jnp.swapaxes(Cm, 0, 1))
            _, ys = jax.lax.scan(step, h0, xs)
            y = jnp.swapaxes(ys, 0, 1)
            return y + x_in * D
        B, C, H, W = x.shape
        L = H * W
        seq = x.reshape(B, C, L).transpose(0, 2, 1)
        proj = seq @ W_proj.T + b_proj
        x_in = proj[..., :DIM]
        delta = proj[..., DIM:2 * DIM]
        Bm = proj[..., 2 * DIM:2 * DIM + D_STATE]
        Cm = proj[..., 2 * DIM + D_STATE:]
        A = -jnp.exp(A_log)
        delta = jax.nn.softplus(delta + dt_bias)
        y = _selective_scan(x_in, delta, A, Bm, Cm, D)
        out = y @ W_out.T + b_out
        return out.transpose(0, 2, 1).reshape(B, C, H, W)

    def _gn(v, G=32, eps=1e-05):
        B_, C_, H_, W_ = v.shape
        g = v.reshape(B_, G, C_ // G, H_, W_)
        m = jnp.mean(g, axis=(2, 3, 4), keepdims=True)
        s = jnp.var(g, axis=(2, 3, 4), keepdims=True)
        return ((g - m) / jnp.sqrt(s + eps)).reshape(v.shape)

    def _ln_c(v, eps=1e-06):
        m = jnp.mean(v, axis=1, keepdims=True)
        s = jnp.var(v, axis=1, keepdims=True)
        return (v - m) / jnp.sqrt(s + eps)

    def _ln_t(v, eps=1e-05):
        m = jnp.mean(v, axis=-1, keepdims=True)
        s = jnp.var(v, axis=-1, keepdims=True)
        return (v - m) / jnp.sqrt(s + eps)

    def _to_tokens(v):
        B_, C_, H_, W_ = v.shape
        return v.reshape(B_, C_, H_ * W_).transpose(0, 2, 1)

    def _from_tokens(t, like):
        B_, C_, H_, W_ = like.shape
        return t.transpose(0, 2, 1).reshape(B_, C_, H_, W_)
    x = x + _L0_conv_ref(_gn(x), L0_conv_w_large, L0_conv_w_small, L0_conv_g_l, L0_conv_b_l, L0_conv_m_l, L0_conv_v_l, L0_conv_g_s, L0_conv_b_s, L0_conv_m_s, L0_conv_v_s, L0_conv_g_i, L0_conv_b_i, L0_conv_m_i, L0_conv_v_i)
    x = x + _L1_conv_ref(_gn(x), L1_conv_w_qkv, L1_conv_b_qkv, L1_conv_w_proj, L1_conv_b_proj, L1_conv_bias_table)
    x = x + _L2_conv_ref(_gn(x), L2_conv_W_proj, L2_conv_b_proj, L2_conv_A_log, L2_conv_D, L2_conv_dt_bias, L2_conv_W_out, L2_conv_b_out)
    x = x + _L3_conv_ref(_gn(x), L3_conv_W_proj, L3_conv_b_proj, L3_conv_A_log, L3_conv_D, L3_conv_dt_bias, L3_conv_W_out, L3_conv_b_out)
    return x

_drawn_inputs = setup_inputs


def setup_inputs(seed=0):
    import zlib

    import numpy as np

    out = dict(_drawn_inputs(seed))
    spreads = {'L1_conv_b_qkv': (0.0, 0.8),
     'L1_conv_b_proj': (0.0, 0.1),
     'L2_conv_b_proj': (0.0, 0.1),
     'L2_conv_D': (1.0, 0.6),
     'L2_conv_dt_bias': (0.0, 2.0),
     'L2_conv_b_out': (0.0, 0.267),
     'L3_conv_b_proj': (0.0, 0.1),
     'L3_conv_D': (1.0, 0.6),
     'L3_conv_dt_bias': (0.0, 2.0),
     'L3_conv_b_out': (0.0, 0.1)}
    factors = {'L1_conv_w_qkv': 3.049, 'L1_conv_w_proj': 2.679}
    for name, (base, spread) in spreads.items():
        noise = np.random.default_rng([zlib.crc32(name.encode()), seed]).standard_normal(out[name].shape)
        drawn = base * np.exp(spread * noise) if base else spread * noise
        out[name] = jnp.asarray(drawn.astype(out[name].dtype))
    for name, factor in factors.items():
        out[name] = (out[name] * factor).astype(out[name].dtype)
    return out
```

```python
import numpy as np
from contextlib import ExitStack
import concourse.bass as bass
from concourse import mybir

F32 = mybir.dt.float32
BF16 = mybir.dt.bfloat16
ALU = mybir.AluOpType
ACT = mybir.ActivationFunctionType
AX = mybir.AxisListType


TAPS, STRIP, STRIPS, IMAGES = 13, 4, 8, 16
ROWS_PER_WINDOW, WINDOWS = 4, 4
J = 16
STEP, QUAD, QUADS = 12, 4, 3
GROUP_CH = 6
STEPS = 192 // STEP
T_FILLS, X_PER_FILL = 8, 4
KT = 116


class Step:

    def __init__(self, it, s):
        self.it, self.s = it, s
        self.first = isinstance(it, int) and it == 0 and s == 0

    def count(self, per_step, more):
        return self.it * (2 * per_step) + (self.s * per_step + more)

    def channel(self, more):
        return self.it * (2 * STEP) + (self.s * STEP + more)


def conv_layer(nc, tag, x_src, x_dst, w, consts):
    ctx = ExitStack()
    with ctx:
        sb = lambda name, shape, dt=F32: ctx.enter_context(nc.sbuf_tensor(f"{tag}_{name}", shape, dt))
        ps = lambda name, shape: ctx.enter_context(nc.psum_tensor(f"{tag}_{name}", shape, F32))
        sem = lambda name: ctx.enter_context(nc.semaphore(f"{tag}_{name}"))
        PIX = STRIP * 32
        TAP_ROWS = ROWS_PER_WINDOW * TAPS
        COLS = (STRIPS + 3) * IMAGES
        KERNEL = 192 * J

        x = sb("x", [128, 192, PIX])
        toeplitz = [sb(f"toeplitz{i}", [128, STEP, 32, J]) for i in range(2)]
        xn = sb("xn", [128, 2, STEP, PIX])
        strips_t = [sb(f"strips_t{i}", [128, QUAD, COLS]) for i in range(2)]
        w_hi_mid = sb("w_hi_mid", [KT, 192, J], BF16)
        w_low = sb("w_low", [KT, 192, J], BF16)
        select = sb("select", [KT, 32, 128], BF16)
        shift_all = sb("shift_all", [128, 192])
        ident = sb("ident", [128, 128])
        strip_avg = sb("strip_avg", [128, 128])
        stats = sb("stats", [128, 4, 2, 6])
        moments = sb("moments", [128, 4, 2])
        g_mom = sb("g_mom", [128, 4, 2])
        var_eps = sb("var_eps", [128, 4])
        rstd = sb("rstd", [128, 4])
        shift = sb("shift", [128, 4])
        minus_half = sb("minus_half", [128, 6])
        variances = sb("variances", [96, 6])
        factors_dram = nc.dram_tensor(f"{tag}_factors", [1, 3 * 192], F32).ap()
        room0 = toeplitz[1][:].rearrange("p c x j -> p (c x j)")
        room1 = xn[:].rearrange("p a c x -> p (a c x)")
        w_large = room0[0:TAP_ROWS, 0:KERNEL]
        scales = room0[:, KERNEL:KERNEL + 12 * 192]
        w_small = room1[0:TAP_ROWS, 0:6 * 192]
        centre = room1[0:TAP_ROWS, 6 * 192:2 * 6 * 192]
        toeplitz_rule = room1[0:KT, 2304:2304 + 4 * 63]
        high_f32 = room1[0:TAP_ROWS, 0:KERNEL]

        t_ps = ps("t_ps", [128, 2, X_PER_FILL, 256])
        tr_ps = ps("tr_ps", [128, 2, 512])
        out_ps = ps("out_ps", [128, 2, 512])

        consts_loaded, weights_step, power_made = sem("consts_loaded"), sem("weights_step"), sem("power_made")
        variances_loaded = sem("variances_loaded")
        factors_stored, factors_loaded = sem("factors_stored"), sem("factors_loaded")
        weights_made, x_loaded, stored = sem("weights_made"), sem("x_loaded"), sem("stored")
        norm_step, averaged, rstd_made, xn_made = sem("norm_step"), sem("averaged"), sem("rstd_made"), sem("xn_made")
        shifted = sem("shifted")
        stats_seen = sem("stats_seen")
        transposed, strips_made = sem("transposed"), sem("strips_made")
        t_filled, t_drained = sem("t_filled"), sem("t_drained")
        conv_done, added = sem("conv_done"), sem("added")

        PAIRS_OF_STEPS = STEPS // 2
        src = x_src.rearrange("b c h w -> b c (h w)")
        dst = x_dst.rearrange("b c h w -> b c (h w)")
        N_CONSTS = 13

        def schedule(eng, step):
            for s in range(2):
                step(Step(0, s))
            with eng.Fori(1, PAIRS_OF_STEPS - 1) as it:
                for s in range(2):
                    step(Step(it, s))
            for s in range(2):
                step(Step(PAIRS_OF_STEPS - 1, s))

        def is_step(k, number):
            return isinstance(k.it, int) and 2 * k.it + k.s == number

        def has_next(k):
            return not is_step(k, STEPS - 1)

        def has_next_pair(k):
            return not (isinstance(k.it, int) and k.it == PAIRS_OF_STEPS - 1)

        def channels(k, first, n):
            c0 = k.channel(first)
            return slice(c0, c0 + n) if isinstance(c0, int) else bass.ds(c0, n)

        with nc.Block() as block:
            @block.sync
            def _(sp):
                for r in range(ROWS_PER_WINDOW):
                    sp.dma_start(w_large[TAPS * r:TAPS * (r + 1), :].rearrange("p (j c) -> p j c", j=J),
                                 w["large"][3 - r:3 - r + J].rearrange("j x c -> x j c")).then_inc(consts_loaded, 16)
                    sp.dma_start(w_small[TAPS * r:TAPS * (r + 1), :].rearrange("p (j c) -> p j c", j=6),
                                 w["small"][8 - r:8 - r + 6].rearrange("j x c -> x j c")).then_inc(consts_loaded, 16)
                sp.dma_start(variances[:, :], w["variances"]).then_inc(variances_loaded, 16)
                for t, a in ((scales[:, 0:9 * 192], w["scales"]), (centre, consts["centre"]), (toeplitz_rule, consts["toeplitz_rule"]),
                             (ident[:], consts["ident"]), (strip_avg[:], consts["strip_avg"])):
                    sp.dma_start(t, a).then_inc(consts_loaded, 16)

                def load(first_pair):
                    for strip in range(STRIPS):
                        c0 = first_pair * (2 * STEP)
                        sl = slice(c0, c0 + 2 * STEP) if isinstance(c0, int) else bass.ds(c0, 2 * STEP)
                        sp.dma_start(x[IMAGES * strip:IMAGES * (strip + 1), sl, :],
                                     src[:, sl, PIX * strip:PIX * (strip + 1)]).then_inc(x_loaded, 16)

                def store(pair):
                    sp.wait_ge(added, pair * (2 * QUADS) + 2 * QUADS)
                    c0 = pair * (2 * STEP)
                    sl = slice(c0, c0 + 2 * STEP) if isinstance(c0, int) else bass.ds(c0, 2 * STEP)
                    for strip in range(STRIPS):
                        sp.dma_start(dst[:, sl, PIX * strip:PIX * (strip + 1)],
                                     x[IMAGES * strip:IMAGES * (strip + 1), sl, :]).then_inc(stored, 16)

                sp.wait_ge(power_made, 2)
                sp.dma_start(factors_dram[0, :].rearrange("(p k) -> p k", k=6), variances[:, :]).then_inc(factors_stored, 16)
                sp.wait_ge(factors_stored, 16)
                sp.dma_start(scales[:, 9 * 192:12 * 192], factors_dram[:, :].to_broadcast([128, 3 * 192])).then_inc(factors_loaded, 16)
                load(0)
                with sp.Fori(1, PAIRS_OF_STEPS) as pair:
                    sp.wait_ge(x_loaded, pair * (16 * STRIPS))
                    load(pair)
                with sp.Fori(0, PAIRS_OF_STEPS) as pair:
                    store(pair)
                sp.wait_ge(stored, 16 * STRIPS * PAIRS_OF_STEPS)

            @block.tensor
            def _(pe):
                def average(pair):
                    pe.wait_ge(norm_step, pair * 8 + 4)
                    nc.tensor.matmul(out_ps[:, 1, 0:8], strip_avg[:, :], moments[:].rearrange("p a b -> p (a b)"),
                                     start=True, stop=True).then_inc(averaged, 1)

                def transposes(k, q):
                    half, quad = (k.s, q) if q < QUADS else (1 - k.s, 0)
                    slot = (QUADS * k.s + q) % 2
                    if quad == 0:
                        pe.wait_ge(xn_made, k.count(1, 1 if q == 0 else 2))
                    if not (isinstance(k.it, int) and k.it == 0 and QUADS * k.s + q < 2):
                        pe.wait_ge(strips_made, k.count(QUADS, q - 1))
                    for i in range(QUAD):
                        last = nc.tensor.transpose(tr_ps[:, slot, PIX * i:PIX * (i + 1)],
                                                   xn[:, half, QUAD * quad + i, :], ident[:, :])
                    last.then_inc(transposed, 1)

                def build(k, fills):
                    for i in fills:
                        unit = i % 2
                        if k is None:
                            if i >= 2:
                                pe.wait_ge(t_drained, i - 1)
                            cs = slice(0, STEP)
                        else:
                            pe.wait_ge(t_drained, k.count(T_FILLS, T_FILLS + i - 1))
                            cs = channels(k, STEP, STEP)
                        for xi in range(X_PER_FILL):
                            for part, t in enumerate((w_hi_mid, w_low)):
                                last = nc.tensor.matmul(t_ps[:, unit, xi, 0:192],
                                                        select[:, X_PER_FILL * i + xi, :], t[:, cs, :],
                                                        start=(part == 0), stop=(part == 1))
                        last.then_inc(t_filled, 1)

                def convolve(k, q):
                    slot = (QUADS * k.s + q) % 2
                    if q == 0:
                        pe.wait_ge(t_drained, k.count(T_FILLS, T_FILLS))
                    pe.wait_ge(strips_made, k.count(QUADS, q + 1))
                    if not (isinstance(k.it, int) and k.it == 0 and QUADS * k.s + q < 2):
                        pe.wait_ge(added, k.count(QUADS, q - 1))
                    for i in range(QUAD):
                        for o in range(WINDOWS):
                            first = 4 * (WINDOWS - 1 - o)
                            last = nc.tensor.matmul(out_ps[:, slot, PIX * i:PIX * (i + 1)],
                                                    strips_t[slot][:, i, IMAGES * o:IMAGES * o + 128],
                                                    toeplitz[k.s][:, QUAD * q + i, :, first:first + 4],
                                                    start=(o == 0), stop=(o == WINDOWS - 1))
                    last.then_inc(conv_done, 1)

                def step(k):
                    for q in range(QUADS):
                        if q + 1 < QUADS or has_next(k):
                            transposes(k, q + 1)
                        if has_next(k):
                            build(k, range(3 * q, min(3 * q + 3, T_FILLS)))
                        if k.s == 0 and q == 1 and has_next_pair(k):
                            if not k.first:
                                pe.wait_ge(added, k.count(QUADS, 0))
                            average(k.it + 1)
                            pe.wait_ge(norm_step, k.it * 8 + 13)
                        convolve(k, q)

                pe.wait_ge(consts_loaded, 16 * N_CONSTS)
                average(0)
                pe.wait_ge(weights_made, 1)
                build(None, range(T_FILLS))
                transposes(Step(0, 0), 0)
                schedule(pe, step)

            @block.scalar
            def _(act):
                def evacuate(k, i):
                    buf = 0 if k is None else 1 - k.s
                    act.wait_ge(t_filled, i + 1 if k is None else k.count(T_FILLS, T_FILLS + i + 1))
                    if k is not None and i == 0 and not k.first:
                        act.wait_ge(conv_done, k.count(QUADS, 0))
                    nc.scalar.activation(
                        toeplitz[buf][:, :, X_PER_FILL * i:X_PER_FILL * (i + 1), :].rearrange("p c x j -> p x c j"),
                        t_ps[:, i % 2, :, 0:192].rearrange("p x (c j) -> p x c j", j=J),
                        ACT.Copy).then_inc(t_drained, 1)

                def step(k):
                    if has_next(k):
                        for i in range(T_FILLS):
                            evacuate(k, i)

                for i in range(T_FILLS):
                    evacuate(None, i)
                schedule(act, step)

            @block.vector
            def _(dve):
                def norm_stats(pair, cs):
                    dve.wait_ge(x_loaded, pair * (16 * STRIPS) + 16 * STRIPS)
                    for g in range(4):
                        for half in range(2):
                            last = nc.vector.bn_stats(stats[:, g, half, :],
                                                      x[:, cs(GROUP_CH * g + 3 * half, 3), :].rearrange("p c x -> p (c x)"))
                    last.then_inc(norm_step, 1)
                    dve.wait_ge(norm_step, pair * 8 + 1)
                    dve.sem_inc(stats_seen, 1)
                    for g in range(4):
                        last = nc.vector.bn_aggr(moments[:, g, :], stats[:, g, :, :].rearrange("p a b -> p (a b)"))
                    last.then_inc(norm_step, 1)
                    dve.wait_ge(norm_step, pair * 8 + 2)
                    nc.vector.tensor_tensor(g_mom[:, :, 0], moments[:, :, 0], moments[:, :, 0], ALU.mult).then_inc(norm_step, 1)
                    dve.wait_ge(norm_step, pair * 8 + 3)
                    nc.vector.tensor_tensor(moments[:, :, 1], moments[:, :, 1], g_mom[:, :, 0], ALU.add).then_inc(norm_step, 1)

                def norm_finish(pair):
                    dve.wait_ge(averaged, pair + 1)
                    nc.vector.tensor_copy(g_mom[:].rearrange("p a b -> p (a b)"), out_ps[:, 1, 0:8]).then_inc(norm_step, 1)
                    dve.wait_ge(norm_step, pair * 8 + 5)
                    nc.vector.tensor_tensor(var_eps[:, :], g_mom[:, :, 0], g_mom[:, :, 0], ALU.mult).then_inc(norm_step, 1)
                    dve.wait_ge(norm_step, pair * 8 + 6)
                    nc.vector.scalar_tensor_tensor(var_eps[:, :], g_mom[:, :, 1], 1e-5, var_eps[:, :],
                                                   ALU.add, ALU.subtract).then_inc(norm_step, 1)
                    dve.wait_ge(rstd_made, pair + 1)
                    nc.vector.scalar_tensor_tensor(shift[:, :], g_mom[:, :, 0], -1.0, rstd[:, :],
                                                   ALU.mult, ALU.mult).then_inc(norm_step, 1)
                    dve.wait_ge(norm_step, pair * 8 + 8)

                def normalise(pair, half, cs):
                    for g in range(2):
                        gg = 2 * half + g
                        last = nc.vector.tensor_scalar(
                            xn[:, half, GROUP_CH * g:GROUP_CH * (g + 1), :].rearrange("p c x -> p (c x)"),
                            x[:, cs(GROUP_CH * gg, GROUP_CH), :].rearrange("p c x -> p (c x)"),
                            rstd[:, gg:gg + 1], shift[:, gg:gg + 1], ALU.mult, ALU.add)
                    last.then_inc(xn_made, 1)

                def strips(k, q):
                    slot = (QUADS * k.s + q) % 2
                    dve.wait_ge(transposed, k.count(QUADS, q + 1))
                    if not (isinstance(k.it, int) and k.it == 0 and QUADS * k.s + q < 2):
                        dve.wait_ge(conv_done, k.count(QUADS, q - 1))
                    t = tr_ps[:, slot, :].rearrange("p (c m) -> p c m", c=QUAD)
                    nc.vector.tensor_copy(strips_t[slot][0:64, :, 2 * IMAGES:2 * IMAGES + 128], t[64:128, :, :])
                    nc.vector.tensor_copy(strips_t[slot][64:128, :, IMAGES:IMAGES + 128], t[0:64, :, :]).then_inc(strips_made, 1)

                def add(k, q):
                    slot = (QUADS * k.s + q) % 2
                    dve.wait_ge(conv_done, k.count(QUADS, q + 1))
                    if q == 0:
                        dve.wait_ge(shifted, k.count(1, 1))
                    view = x[:, channels(k, QUAD * q, QUAD), :].rearrange("p c (y x) -> p c y x", y=STRIP)
                    nc.vector.tensor_tensor(view, out_ps[:, slot, :].rearrange("p (c x y) -> p c y x", c=QUAD, y=STRIP),
                                            view, ALU.add).then_inc(added, 1)

                def in_pair(k, pairs_on):
                    c0 = k.it * (2 * STEP) + 2 * STEP * pairs_on
                    return lambda a, n: slice(c0 + a, c0 + a + n) if isinstance(c0, int) else bass.ds(c0 + a, n)

                def step(k):
                    nxt = in_pair(k, 1)
                    for q in range(QUADS):
                        if q + 1 < QUADS or has_next(k):
                            strips(k, q + 1)
                        if not (k.first and q == 0):
                            add(k, q - 1)
                        if not has_next_pair(k):
                            continue
                        if k.s == 0 and q == 0:
                            norm_stats(k.it + 1, nxt)
                        if k.s == 0 and q == 1:
                            norm_finish(k.it + 1)
                        if k.s == 1 and q == 0:
                            normalise(k.it + 1, 0, nxt)
                        if k.s == 1 and q == 2:
                            normalise(k.it + 1, 1, nxt)

                def prepare():
                    kinds = scales.rearrange("p (k b c) -> p k b c", k=4, b=3)
                    g, m, b, factor = (kinds[:, i] for i in range(4))
                    nc.vector.memset(minus_half[:, :], -0.5)
                    nc.vector.memset(w_hi_mid[:, :, :], 0.0)
                    nc.vector.memset(w_low[:, :, :], 0.0)
                    for t in strips_t:
                        nc.vector.memset(t[:, :, :], 0.0)
                    dve.wait_ge(variances_loaded, 16)
                    nc.vector.tensor_scalar(variances[:, :], variances[:, :], 1e-5, None, ALU.add).then_inc(power_made, 1)
                    dve.wait_ge(consts_loaded, 16 * N_CONSTS)
                    for xo in range(32):
                        nc.vector.tensor_copy(select[:, xo, :].rearrange("p (r x) -> p r x", r=4),
                                              toeplitz_rule.rearrange("p (r u) -> p r u", r=4)[:, :, 31 - xo:63 - xo])
                    dve.wait_ge(factors_loaded, 16)
                    nc.vector.tensor_tensor(g, g, factor, ALU.mult).then_inc(weights_step, 1)
                    dve.wait_ge(weights_step, 1)
                    scale = lambda branch, js: g[0:TAP_ROWS, branch, None, :].to_broadcast([TAP_ROWS, js, 192])
                    by_j = lambda t, js: t.rearrange("p (j c) -> p j c", j=js)
                    nc.vector.tensor_tensor(m, m, g, ALU.mult)
                    nc.vector.tensor_tensor(by_j(w_small, 6), by_j(w_small, 6), scale(1, 6), ALU.mult)
                    nc.vector.tensor_tensor(by_j(centre, 6), by_j(centre, 6), scale(2, 6), ALU.mult)
                    nc.vector.tensor_tensor(by_j(w_large, J), by_j(w_large, J), scale(0, J), ALU.mult).then_inc(weights_step, 1)
                    dve.wait_ge(weights_step, 2)
                    nc.vector.tensor_tensor(b, b, m, ALU.subtract)
                    nc.vector.tensor_tensor(w_small, w_small, centre, ALU.add).then_inc(weights_step, 1)
                    dve.wait_ge(weights_step, 3)
                    nc.vector.tensor_tensor(shift_all[:, :], b[:, 0, :], b[:, 1, :], ALU.add)
                    some = w_large[:, 5 * 192:11 * 192]
                    nc.vector.tensor_tensor(some, some, w_small, ALU.add).then_inc(weights_step, 1)
                    dve.wait_ge(weights_step, 4)
                    nc.vector.tensor_tensor(shift_all[:, :], shift_all[:, :], b[:, 2, :], ALU.add)
                    full = w_large.rearrange("p (j c) -> p c j", j=J)
                    rest = high_f32.rearrange("p (c j) -> p c j", j=J)
                    nc.vector.tensor_copy(w_hi_mid[0:TAP_ROWS], full).then_inc(weights_step, 1)
                    dve.wait_ge(weights_step, 5)
                    nc.vector.tensor_tensor(rest, full, w_hi_mid[0:TAP_ROWS], ALU.subtract).then_inc(weights_step, 1)
                    dve.wait_ge(weights_step, 6)
                    nc.vector.tensor_copy(w_hi_mid[64:64 + TAP_ROWS], rest)
                    nc.vector.tensor_copy(w_low[0:TAP_ROWS], rest).then_inc(weights_step, 1)
                    dve.wait_ge(weights_step, 7)
                    nc.vector.tensor_tensor(w_low[0:TAP_ROWS], rest, w_low[0:TAP_ROWS], ALU.subtract).then_inc(weights_step, 1)
                    dve.wait_ge(weights_step, 8)
                    dve.sem_inc(weights_made, 1)

                prepare()
                cs0 = lambda a, n: slice(a, a + n)
                norm_stats(0, cs0)
                norm_finish(0)
                normalise(0, 0, cs0)
                normalise(0, 1, cs0)
                strips(Step(0, 0), 0)
                schedule(dve, step)
                add(Step(PAIRS_OF_STEPS - 1, 1), 2)

            @block.gpsimd
            def _(pool):
                def power(pair):
                    pool.wait_ge(norm_step, pair * 8 + 7)
                    nc.gpsimd.tensor_tensor(rstd[:, :], var_eps[:, :], minus_half[:, 0:4], ALU.pow).then_inc(rstd_made, 1)

                def add_shift(k):
                    pool.wait_ge(xn_made, k.count(1, 1))
                    cs = channels(k, 0, STEP)
                    view = x[:, cs, :]
                    nc.gpsimd.tensor_tensor(view, view, shift_all[:, cs, None].to_broadcast([128, STEP, PIX]),
                                            ALU.add).then_inc(shifted, 1)

                def step(k):
                    add_shift(k)
                    if k.s == 0 and has_next_pair(k):
                        power(k.it + 1)

                pool.wait_ge(power_made, 1)
                nc.gpsimd.tensor_tensor(variances[:, :], variances[:, :], minus_half[0:96, :], ALU.pow).then_inc(power_made, 1)
                power(0)
                schedule(pool, step)


CHUNK = 96
BLOCK = 32
STATES = 16
TILE_STATES = 128 // BLOCK
PAIRS = 12
RING = 8
FILLS = 29
NORM, DELTA_P, X_P, B_REP = 0, 1, 5, 9


def fill_prologue(n, j):
    return (n, 25 + j)


class Batch:

    def __init__(self, it, s):
        self.it, self.s = it, s
        self.first = isinstance(it, int) and it == 0 and s == 0

    def count(self, per_batch, more):
        return self.it * (2 * per_batch) + (self.s * per_batch + more)


class Fill:

    def __init__(self, n, offset):
        self.bank = (FILLS * n.s + offset) % 2
        self.number = n.it * (2 * FILLS) + (FILLS * n.s + offset)
        self.before = n.it * FILLS + (FILLS * n.s + offset) // 2
        self.static_first = isinstance(self.before, int) and self.before == 0


def ssm_layer(nc, tag, x_src, x_dst, w, consts, batches):
    L = 1024
    HALF = 512
    ctx = ExitStack()
    with ctx:
        sb = lambda name, shape, dt=F32: ctx.enter_context(nc.sbuf_tensor(f"{tag}_{name}", shape, dt))
        ps = lambda name, shape: ctx.enter_context(nc.psum_tensor(f"{tag}_{name}", shape, F32))
        sem = lambda name: ctx.enter_context(nc.semaphore(f"{tag}_{name}"))

        x = sb("x", [CHUNK, 2, L])
        x_res = sb("x_res", [CHUNK, 2, L])
        xn = sb("xn", [CHUNK, 2, L])
        x_in = [sb(f"x_in{i}", [CHUNK, 2, L]) for i in range(2)]
        relu_t = sb("relu_t", [128, 2, L])
        log_t = sb("log_t", [CHUNK, 2, L])
        delta = sb("delta", [CHUNK, 2, L])
        dx = sb("dx", [CHUNK, 2, L])
        b_rep = sb("b_rep", [128, 4, L])
        c_rep = sb("c_rep", [128, 4, L])
        decay = sb("decay", [128, 2, 2 * L])
        h = sb("h", [128, RING, 2 * L])
        y_sb = sb("y_sb", [CHUNK, 2, L])
        bc_parts = sb("bc_parts", [128, L], BF16)
        mid_t = sb("mid_t", [128, L], BF16)
        w_proj = sb("w_proj", [CHUNK, 2, 416])
        w_out = sb("w_out", [CHUNK, 2, 192])
        a_neg = sb("a_neg", [128, 24])
        vecs = sb("vecs", [CHUNK, 10])
        bc_bias = sb("bc_bias", [128, 1])
        rep_sel = sb("rep_sel", [CHUNK, 3, 128])
        state_sum = sb("state_sum", [128, BLOCK])
        group_avg = sb("group_avg", [CHUNK, CHUNK])
        bc_sel = sb("bc_sel", [128, 8, 128], BF16)
        stats = sb("stats", [CHUNK, 4, 6])
        moments = sb("moments", [CHUNK, 2, 2])
        g_mom = sb("g_mom", [CHUNK, 2, 2])
        var_eps = sb("var_eps", [CHUNK, 2])
        rstd = sb("rstd", [CHUNK, 2])
        shift = sb("shift", [CHUNK, 2])
        minus_half = sb("minus_half", [CHUNK, 2])

        delta_rep = ps("delta_rep", [128, L])
        dx_rep = ps("dx_rep", [128, L])
        y_ps = ps("y_ps", [128, L])
        scratch = ps("scratch", [128, 2, HALF])

        consts_loaded = sem("consts_loaded")
        consts_made = sem("consts_made")
        x_loaded = sem("x_loaded")
        res_loaded = sem("res_loaded")
        out_stored = sem("out_stored")
        filled = sem("filled")
        wait_passed = sem("wait_passed")
        stats_seen = sem("stats_seen")
        drained = [sem(f"drained{i}") for i in range(2)]
        norm_step = sem("norm_step")
        rstd_made = sem("rstd_made")
        xn_made = sem("xn_made")
        soft_step = sem("soft_step")
        bc_high = sem("bc_high")
        bc_step = sem("bc_step")
        bc_mid = sem("bc_mid")
        delta_made = sem("delta_made")
        dx_made = sem("dx_made")
        delta_replicated = sem("delta_replicated")
        dx_replicated = sem("dx_replicated")
        decay_made = sem("decay_made")
        u_made = sem("u_made")
        scanned = sem("scanned")
        c_applied = sem("c_applied")
        y_summed = sem("y_summed")
        y_kept = sem("y_kept")

        bx, bdl, dtb, d_skip, b_out = (vecs[:, 2 * i:2 * i + 2] for i in range(5))

        def prologue_fill(m_of, j):
            return Fill(Batch(0, 0), j) if m_of is None else Fill(m_of, 25 + j)

        def c_fill(n, i):
            return Fill(n, (17 if n.first else 13) + i)

        def tail_fill(n_next, i):
            ended = isinstance(n_next.it, int) and n_next.it == batches // 2
            return Fill(n_next, (-4 if ended else 21) + i)

        def await_bank(pe, f):
            if not f.static_first:
                pe.wait_ge(drained[f.bank], f.before)

        def await_all(eng, waits):
            for semaphore, value in waits:
                eng.wait_ge(semaphore, value)
                eng.sem_inc(wait_passed, 1)

        def await_fill(eng, f):
            eng.wait_ge(filled, f.number + 1)

        def await_drained(eng, f):
            eng.wait_ge(drained[f.bank], f.before + 1)

        def following(n):
            return Batch(0, 0) if n is None else (Batch(n.it, 1) if n.s == 0 else Batch(n.it + 1, 0))

        def schedule(eng, prologue, main, tail):
            prologue(None)
            main(Batch(0, 0), False)
            main(Batch(0, 1), False)
            last = batches // 2 - 1
            if last > 1:
                with eng.Fori(1, last) as it:
                    main(Batch(it, 0), False)
                    main(Batch(it, 1), False)
            main(Batch(last, 0), False)
            main(Batch(last, 1), True)
            tail(Batch(last + 1, 0))

        src = x_src.rearrange("b (c p) h w -> b p c (h w)", p=CHUNK)
        dst = x_dst.rearrange("b (c p) h w -> b p c (h w)", p=CHUNK)
        N_CONSTS = 9

        with nc.Block() as block:
            @block.sync
            def _(sp):
                for t, a in ((w_proj, w["w_proj"]), (w_out, w["w_out"]), (a_neg, w["a_log"]), (vecs, w["vecs"]),
                             (rep_sel, consts["rep_sel"]), (state_sum, consts["state_sum"]),
                             (group_avg, consts["group_avg"])):
                    sp.dma_start(t[:], a).then_inc(consts_loaded, 16)
                sp.dma_start(bc_bias[96:128, :], w["bc_bias"]).then_inc(consts_loaded, 16)
                sp.dma_start(h[:, 0, 0:1024].rearrange("p (t m) -> p t m", t=8), consts["bc_sel"]).then_inc(consts_loaded, 16)

                def load(n):
                    sp.dma_start(x[:, :, :], src[n.count(1, 0)]).then_inc(x_loaded, 16)

                def load_residual(n):
                    sp.dma_start(x_res[:, :, :], src[n.count(1, 0)]).then_inc(res_loaded, 16)

                def store(n_next):
                    await_all(sp, [(drained[f.bank], f.before + 1) for f in (tail_fill(n_next, 2), tail_fill(n_next, 3))])
                    sp.dma_start(dst[n_next.count(1, -1)], x_res[:, :, :]).then_inc(out_stored, 16)
                    sp.wait_ge(out_stored, n_next.count(16, 0))

                def main(n, last):
                    if not n.first:
                        store(n)
                        load_residual(n)
                    if not (isinstance(n.it, int) and n.it == batches // 2 - 1):
                        sp.wait_ge(xn_made, n.count(1, 2))
                        load(Batch(n.it + 1, n.s))

                load(Batch(0, 0))
                load_residual(Batch(0, 0))
                sp.wait_ge(xn_made, 1)
                load(Batch(0, 1))
                schedule(sp, lambda n: None, main, store)

            @block.tensor
            def _(pe):
                def replicate(n, d):
                    if d == 0:
                        pe.wait_ge(delta_made, n.count(1, 1))
                    if not (n.first and d == 0):
                        pe.wait_ge(decay_made, n.count(PAIRS, 2 * d))
                    for half in range(2):
                        t = slice(half * HALF, (half + 1) * HALF)
                        last = nc.tensor.matmul(delta_rep[:, t], rep_sel[:, d % 3, :], delta[:, d // 3, t],
                                                start=True, stop=True)
                    last.then_inc(delta_replicated, 1)
                    if d == 0:
                        pe.wait_ge(dx_made, n.count(1, 1))
                    if not (n.first and d == 0):
                        pe.wait_ge(u_made, n.count(PAIRS, 2 * d))
                    for half in range(2):
                        t = slice(half * HALF, (half + 1) * HALF)
                        last = nc.tensor.matmul(dx_rep[:, t], rep_sel[:, d % 3, :], dx[:, d // 3, t],
                                                start=True, stop=True)
                    last.then_inc(dx_replicated, 1)

                def sum_states(n, g):
                    if not (n.first and g == 0):
                        pe.wait_ge(y_kept, n.count(2, g))
                    for np_ in range(2):
                        pe.wait_ge(c_applied, n.count(PAIRS, 6 * g + 5 + np_))
                        for sub in range(2):
                            for half in range(2):
                                for dd in range(3):
                                    p = 6 * g + 2 * dd + np_
                                    slot = (PAIRS * n.s + p) % RING
                                    at = sub * L + half * HALF
                                    last = nc.tensor.matmul(
                                        y_ps[BLOCK * dd:BLOCK * (dd + 1), half * HALF:(half + 1) * HALF],
                                        state_sum[:, :], h[:, slot, at:at + HALF],
                                        start=(np_ == 0 and sub == 0), stop=(np_ == 1 and sub == 1))
                        last.then_inc(y_summed, 1)

                def project_out(n_next):
                    p = n_next
                    pe.wait_ge(y_kept, p.count(2, 0))
                    for i in range(4):
                        co, half = divmod(i, 2)
                        f = tail_fill(p, i)
                        await_bank(pe, f)
                        for ci in range(2):
                            last = nc.tensor.matmul(scratch[0:CHUNK, f.bank, :],
                                                    w_out[:, ci, co * CHUNK:(co + 1) * CHUNK],
                                                    y_sb[:, ci, half * HALF:(half + 1) * HALF],
                                                    start=(ci == 0), stop=(ci == 1))
                        last.then_inc(filled, 1)

                def norm(m_of):
                    f = prologue_fill(m_of, NORM)
                    await_bank(pe, f)
                    pe.wait_ge(norm_step, following(m_of).count(7, 3))
                    nc.tensor.matmul(scratch[0:CHUNK, f.bank, 0:4], group_avg[:, :],
                                     moments[:, :, :].rearrange("p a b -> p (a b)"), start=True,
                                     stop=True).then_inc(filled, 1)

                def project(m_of, first_fill, cols):
                    pe.wait_ge(xn_made, following(m_of).count(1, 1))
                    for i, (m0, m1) in enumerate(cols):
                        for half in range(2):
                            f = prologue_fill(m_of, first_fill + 2 * i + half)
                            await_bank(pe, f)
                            for ci in range(2):
                                last = nc.tensor.matmul(scratch[0:m1 - m0, f.bank, :], w_proj[:, ci, m0:m1],
                                                        xn[:, ci, half * HALF:(half + 1) * HALF],
                                                        start=(ci == 0), stop=(ci == 1))
                            last.then_inc(filled, 1)

                def replicate_bc(fills, tiles):
                    for i, f in enumerate(fills):
                        await_bank(pe, f)
                        half = i % 2
                        nc.tensor.matmul(scratch[:, f.bank, :], bc_sel[:, tiles + i // 2, :],
                                         bc_parts[:, half * HALF:(half + 1) * HALF],
                                         start=True, stop=True).then_inc(filled, 1)

                def b_tiles(m_of):
                    m = following(m_of)
                    pe.wait_ge(bc_mid, m.count(1, 1))
                    pe.wait_ge(bc_step, m.count(3, 3))
                    replicate_bc([prologue_fill(m_of, B_REP + i) for i in range(8)], 0)

                def prologue(m_of):
                    norm(m_of)
                    project(m_of, DELTA_P, ((224, 320), (320, 416)))
                    project(m_of, X_P, ((0, 128), (128, 224)))
                    b_tiles(m_of)

                def main(n, last):
                    replicate(n, 0)
                    replicate_bc([c_fill(n, i) for i in range(8)], 4)
                    replicate(n, 1)
                    if not n.first:
                        sum_states_before(n)
                    replicate(n, 2)
                    if not n.first:
                        project_out(n)
                    if not last:
                        norm(n)
                    replicate(n, 3)
                    if not last:
                        project(n, DELTA_P, ((224, 320), (320, 416)))
                        project(n, X_P, ((0, 128), (128, 224)))
                    sum_states(n, 0)
                    replicate(n, 4)
                    replicate(n, 5)
                    if not last:
                        b_tiles(n)

                def sum_states_before(n):
                    sum_states(Batch(n.it, 0) if n.s else Batch(n.it - 1, 1), 1)

                def tail(n):
                    sum_states_before(n)
                    project_out(n)

                pe.wait_ge(consts_loaded, 16 * N_CONSTS)
                pe.wait_ge(consts_made, 5)
                schedule(pe, prologue, main, tail)

            @block.scalar
            def _(act):
                def exp_pair(n, p):
                    d, np_ = divmod(p, 2)
                    if np_ == 0:
                        act.wait_ge(delta_replicated, n.count(6, d + 1))
                    if not (n.first and p < 2):
                        act.wait_ge(scanned, n.count(PAIRS, p - 1))
                    for sub in range(2):
                        col = 4 * d + 2 * np_ + sub
                        last = nc.scalar.activation(decay[:, p % 2, sub * L + 1:(sub + 1) * L], delta_rep[:, 1:L],
                                                    ACT.Exp, scale=a_neg[:, col:col + 1])
                    last.then_inc(decay_made, 1)

                def drain_rep(f, out):
                    await_fill(act, f)
                    nc.scalar.activation(out, scratch[:, f.bank, :], ACT.Copy).then_inc(drained[f.bank], 1)

                def c_tiles(n, np_):
                    if not n.first:
                        act.wait_ge(c_applied, n.count(PAIRS, np_ - 1))
                    for i in range(4 * np_, 4 * np_ + 4):
                        drain_rep(c_fill(n, i), c_rep[:, i // 2, (i % 2) * HALF:(i % 2 + 1) * HALF])

                def b_tiles(m_of, np_):
                    if m_of is not None:
                        act.wait_ge(u_made, m_of.count(PAIRS, 11 + np_))
                    for i in range(4 * np_, 4 * np_ + 4):
                        drain_rep(prologue_fill(m_of, B_REP + i), b_rep[:, i // 2, (i % 2) * HALF:(i % 2 + 1) * HALF])

                def normalise(m_of):
                    m = following(m_of)
                    act.wait_ge(norm_step, m.count(7, 7))
                    for c in range(2):
                        last = nc.scalar.activation(xn[:, c, :], x[:, c, :], ACT.Identity,
                                                    scale=rstd[:, c:c + 1], bias=shift[:, c:c + 1])
                    last.then_inc(xn_made, 1)

                def softplus(m_of):
                    m = following(m_of)
                    if m_of is not None:
                        act.wait_ge(delta_made, m.count(1, 0))
                    for i in range(4):
                        c, half = divmod(i, 2)
                        t = slice(half * HALF, (half + 1) * HALF)
                        f = prologue_fill(m_of, DELTA_P + i)
                        await_fill(act, f)
                        nc.scalar.activation(log_t[:, c, t], scratch[0:CHUNK, f.bank, :], ACT.Abs, bias=bdl[:, c:c + 1])
                        nc.scalar.activation(relu_t[0:CHUNK, c, t], scratch[0:CHUNK, f.bank, :], ACT.Relu,
                                             bias=bdl[:, c:c + 1]).then_inc(drained[f.bank], 1)
                    for i in (2, 3):
                        await_drained(act, prologue_fill(m_of, DELTA_P + i))
                    nc.scalar.activation(log_t[:, :, :], log_t[:, :, :], ACT.Exp, scale=-1.0).then_inc(soft_step, 1)
                    act.wait_ge(soft_step, m.count(2, 1))
                    nc.scalar.activation(log_t[:, :, :], log_t[:, :, :], ACT.Ln, bias=1.0).then_inc(soft_step, 1)

                def inputs(m_of):
                    m = following(m_of)
                    if m_of is not None:
                        act.wait_ge(bc_step, m.count(3, 0))
                        if not m_of.first:
                            act.wait_ge(y_kept, m_of.count(2, 0))
                    for i in range(4):
                        c, half = divmod(i, 2)
                        t = slice(half * HALF, (half + 1) * HALF)
                        f = prologue_fill(m_of, X_P + i)
                        await_fill(act, f)
                        if c == 0:
                            nc.scalar.activation(relu_t[CHUNK:128, 0, t], scratch[CHUNK:128, f.bank, :], ACT.Identity,
                                                 bias=bc_bias[CHUNK:128, :])
                        nc.scalar.activation(x_in[m.s][:, c, t], scratch[0:CHUNK, f.bank, :], ACT.Identity,
                                             bias=bx[:, c:c + 1]).then_inc(drained[f.bank], 1)
                    for i in (0, 1):
                        await_drained(act, prologue_fill(m_of, X_P + i))
                    nc.scalar.activation(bc_parts[CHUNK:128, :], relu_t[CHUNK:128, 0, :], ACT.Copy).then_inc(bc_high, 1)

                def middle_part(m_of):
                    m = following(m_of)
                    act.wait_ge(bc_step, m.count(3, 1))
                    nc.scalar.activation(bc_parts[0:32, :], relu_t[CHUNK:128, 1, :], ACT.Copy).then_inc(bc_mid, 1)

                def prologue(m_of):
                    normalise(m_of)
                    softplus(m_of)
                    inputs(m_of)
                    middle_part(m_of)
                    b_tiles(m_of, 0)
                    b_tiles(m_of, 1)

                def main(n, last):
                    for p in range(PAIRS):
                        exp_pair(n, p)
                        if p < 2:
                            c_tiles(n, p)
                        if last:
                            continue
                        if p == 5:
                            normalise(n)
                        if p == 7:
                            softplus(n)
                            inputs(n)
                        if p == 9:
                            middle_part(n)
                    if not last:
                        b_tiles(n, 0)
                        b_tiles(n, 1)

                act.wait_ge(consts_loaded, 16 * N_CONSTS)
                nc.scalar.activation(a_neg[:, :], a_neg[:, :], ACT.Exp).then_inc(consts_made, 1)
                act.wait_ge(consts_made, 5)
                schedule(act, prologue, main, lambda n: None)

            @block.vector
            def _(dve):
                def make_u(n, p):
                    d, np_ = divmod(p, 2)
                    if p == 0:
                        pass
                    if np_ == 0:
                        dve.wait_ge(dx_replicated, n.count(6, d + 1))
                    if p < 2:
                        m_of = None if n.first else before(n)
                        for i in (2, 3):
                            await_drained(dve, prologue_fill(m_of, B_REP + 4 * np_ + i))
                    if p >= RING:
                        dve.wait_ge(y_summed, n.count(4, np_ + 1))
                    elif not n.first:
                        dve.wait_ge(y_summed, n.count(4, -4 + 2 * ((p + 4) // 6) + np_ + 1))
                    slot = (PAIRS * n.s + p) % RING
                    nc.vector.tensor_tensor(h[:, slot, :].rearrange("p (s t) -> p s t", s=2),
                                            dx_rep[:, None, :].to_broadcast([128, 2, L]),
                                            b_rep[:, 2 * np_:2 * np_ + 2, :], ALU.mult).then_inc(u_made, 1)

                def before(n):
                    return Batch(n.it, 0) if n.s else Batch(n.it - 1, 1)

                def scan(n, p):
                    dve.wait_ge(decay_made, n.count(PAIRS, p + 1))
                    dve.wait_ge(u_made, n.count(PAIRS, p + 1))
                    slot = (PAIRS * n.s + p) % RING
                    nc.vector.tensor_tensor_scan(h[:, slot, :], decay[:, p % 2, :], h[:, slot, :], 0.0,
                                                 ALU.mult, ALU.add).then_inc(scanned, 1)

                def keep_y(n, g, next_):
                    dve.wait_ge(y_summed, n.count(4, 2 * g + 2))
                    if g == 0 and not n.first:
                        await_fill(dve, tail_fill(n, 3))
                    nc.vector.scalar_tensor_tensor(y_sb[:, g, :], x_in[n.s][:, g, :], d_skip[:, g:g + 1],
                                                   y_ps[0:CHUNK, :], ALU.mult, ALU.add).then_inc(y_kept, 1)

                def residual(n_next):
                    dve.wait_ge(res_loaded, n_next.count(16, 0))
                    for i in range(4):
                        co, half = divmod(i, 2)
                        t = slice(half * HALF, (half + 1) * HALF)
                        f = tail_fill(n_next, i)
                        await_fill(dve, f)
                        nc.vector.scalar_tensor_tensor(x_res[:, co, t], scratch[0:CHUNK, f.bank, :],
                                                       b_out[:, co:co + 1], x_res[:, co, t],
                                                       ALU.add, ALU.add).then_inc(drained[f.bank], 1)

                def norm_stats(m_of):
                    m = following(m_of)
                    k = m.count(7, 0)
                    dve.wait_ge(x_loaded, m.count(16, 16))
                    for i in range(4):
                        c, half = divmod(i, 2)
                        last = nc.vector.bn_stats(stats[:, i, :], x[:, c, half * HALF:(half + 1) * HALF])
                    last.then_inc(norm_step, 1)
                    dve.wait_ge(norm_step, k + 1)
                    if m_of is not None:
                        await_fill(dve, prologue_fill_before(m_of))
                    dve.sem_inc(stats_seen, 1)
                    for c in range(2):
                        last = nc.vector.bn_aggr(moments[:, c, :], stats[:, 2 * c:2 * c + 2, :].rearrange("p a b -> p (a b)"))
                    last.then_inc(norm_step, 1)
                    dve.wait_ge(norm_step, k + 2)
                    for c in range(2):
                        last = nc.vector.scalar_tensor_tensor(moments[:, c, 1:2], moments[:, c, 0:1],
                                                              moments[:, c, 0:1], moments[:, c, 1:2], ALU.mult, ALU.add)
                    last.then_inc(norm_step, 1)

                def prologue_fill_before(m_of):
                    return prologue_fill(None if m_of.first else before(m_of), NORM)

                def norm_finish(m_of):
                    m = following(m_of)
                    k = m.count(7, 0)
                    f = prologue_fill(m_of, NORM)
                    await_fill(dve, f)
                    nc.vector.tensor_copy(g_mom[:, :, :].rearrange("p a b -> p (a b)"),
                                          scratch[0:CHUNK, f.bank, 0:4]).then_inc(drained[f.bank], 1)
                    await_drained(dve, f)
                    for c in range(2):
                        last = nc.vector.scalar_tensor_tensor(var_eps[:, c:c + 1], g_mom[:, c, 0:1], g_mom[:, c, 0:1],
                                                              g_mom[:, c, 1:2], ALU.mult, ALU.subtract)
                    last.then_inc(norm_step, 1)
                    dve.wait_ge(norm_step, k + 4)
                    nc.vector.tensor_scalar(var_eps[:, :], var_eps[:, :], -1.0, 1e-5, ALU.mult, ALU.add).then_inc(norm_step, 1)

                def norm_shift(m_of):
                    m = following(m_of)
                    k = m.count(7, 0)
                    dve.wait_ge(rstd_made, m.count(1, 1))
                    nc.vector.scalar_tensor_tensor(shift[:, :], g_mom[:, :, 0], -1.0, rstd[:, :],
                                                   ALU.mult, ALU.mult).then_inc(norm_step, 2)

                def bc_split(m_of):
                    m = following(m_of)
                    k = m.count(3, 0)
                    q = slice(CHUNK, 128)
                    dve.wait_ge(bc_high, m.count(1, 1))
                    nc.vector.tensor_tensor(relu_t[q, 1, :], relu_t[q, 0, :], bc_parts[q, :], ALU.subtract).then_inc(bc_step, 1)
                    dve.wait_ge(bc_step, k + 1)
                    nc.vector.tensor_copy(mid_t[q, :], relu_t[q, 1, :]).then_inc(bc_step, 1)
                    dve.wait_ge(bc_step, k + 2)
                    dve.wait_ge(bc_mid, m.count(1, 1))
                    nc.vector.tensor_tensor(bc_parts[32:64, :], relu_t[q, 1, :], mid_t[q, :], ALU.subtract).then_inc(bc_step, 1)

                def finish_inputs(m_of):
                    m = following(m_of)
                    dve.wait_ge(soft_step, m.count(2, 2))
                    if m_of is not None:
                        dve.wait_ge(dx_replicated, m_of.count(6, 6))
                    nc.vector.tensor_tensor(delta[:, :, :], relu_t[0:CHUNK, :, :], log_t[:, :, :], ALU.add).then_inc(delta_made, 1)
                    dve.wait_ge(delta_made, m.count(1, 1))
                    for i in (2, 3):
                        await_drained(dve, prologue_fill(m_of, X_P + i))
                    nc.vector.tensor_tensor(dx[:, :, :], delta[:, :, :], x_in[m.s][:, :, :], ALU.mult).then_inc(dx_made, 1)

                def prologue(m_of):
                    norm_stats(m_of)
                    norm_finish(m_of)
                    norm_shift(m_of)
                    bc_split(m_of)
                    finish_inputs(m_of)

                def main(n, last):
                    make_u(n, 0)
                    for p in range(PAIRS):
                        if p + 1 < PAIRS:
                            make_u(n, p + 1)
                        elif not last:
                            finish_inputs(n)
                        scan(n, p)
                        if p == 3 and not n.first:
                            keep_y(before(n), 1, n)
                        if p == 4 and not n.first:
                            residual(n)
                        if p == 7:
                            keep_y(n, 0, n)
                        if last:
                            continue
                        if p == 2:
                            norm_stats(n)
                        if p == 4:
                            norm_finish(n)
                        if p == 5:
                            norm_shift(n)
                        if p == 9:
                            bc_split(n)

                def tail(n):
                    keep_y(before(n), 1, n)
                    residual(n)

                nc.vector.memset(decay[:, :, 0:1], 0.0).then_inc(consts_made, 1)
                nc.vector.memset(decay[:, :, L:L + 1], 0.0)
                nc.vector.memset(minus_half[:, :], -0.5)
                nc.vector.memset(bc_parts[64:96, :], 0.0).then_inc(consts_made, 1)
                dve.wait_ge(consts_loaded, 16 * N_CONSTS)
                nc.vector.tensor_tensor(bdl, bdl, dtb, ALU.add)
                nc.vector.tensor_copy(bc_sel[:, :, :], h[:, 0, 0:1024].rearrange("p (t m) -> p t m", t=8)).then_inc(consts_made, 1)
                dve.wait_ge(consts_made, 4)
                nc.vector.tensor_scalar(a_neg[:, :], a_neg[:, :], -1.0, None, ALU.mult).then_inc(consts_made, 1)
                dve.wait_ge(consts_made, 5)
                schedule(dve, prologue, main, tail)

            @block.gpsimd
            def _(pool):
                def before(n):
                    return Batch(n.it, 0) if n.s else Batch(n.it - 1, 1)

                def apply_c(n, p):
                    np_ = p % 2
                    if p < 2:
                        for i in (2, 3):
                            await_drained(pool, c_fill(n, 4 * np_ + i))
                    pool.wait_ge(scanned, n.count(PAIRS, p + 1))
                    slot = (PAIRS * n.s + p) % RING
                    view = h[:, slot, :].rearrange("p (s t) -> p s t", s=2)
                    nc.gpsimd.tensor_tensor(view, view, c_rep[:, 2 * np_:2 * np_ + 2, :], ALU.mult).then_inc(c_applied, 1)

                def power(m_of):
                    m = following(m_of)
                    pool.wait_ge(norm_step, m.count(7, 5))
                    nc.gpsimd.tensor_tensor(rstd[:, :], var_eps[:, :], minus_half[:, :], ALU.pow).then_inc(rstd_made, 1)

                def main(n, last):
                    for p in range(PAIRS):
                        apply_c(n, p)
                        if p == 3 and not last:
                            power(n)

                pool.wait_ge(consts_made, 5)
                schedule(pool, power, main, lambda n: None)


HEADS, HEAD = 6, 32
WIN, PAD, SIDE = 7, 3, 32
TILE_H, TILE_W = 8, 16
TILES = [(ty, tx) for ty in (0, 3, 1, 2) for tx in (0, 1)]
GROUP = 3
UNIT_PAIRS = 12
MASK_ROWS = slice(64, 112)
A_FILLS = 59


def halo(tile):
    ty, tx = tile
    y = TILE_H * ty
    r0, r1 = max(0, y - PAD), min(SIDE, y + TILE_H + PAD)
    return r0, r1, (r1 - r0) * TILE_W, (r1 - r0) * (TILE_W + PAD), (slice(0, PAD) if tx == 0 else slice(TILE_W - PAD, TILE_W))


def tile_at(tile):
    ty, tx = tile
    first = 512 * tx + 128 * ty
    return slice(first, first + 128)


def attention(nc, tag, x_src, x_dst, w, consts, batches):
    L, HALF = 1024, 512
    ctx = ExitStack()
    with ctx:
        sb = lambda name, shape, dt=F32: ctx.enter_context(nc.sbuf_tensor(f"{tag}_{name}", shape, dt))
        ps = lambda name, shape: ctx.enter_context(nc.psum_tensor(f"{tag}_{name}", shape, F32))
        sem = lambda name: ctx.enter_context(nc.semaphore(f"{tag}_{name}"))

        x = sb("x", [CHUNK, 2, L])
        x_res = sb("x_res", [CHUNK, 2, L])
        xn = sb("xn", [CHUNK, 2, L])
        qk = sb("qk", [128, 3, L])
        qk1 = sb("qk1", [128, 3, L], BF16)
        qk2 = sb("qk2", [128, 3, L], BF16)
        qk3 = sb("qk3", [128, 3, L], BF16)
        q_a = [sb(f"q_a{i}", [128, HEADS, L], BF16) for i in range(2)]
        k_a = [sb(f"k_a{i}", [128, HEADS, L], BF16) for i in range(2)]
        q_b = [sb(f"q_b{i}", [128, HEADS, L], BF16) for i in range(2)]
        k_b = [sb(f"k_b{i}", [128, HEADS, L], BF16) for i in range(2)]
        v = [sb(f"v{i}", [128, 8, 192]) for i in range(2)]
        P_SLOTS = 3
        probs = sb("probs", [128, P_SLOTS, 2, 266])
        att = sb("att", [CHUNK, 2, L])
        den = sb("den", [CHUNK, L])
        pad_rows = sb("pad_rows", [18, L], BF16)
        w_qk = sb("w_qk", [CHUNK, 2, 384])
        w_v = sb("w_v", [CHUNK, 2, 192])
        w_o = sb("w_o", [CHUNK, 2, 192])
        b_v = sb("b_v", [128, 192])
        qk_scale = sb("qk_scale", [128, 3])
        qk_bias = sb("qk_bias", [128, 3])
        b_o = sb("b_o", [CHUNK, 2])
        group_avg = sb("group_avg", [CHUNK, CHUNK])
        ident = sb("ident", [128, 128])
        ones = sb("ones", [128, HEAD])
        den_sel = sb("den_sel", [18, 3, CHUNK], BF16)
        floor = sb("floor", [128, HEADS, 2, 4])
        ln_pad = sb("ln_pad", [128, HEADS, 2, 4])
        m_raw = sb("m_raw", [128, 48])
        m_max = sb("m_max", [128, HEADS, 2, 4])
        m_hi = sb("m_hi", [128, HEADS, 2, 4], BF16)
        m_lo = sb("m_lo", [128, HEADS, 2, 4], BF16)
        pad_arg = sb("pad_arg", [128, HEADS, 2, 4])
        pad_exp = sb("pad_exp", [128, HEADS, 2, 4])
        pad_hi = sb("pad_hi", [128, HEADS, 2, 4], BF16)
        to_rows = sb("to_rows", [128, 2, 5, GROUP * 8])
        rows_bf = sb("rows_bf", [120, 2, 128], BF16)
        stats = sb("stats", [CHUNK, 4, 6])
        moments = sb("moments", [CHUNK, 2, 2])
        g_mom = sb("g_mom", [CHUNK, 2, 2])
        var_eps = sb("var_eps", [CHUNK, 2])
        rstd = sb("rstd", [CHUNK, 2])
        shift = sb("shift", [CHUNK, 2])
        minus_half = sb("minus_half", [CHUNK, 2])
        qk_dram = nc.dram_tensor(f"{tag}_qk_parts", [3, 384, L], BF16).ap()
        row_dram = nc.dram_tensor(f"{tag}_max_rows", [30, L], BF16).ap()

        work = ps("work", [128, 2, 2, HALF])
        acc = ps("acc", [128, L])
        acc_den = ps("acc_den", [128, L])

        consts_loaded, consts_made = sem("consts_loaded"), sem("consts_made")
        x_loaded, res_loaded, out_stored = sem("x_loaded"), sem("res_loaded"), sem("out_stored")
        filled = sem("filled")
        wait_passed = sem("wait_passed")
        stats_seen = sem("stats_seen")
        drained = [sem(f"drained{i}") for i in range(2)]
        norm_step, rstd_made, xn_made = sem("norm_step"), sem("rstd_made"), sem("xn_made")
        high_made, rest_made, mid_made, low_made = sem("high_made"), sem("rest_made"), sem("mid_made"), sem("low_made")
        parts_stored, stacks_loaded = sem("parts_stored"), sem("stacks_loaded")
        max_step, pad_made, small_step = sem("max_step"), sem("pad_made"), sem("small_step")
        rows_made, rows_stored, rows_loaded = sem("rows_made"), sem("rows_stored"), sem("rows_loaded")
        probs_made, probs_used = sem("probs_made"), sem("probs_used")
        group_done, acc_kept = sem("group_done"), sem("acc_kept")
        den_inverted, att_made = sem("den_inverted"), sem("att_made")

        last_pair = batches // 2 - 1

        def is_static(n, v):
            return isinstance(n.it, int) and 2 * n.it + n.s == v

        def has(n, k):
            return not isinstance(n.it, int) or 2 * n.it + n.s + k < batches

        class Use:
            def __init__(self, n, offset):
                self.unit = (A_FILLS * n.s + offset) % 2
                self.number = n.it * (2 * A_FILLS) + (A_FILLS * n.s + offset)
                self.before = n.it * A_FILLS + (A_FILLS * n.s + offset) // 2
                self.none_before = isinstance(self.before, int) and self.before == 0

        ZERO = Batch(0, 0)

        def project_use(n, j):
            return Use(ZERO, 1 + j) if n is None else Use(n, (34 if n.first else 32) + j)

        def a_use(n, i):
            return Use(ZERO, 8 + i) if n is None else Use(n, 53 + i)

        def norm_use(n):
            return Use(ZERO, 0) if n == "start" else Use(ZERO, 32) if n is None else Use(n, 77)

        def rows_use(n):
            return Use(ZERO, 33) if n is None else Use(n, 90 if has(n, 2) else 89)

        def out_use(n_next, i):
            if is_static(n_next, batches):
                return Use(n_next, -2 + i)
            return Use(n_next, (39 if has(n_next, 1) else 31) + i)

        def b_use(n, g, i):
            if not has(n, 1):
                return Use(n, (33, 45)[g] + i)
            return Use(n, (41, 78 if has(n, 2) else 77)[g] + i)

        def await_unit(pe, f):
            if not f.none_before:
                pe.wait_ge(drained[f.unit], f.before)

        def await_all(eng, waits):
            for semaphore, value in waits:
                eng.wait_ge(semaphore, value)
                eng.sem_inc(wait_passed, 1)

        def await_fill(eng, f):
            eng.wait_ge(filled, f.number + 1)

        def await_drained(eng, f):
            eng.wait_ge(drained[f.unit], f.before + 1)

        def after(n):
            return ZERO if n is None else (Batch(n.it, 1) if n.s == 0 else Batch(n.it + 1, 0))

        def before(n):
            return Batch(n.it, 0) if n.s else Batch(n.it - 1, 1)

        def schedule(eng, prologue, main, tail):
            prologue()
            main(Batch(0, 0))
            main(Batch(0, 1))
            if last_pair > 1:
                with eng.Fori(1, last_pair) as it:
                    main(Batch(it, 0))
                    main(Batch(it, 1))
            main(Batch(last_pair, 0))
            main(Batch(last_pair, 1))
            tail(Batch(last_pair + 1, 0))

        def units(i):
            return [divmod(2 * i + k, GROUP) for k in range(2)]

        def image(ap):
            return ap.rearrange("p (s y x) -> p s y x", s=2, x=TILE_W)

        src = x_src.rearrange("b (c p) h w -> b p c (h w)", p=CHUNK)
        dst = x_dst.rearrange("b (c p) h w -> b p c (h w)", p=CHUNK)
        N_CONSTS = 13

        with nc.Block() as block:
            @block.sync
            def _(sp):
                for t, a in ((w_qk, w["w_qk"]), (w_v, w["w_v"]), (w_o, w["w_o"]), (b_v, w["b_v"]),
                             (qk_bias, w["b_qk"]), (b_o, w["b_o"]), (qk_scale, consts["qk_scale"]),
                             (group_avg, consts["group_avg"]), (ident, consts["ident"]),
                             (floor, consts["floor"]), (ln_pad, consts["ln_pad"])):
                    sp.dma_start(t[:], a).then_inc(consts_loaded, 16)
                sp.dma_start(qk[:, 0:2, :], consts["masks"]).then_inc(consts_loaded, 16)
                sp.dma_start(qk[0:18, 2, 0:3 * CHUNK], consts["den_sel"]).then_inc(consts_loaded, 16)

                def load(n):
                    sp.dma_start(x[:, :, :], src[n.count(1, 0)]).then_inc(x_loaded, 16)

                def load_residual(n):
                    sp.dma_start(x_res[:, :, :], src[n.count(1, 0)]).then_inc(res_loaded, 16)

                def store_parts(n):
                    m = after(n)
                    if n is not None:
                        sp.wait_ge(stacks_loaded, m.count(384, 0))
                    for part, (t, made, k) in enumerate(((qk1, high_made, 3), (qk2, mid_made, 1), (qk3, low_made, 3))):
                        sp.wait_ge(made, m.count(k, k))
                        sp.dma_start(qk_dram[part].rearrange("(t p) c -> p t c", p=128), t[:, :, :]).then_inc(parts_stored, 16)

                def load_stacks(n):
                    m = after(n)
                    sp.wait_ge(parts_stored, m.count(48, 48))
                    if n is not None and not n.first:
                        sp.wait_ge(group_done, before(n).count(2, 2))
                    for first_row, k_row, h0, h1 in ((0, 128, 0, 4), (256, 320, 4, 6)):
                        rows = (h1 - h0) * HEAD
                        q = lambda part: qk_dram[part, first_row:first_row + rows, :].rearrange("(h d) t -> d h t", d=HEAD)
                        k = lambda part: qk_dram[part, k_row:k_row + rows, :].rearrange("(h d) t -> d h t", d=HEAD)
                        for base, out, part in ((0, q_a, q(0)), (32, q_a, q(0)), (64, q_a, q(1)), (96, q_a, q(1)),
                                                (0, q_b, q(0)), (32, q_b, q(2)), (0, k_b, k(2)), (32, k_b, k(0)),
                                                (0, k_a, k(0)), (32, k_a, k(1)), (64, k_a, k(0)), (96, k_a, k(1))):
                            sp.dma_start(out[m.s][base:base + 32, h0:h1, :], part).then_inc(stacks_loaded, 16)

                def move_rows(n):
                    m = after(n)
                    await_all(sp, [(rows_made, m.count(1, 1))] + ([(rows_loaded, m.count(32, 0)), (group_done, m.count(2, 0))]
                                                                  if n is not None else []))
                    for g in range(2):
                        sp.dma_start(row_dram[:, :].rearrange("(a h) (t c) -> h a t c", h=HEADS, c=128)[GROUP * g:GROUP * (g + 1)]
                                     .rearrange("h a t c -> a h t c"),
                                     rows_bf[:, g, :]).then_inc(rows_stored, 16)
                    sp.wait_ge(rows_stored, m.count(32, 32))
                    sp.dma_start(q_b[m.s][112:114, :, :], row_dram[0:12, :].rearrange("(a h) t -> a h t", a=2)).then_inc(rows_loaded, 16)
                    sp.dma_start(pad_rows[:, :], row_dram[12:30, :]).then_inc(rows_loaded, 16)

                def store(n_next):
                    await_all(sp, [(drained[f.unit], f.before + 1) for f in (out_use(n_next, 0), out_use(n_next, 1))])
                    sp.dma_start(dst[n_next.count(1, -1)], x_res[:, :, :]).then_inc(out_stored, 16)
                    sp.wait_ge(out_stored, n_next.count(16, 0))

                def prologue():
                    load(ZERO)
                    load_residual(ZERO)
                    store_parts(None)
                    load(Batch(0, 1))
                    load_stacks(None)
                    move_rows(None)

                def main(n):
                    if has(n, 2):
                        sp.wait_ge(xn_made, n.count(1, 2))
                        load(Batch(n.it + 1, n.s))
                    if not n.first:
                        store(n)
                        load_residual(n)
                    if has(n, 1):
                        store_parts(n)
                        load_stacks(n)
                        move_rows(n)

                schedule(sp, prologue, main, store)

            @block.tensor
            def _(pe):
                def norm(n):
                    f = norm_use(n)
                    await_unit(pe, f)
                    pe.wait_ge(norm_step, (ZERO if n == "start" else Batch(0, 1) if n is None else Batch(n.it + 1, n.s)).count(7, 3))
                    nc.tensor.matmul(work[0:CHUNK, f.unit, 0, 0:4], group_avg[:, :],
                                     moments[:, :, :].rearrange("p a b -> p (a b)"), start=True,
                                     stop=True).then_inc(filled, 1)

                def project(n):
                    m = after(n)
                    pe.wait_ge(xn_made, m.count(1, 1))
                    for j in range(3):
                        f = project_use(n, j)
                        await_unit(pe, f)
                        for half in range(2):
                            for c in range(2):
                                last = nc.tensor.matmul(work[:, f.unit, half, :], w_qk[:, c, 128 * j:128 * (j + 1)],
                                                        xn[:, c, half * HALF:(half + 1) * HALF],
                                                        start=(c == 0), stop=(c == 1))
                        last.then_inc(filled, 1)
                    for j in range(4):
                        f = project_use(n, 3 + j)
                        await_unit(pe, f)
                        for i in range(2):
                            for c in range(2):
                                last = nc.tensor.matmul(work[:, f.unit, i, 0:192], xn[:, c, tile_at(TILES[2 * j + i])], w_v[:, c, :],
                                                        start=(c == 0), stop=(c == 1))
                        last.then_inc(filled, 1)

                def scores(f, m, g, i, on_a, on_b, off_a, off_b, rows):
                    await_unit(pe, f)
                    for k, (ti, hh) in enumerate(units(i)):
                        tx = TILES[ti][1]
                        head = GROUP * g + hh
                        r0, r1, own, size, cols = halo(TILES[ti])
                        out = work[:, f.unit, k, :]
                        for part in range(2):
                            for on, off, r, first in ((on_a, off_a, 128, True), (on_b, off_b, rows, False)):
                                tokens = image(off[m.s][0:r, head, :])
                                last = nc.tensor.matmul(
                                    out[:, 0:own] if part == 0 else out[:, own:size], on[m.s][0:r, head, tile_at(TILES[ti])],
                                    off[m.s][0:r, head, 512 * tx + TILE_W * r0:512 * tx + TILE_W * r1] if part == 0
                                    else tokens[:, 1 - tx, r0:r1, cols], start=first, stop=not first)
                    last.then_inc(filled, 1)

                def pass_a(n):
                    m = after(n)
                    pe.wait_ge(stacks_loaded, m.count(384, 384))
                    for i in range(2 * UNIT_PAIRS):
                        scores(a_use(n, i), m, i // UNIT_PAIRS, i % UNIT_PAIRS, q_a, q_b, k_a, k_b, 112)

                def values(n, g, i):
                    slot = i % P_SLOTS
                    pe.wait_ge(probs_made, n.count(24, UNIT_PAIRS * g + i + 1))
                    for k, (ti, hh) in enumerate(units(i)):
                        tx = TILES[ti][1]
                        r0, r1, own, size, cols = halo(TILES[ti])
                        rows = slice(HEAD * hh, HEAD * (hh + 1))
                        head = GROUP * g + hh
                        for part in range(2):
                            p = probs[:, slot, k, 0:own] if part == 0 else \
                                probs[:, slot, k, own:size].rearrange("p (y x) -> p y x", x=PAD)
                            for to, by in ((acc, v[n.s][:, ti, HEAD * head:HEAD * (head + 1)]), (acc_den, ones[:, :])):
                                out = to[rows, 512 * tx + TILE_W * r0:512 * tx + TILE_W * r1] if part == 0 else \
                                    image(to[rows, :])[:, 1 - tx, r0:r1, cols]
                                last = nc.tensor.matmul(out, by, p, start=False, stop=(i == UNIT_PAIRS - 1),
                                                        skip_group_check=True)
                    last.then_inc(probs_used, 1)

                def pass_b(n, g):
                    if not (n.first and g == 0):
                        pe.wait_ge(acc_kept, n.count(2, g))
                    if g == 0:
                        pe.wait_ge(rows_loaded, n.count(32, 32))
                        pe.wait_ge(v_made(n)[0], v_made(n)[1])
                    for half in range(2):
                        t = slice(half * HALF, (half + 1) * HALF)
                        nc.tensor.matmul(acc[0:CHUNK, t], den_sel[:, 2, :], pad_rows[:, t], start=True, stop=False,
                                         skip_group_check=True)
                        nc.tensor.matmul(acc_den[0:CHUNK, t], den_sel[:, g, :], pad_rows[:, t], start=True, stop=False,
                                         skip_group_check=True)
                    for i in range(UNIT_PAIRS + 1):
                        if i < UNIT_PAIRS:
                            scores(b_use(n, g, i), n, g, i, k_a, k_b, q_a, q_b, 114)
                        if i:
                            values(n, g, i - 1)
                    nc.tensor.matmul(acc_den[0:CHUNK, 0:1], den_sel[:, 2, :], pad_rows[:, 0:1], start=False, stop=True,
                                     skip_group_check=True).then_inc(group_done, 1)

                def v_made(n):
                    f = project_use(None if n.first else before(n), 6)
                    return drained[f.unit], f.before + 1

                def project_out(n_next):
                    pe.wait_ge(att_made, n_next.count(2, 0))
                    for co in range(2):
                        f = out_use(n_next, co)
                        await_unit(pe, f)
                        for half in range(2):
                            for ci in range(2):
                                last = nc.tensor.matmul(work[0:CHUNK, f.unit, half, :],
                                                        w_o[:, ci, co * CHUNK:(co + 1) * CHUNK],
                                                        att[:, ci, half * HALF:(half + 1) * HALF],
                                                        start=(ci == 0), stop=(ci == 1))
                        last.then_inc(filled, 1)

                def to_row_layout(n):
                    f = rows_use(n)
                    await_unit(pe, f)
                    pe.wait_ge(max_step, after(n).count(5, 5))
                    for g in range(2):
                        last = nc.tensor.transpose(work[0:120, f.unit, g, 0:128],
                                                   to_rows[:, g, :, :].rearrange("p a b -> p (a b)"), ident[:, :])
                    last.then_inc(filled, 1)

                def prologue():
                    norm("start")
                    project(None)
                    pass_a(None)
                    norm(None)
                    to_row_layout(None)

                def main(n):
                    if has(n, 1):
                        project(n)
                    if not n.first:
                        project_out(n)
                    pass_b(n, 0)
                    if has(n, 1):
                        pass_a(n)
                    if has(n, 2):
                        norm(n)
                    pass_b(n, 1)
                    if has(n, 1):
                        to_row_layout(n)

                pe.wait_ge(consts_loaded, 16 * N_CONSTS)
                pe.wait_ge(consts_made, 3)
                schedule(pe, prologue, main, project_out)

            @block.scalar
            def _(act):
                def normalise(m):
                    act.wait_ge(norm_step, m.count(7, 7))
                    if not m.first:
                        f = project_use(None if is_static(m, 1) else before(before(m)), 6)
                        await_fill(act, f)
                    for c in range(2):
                        last = nc.scalar.activation(image(xn[:, c, :]), x[:, c, :].rearrange("p (y s x) -> p s y x", s=2, x=TILE_W), ACT.Identity,
                                                    scale=rstd[:, c:c + 1], bias=shift[:, c:c + 1])
                    last.then_inc(xn_made, 1)

                def take_qk(n):
                    m = after(n)
                    if n is not None:
                        act.wait_ge(low_made, m.count(3, 0))
                        act.wait_ge(parts_stored, m.count(48, 0))
                    for j in range(3):
                        f = project_use(n, j)
                        await_fill(act, f)
                        whole = work[:, f.unit, :, :].rearrange("p a b -> p (a b)")
                        nc.scalar.activation(qk1[:, j, :], whole, ACT.Identity, scale=qk_scale[:, j:j + 1],
                                             bias=qk_bias[:, j:j + 1]).then_inc(high_made, 1)
                        nc.scalar.activation(qk[:, j, :], whole, ACT.Identity, scale=qk_scale[:, j:j + 1],
                                             bias=qk_bias[:, j:j + 1]).then_inc(drained[f.unit], 1)

                def middle_part(n):
                    act.wait_ge(rest_made, after(n).count(3, 3))
                    nc.scalar.activation(qk2[:, :, :], qk[:, :, :], ACT.Copy).then_inc(mid_made, 1)

                def exps(n, g, i):
                    f = b_use(n, g, i)
                    await_fill(act, f)
                    k = UNIT_PAIRS * g + i
                    if not (n.first and k < P_SLOTS):
                        act.wait_ge(probs_used, n.count(24, k - P_SLOTS + 1))
                    size = halo(TILES[units(i)[0][0]])[3]
                    nc.scalar.activation(probs[:, i % P_SLOTS, :, 0:size], work[:, f.unit, :, 0:size],
                                         ACT.Exp).then_inc(probs_made, 1)
                    act.wait_ge(probs_made, n.count(24, k + 1))
                    act.sem_inc(drained[f.unit], 1)

                def keep_acc(n, g):
                    act.wait_ge(group_done, n.count(2, g + 1))
                    if g == 0 and not n.first:
                        await_fill(act, out_use(n, 1))
                    if not (n.first and g == 0):
                        act.wait_ge(att_made, n.count(2, g))
                    nc.scalar.activation(att[:, g, :], acc[0:CHUNK, :], ACT.Copy)
                    nc.scalar.activation(den[:, :], acc_den[0:CHUNK, :], ACT.Copy).then_inc(acc_kept, 1)

                def padding_terms(n):
                    act.wait_ge(max_step, after(n).count(5, 3))
                    nc.scalar.activation(pad_exp[:, :, :, :], pad_arg[:, :, :, :], ACT.Exp).then_inc(pad_made, 1)

                def take_rows(n):
                    f = rows_use(n)
                    await_fill(act, f)
                    if n is not None:
                        act.wait_ge(rows_stored, after(n).count(32, 0))
                    nc.scalar.activation(rows_bf[:, :, :], work[0:120, f.unit, :, 0:128], ACT.Copy).then_inc(rows_made, 1)
                    act.wait_ge(rows_made, after(n).count(1, 1))
                    act.sem_inc(drained[f.unit], 1)

                def prologue():
                    normalise(ZERO)
                    take_qk(None)
                    middle_part(None)
                    padding_terms(None)
                    normalise(Batch(0, 1))
                    take_rows(None)

                def main(n):
                    if has(n, 1):
                        take_qk(n)
                    for i in range(UNIT_PAIRS):
                        exps(n, 0, i)
                        if i == 6 and has(n, 1):
                            middle_part(n)
                    keep_acc(n, 0)
                    for i in range(UNIT_PAIRS):
                        exps(n, 1, i)
                        if i == 3 and has(n, 1):
                            padding_terms(n)
                        if i == 7 and has(n, 2):
                            normalise(Batch(n.it + 1, n.s))
                    keep_acc(n, 1)
                    if has(n, 1):
                        take_rows(n)

                act.wait_ge(consts_loaded, 16 * N_CONSTS)
                act.wait_ge(consts_made, 3)
                schedule(act, prologue, main, lambda n: None)

            @block.vector
            def _(dve):
                def norm_stats(m):
                    k = m.count(7, 0)
                    dve.wait_ge(x_loaded, m.count(16, 16))
                    for i in range(4):
                        c, half = divmod(i, 2)
                        last = nc.vector.bn_stats(stats[:, i, :], x[:, c, half * HALF:(half + 1) * HALF])
                    last.then_inc(norm_step, 1)
                    dve.wait_ge(norm_step, k + 1)
                    dve.sem_inc(stats_seen, 1)
                    for c in range(2):
                        last = nc.vector.bn_aggr(moments[:, c, :], stats[:, 2 * c:2 * c + 2, :].rearrange("p a b -> p (a b)"))
                    last.then_inc(norm_step, 1)
                    dve.wait_ge(norm_step, k + 2)
                    for c in range(2):
                        last = nc.vector.scalar_tensor_tensor(moments[:, c, 1:2], moments[:, c, 0:1],
                                                              moments[:, c, 0:1], moments[:, c, 1:2], ALU.mult, ALU.add)
                    last.then_inc(norm_step, 1)

                def norm_finish(f, m):
                    k = m.count(7, 0)
                    await_fill(dve, f)
                    nc.vector.tensor_copy(g_mom[:, :, :].rearrange("p a b -> p (a b)"),
                                          work[0:CHUNK, f.unit, 0, 0:4]).then_inc(drained[f.unit], 1)
                    await_drained(dve, f)
                    for c in range(2):
                        last = nc.vector.scalar_tensor_tensor(var_eps[:, c:c + 1], g_mom[:, c, 0:1], g_mom[:, c, 0:1],
                                                              g_mom[:, c, 1:2], ALU.mult, ALU.subtract)
                    last.then_inc(norm_step, 1)
                    dve.wait_ge(norm_step, k + 4)
                    nc.vector.tensor_scalar(var_eps[:, :], var_eps[:, :], -1.0, 1e-5, ALU.mult, ALU.add).then_inc(norm_step, 1)
                    dve.wait_ge(rstd_made, m.count(1, 1))
                    nc.vector.scalar_tensor_tensor(shift[:, :], g_mom[:, :, 0], -1.0, rstd[:, :],
                                                   ALU.mult, ALU.mult).then_inc(norm_step, 2)

                def take_v(n):
                    m = after(n)
                    if n is not None and not n.first:
                        dve.wait_ge(group_done, before(n).count(2, 2))
                    for j in range(4):
                        f = project_use(n, 3 + j)
                        await_fill(dve, f)
                        nc.vector.tensor_tensor(v[m.s][:, 2 * j:2 * j + 2, :], work[:, f.unit, :, 0:192],
                                                b_v[:, None, :].to_broadcast([128, 2, 192]), ALU.add).then_inc(drained[f.unit], 1)

                def maxima(n):
                    m = after(n)
                    for i in range(2 * UNIT_PAIRS):
                        f = a_use(n, i)
                        await_fill(dve, f)
                        size = halo(TILES[units(i % UNIT_PAIRS)[0][0]])[3]
                        nc.vector.tensor_reduce(m_raw[:, 2 * i:2 * i + 2], work[:, f.unit, :, 0:size],
                                                AX.X, ALU.max).then_inc(drained[f.unit], 1)
                    for i in (2 * UNIT_PAIRS - 2, 2 * UNIT_PAIRS - 1):
                        await_drained(dve, a_use(n, i))
                    for g in range(2):
                        for size, rows in ((0, slice(0, 4, 3)), (1, slice(1, 3, 1))):
                            view = lambda t: t[:, GROUP * g:GROUP * (g + 1), :, rows].rearrange("p h x y -> p y x h")
                            last = nc.vector.tensor_tensor(
                                view(m_max),
                                m_raw[:, 24 * g + 12 * size:24 * g + 12 * (size + 1)].rearrange("p (y x h) -> p y x h", y=2, x=2),
                                view(floor), ALU.max)
                    last.then_inc(max_step, 1)
                    dve.wait_ge(max_step, m.count(5, 1))
                    if n is not None:
                        await_fill(dve, rows_use(None if n.first else before(n)))
                    nc.vector.tensor_scalar(m_hi[:], m_max[:], -1.0, None, ALU.mult).then_inc(max_step, 1)
                    dve.wait_ge(max_step, m.count(5, 2))
                    nc.vector.scalar_tensor_tensor(flat(m_lo), flat(m_max), -1.0, flat(m_hi), ALU.mult, ALU.subtract)
                    nc.vector.tensor_tensor(pad_arg[:], m_hi[:], ln_pad[:], ALU.add)
                    nc.vector.tensor_copy(rows4(0), by_group(m_hi)).then_inc(small_step, 1)
                    dve.wait_ge(small_step, m.count(4, 1))
                    nc.vector.tensor_copy(rows4(1), by_group(m_lo))
                    nc.vector.tensor_tensor(pad_arg[:], pad_arg[:], m_lo[:], ALU.add).then_inc(max_step, 1)

                def rows4(part):
                    return to_rows[:, :, part, :]

                def by_group(t):
                    return t[:].rearrange("p (g h) x y -> p g (h x y)", g=2)

                def flat(t):
                    return t[:].rearrange("p a b c -> p (a b c)")

                def split_padding(n):
                    m = after(n)
                    dve.wait_ge(pad_made, m.count(1, 1))
                    nc.vector.tensor_copy(pad_hi[:], pad_exp[:]).then_inc(small_step, 1)
                    dve.wait_ge(small_step, m.count(4, 2))
                    nc.vector.tensor_copy(rows4(2), by_group(pad_hi))
                    nc.vector.tensor_tensor(pad_exp[:], pad_exp[:], pad_hi[:], ALU.subtract).then_inc(small_step, 1)
                    dve.wait_ge(small_step, m.count(4, 3))
                    nc.vector.tensor_copy(pad_hi[:], pad_exp[:]).then_inc(small_step, 1)
                    dve.wait_ge(small_step, m.count(4, 4))
                    nc.vector.tensor_copy(rows4(3), by_group(pad_hi))
                    nc.vector.tensor_tensor(rows4(4), by_group(pad_exp), by_group(pad_hi), ALU.subtract).then_inc(max_step, 2)

                def divide(n, g):
                    dve.wait_ge(acc_kept, n.count(2, g + 1))
                    nc.vector.reciprocal(den[:, :], den[:, :]).then_inc(den_inverted, 1)
                    dve.wait_ge(den_inverted, n.count(2, g + 1))
                    nc.vector.tensor_tensor(att[:, g, :], att[:, g, :], den[:, :], ALU.mult).then_inc(att_made, 1)

                def residual(n_next):
                    dve.wait_ge(res_loaded, n_next.count(16, 0))
                    for co in range(2):
                        f = out_use(n_next, co)
                        await_fill(dve, f)
                        for tx in range(2):
                            old = x_res[:, co, :].rearrange("p (y s x) -> p s y x", s=2, x=TILE_W)[:, tx]
                            last = nc.vector.scalar_tensor_tensor(
                                old, work[0:CHUNK, f.unit, tx, :].rearrange("p (y x) -> p y x", x=TILE_W),
                                b_o[:, co:co + 1], old, ALU.add, ALU.add)
                        last.then_inc(drained[f.unit], 1)

                def prologue():
                    norm_stats(ZERO)
                    norm_finish(norm_use("start"), ZERO)
                    take_v(None)
                    norm_stats(Batch(0, 1))
                    maxima(None)
                    norm_finish(norm_use(None), Batch(0, 1))
                    split_padding(None)

                def main(n):
                    if not n.first:
                        divide(before(n), 1)
                    if has(n, 1):
                        take_v(n)
                    if not n.first:
                        residual(n)
                    if has(n, 2):
                        norm_stats(Batch(n.it + 1, n.s))
                    if has(n, 1):
                        maxima(n)
                    if has(n, 2):
                        norm_finish(norm_use(n), Batch(n.it + 1, n.s))
                    divide(n, 0)
                    if has(n, 1):
                        split_padding(n)

                def tail(n_next):
                    divide(before(n_next), 1)
                    residual(n_next)

                nc.vector.memset(minus_half[:, :], -0.5)
                nc.vector.memset(ones[:, :], 1.0).then_inc(consts_made, 1)
                dve.wait_ge(consts_loaded, 16 * N_CONSTS)
                nc.vector.tensor_tensor(qk_bias[:, :], qk_bias[:, :], qk_scale[:, :], ALU.mult)
                for i in range(2):
                    for head in range(HEADS):
                        nc.vector.tensor_copy(q_b[i][64:128, head, :], qk[64:128, 0, :])
                        nc.vector.tensor_copy(k_b[i][64:128, head, :], qk[64:128, 1, :])
                nc.vector.tensor_copy(den_sel[:, :, :].rearrange("p a b -> p (a b)"), qk[0:18, 2, 0:3 * CHUNK]).then_inc(consts_made, 2)
                dve.wait_ge(consts_made, 3)
                schedule(dve, prologue, main, tail)

            @block.gpsimd
            def _(pool):
                def split(n):
                    m = after(n)
                    for j in range(3):
                        await_drained(pool, project_use(n, j))
                        nc.gpsimd.tensor_tensor(qk[:, j, :], qk[:, j, :], qk1[:, j, :], ALU.subtract).then_inc(rest_made, 1)
                    pool.wait_ge(mid_made, m.count(1, 1))
                    if n is not None:
                        pool.wait_ge(parts_stored, m.count(48, 0))
                    for j in range(3):
                        nc.gpsimd.tensor_tensor(qk3[:, j, :], qk[:, j, :], qk2[:, j, :], ALU.subtract).then_inc(low_made, 1)

                def power(m):
                    pool.wait_ge(norm_step, m.count(7, 5))
                    nc.gpsimd.tensor_tensor(rstd[:, :], var_eps[:, :], minus_half[:, :], ALU.pow).then_inc(rstd_made, 1)

                def prologue():
                    power(ZERO)
                    split(None)
                    power(Batch(0, 1))

                def main(n):
                    if has(n, 1):
                        split(n)
                    if has(n, 2):
                        power(Batch(n.it + 1, n.s))

                pool.wait_ge(consts_made, 3)
                schedule(pool, prologue, main, lambda n: None)


def shape_constants():
    p = np.arange(128)
    out = {}
    out["rep_sel"] = np.stack([(np.arange(96)[:, None] == 32 * j + p[None, :] % 32) for j in range(3)], 1).astype(np.float32)
    out["state_sum"] = (p[:, None] % 32 == np.arange(32)[None, :]).astype(np.float32)
    g = np.arange(96) // 6
    out["group_avg"] = ((g[:, None] == g[None, :]) / 6.0).astype(np.float32)
    row, quad = p % 32, p // 32
    out["bc_sel"] = np.stack([((row[:, None] == (t // 4) * 16 + (t % 4) * 4 + p[None, :] // 32) & (quad[:, None] != 2))
                              for t in range(8)], 1).astype(np.float32)
    BIG = 1e30
    yy, xx = np.divmod(np.arange(1024), 32)
    q_rows, k_rows = np.zeros((128, 1024), np.float32), np.zeros((128, 1024), np.float32)
    for r in range(16):
        q_rows[64 + r] = yy % 16 == r
        d = (yy - r) % 16
        k_rows[64 + r] = np.where(np.minimum(d, 16 - d) <= 3, 0.0, -BIG)
    for r in range(32):
        q_rows[80 + r] = xx == r
        k_rows[80 + r] = np.where(np.abs(xx - r) <= 3, 0.0, -BIG)
    k_rows[112:114] = 1.0
    halves = lambda a: a.reshape(128, 32, 2, 16).transpose(0, 2, 1, 3).reshape(128, 1024)
    out["masks"] = np.stack([halves(q_rows), halves(k_rows)], 1)
    out["qk_scale"] = np.stack([np.full(128, 32 ** -0.5), np.ones(128), np.where(p < 64, 32 ** -0.5, 1.0)], 1).astype(np.float32)
    out["ident"] = np.eye(128, dtype=np.float32)
    inside = lambda c: np.minimum(31, c + 3) - np.maximum(0, c - 3) + 1
    y, x = p // 16, p % 16
    padded = np.stack([np.stack([49 - inside(8 * ty + y) * inside(16 * tx + x) for ty in range(4)], 1) for tx in range(2)], 1)
    padded = np.repeat(padded[:, None], 6, 1)
    out["floor"] = np.where(padded > 0, 0.0, -BIG).astype(np.float32)
    out["ln_pad"] = np.where(padded > 0, np.log(np.maximum(padded, 1)), -BIG).astype(np.float32)
    r18, c96 = np.arange(18), np.arange(96)
    out["den_sel"] = np.concatenate([(r18[:, None] % 6 == 3 * g + c96[None] // 32) for g in range(2)]
                                    + [np.zeros((18, 96))], 1).astype(np.float32)
    out["strip_avg"] = ((p[:, None] % 16 == p[None, :] % 16) / 8.0).astype(np.float32)
    r, dx = np.divmod(np.arange(52), 13)
    centre = (dx[:, None] == 6) & (5 + np.arange(6)[None, :] == 6 + r[:, None])
    out["centre"] = np.repeat(centre.astype(np.float32), 192, 1)
    rule = np.zeros((116, 4, 63), np.float32)
    for base in (0, 64):
        rule[base:base + 52] = (r[:, None, None] == np.arange(4)[None, :, None]) & (dx[:, None, None] == np.arange(63)[None, None] - 25)
    out["toeplitz_rule"] = rule.reshape(116, 252)
    return out


def conv_weights(w_large, w_small, *norms):
    def laid(w):
        k = w.shape[-1]
        padded = np.zeros((19, 13, w.shape[0]), w.dtype)
        y0, x0 = 3 + (13 - k) // 2, (13 - k) // 2
        padded[y0:y0 + k, x0:x0 + k] = w[:, 0].transpose(1, 2, 0)
        return np.ascontiguousarray(padded[::-1])
    g, b, m, v = (np.stack(norms[i::4]) for i in range(4))
    rows = np.stack([g, m, b]).reshape(1, -1)
    return {"large": laid(w_large), "small": laid(w_small), "variances": v.reshape(96, 6),
            "scales": np.ascontiguousarray(np.broadcast_to(rows, (128, rows.shape[1])))}


def ssm_weights(W_proj, b_proj, A_log, D, dt_bias, W_out, b_out):
    wt = W_proj.T
    wt = np.concatenate([wt[:, 0:96], wt[:, 384:416], wt[:, 96:192], wt[:, 192:384]], 1)
    return {
        "w_proj": np.ascontiguousarray(wt.reshape(2, 96, 416).transpose(1, 0, 2)),
        "w_out": np.ascontiguousarray(W_out.T.reshape(2, 96, 192).transpose(1, 0, 2)),
        "a_log": np.ascontiguousarray(A_log.reshape(6, 32, 4, 4).transpose(3, 1, 0, 2).reshape(128, 24)),
        "vecs": np.ascontiguousarray(np.concatenate([v.reshape(2, 96).T for v in (b_proj[0:192], b_proj[192:384], dt_bias, D, b_out)], 1)),
        "bc_bias": np.ascontiguousarray(b_proj[384:416].reshape(32, 1)),
    }


def attention_weights(w_qkv, b_qkv, w_proj, b_proj):
    chunks = lambda w: np.ascontiguousarray(w.T.reshape(2, 96, w.shape[0]).transpose(1, 0, 2))
    order = np.concatenate([np.arange(0, 128), np.arange(192, 320), np.arange(128, 192), np.arange(320, 384)])
    return {
        "w_qk": chunks(w_qkv[order]),
        "w_v": chunks(w_qkv[384:576]),
        "w_o": chunks(w_proj),
        "b_v": np.ascontiguousarray(np.broadcast_to(b_qkv[384:576], (128, 192))),
        "b_qk": np.ascontiguousarray(b_qkv[order].reshape(3, 128).T),
        "b_o": np.ascontiguousarray(b_proj.reshape(2, 96).T),
    }


def program(nc, x, out, weights, consts):
    between = [nc.dram_tensor(f"x_after_l{i}", list(x.shape), F32).ap() for i in range(3)]
    conv_layer(nc, "l0", x, between[0], weights["l0"], consts)
    attention(nc, "l1", between[0], between[1], weights["l1"], consts, x.shape[0])
    ssm_layer(nc, "l2", between[1], between[2], weights["l2"], consts, x.shape[0])
    ssm_layer(nc, "l3", between[2], out, weights["l3"], consts, x.shape[0])


def kernel(**inputs):
    import concourse.bacc as bacc
    from concourse.bass_utils import run_bass_kernel_spmd

    a = {name: np.ascontiguousarray(value) for name, value in inputs.items()}
    of = lambda layer, names: [a[f"{layer}_conv_{name}"] for name in names.split()]
    weights = {
        "l0": conv_weights(*of("L0", "w_large w_small g_l b_l m_l v_l g_s b_s m_s v_s g_i b_i m_i v_i")),
        "l1": attention_weights(*of("L1", "w_qkv b_qkv w_proj b_proj")),
        "l2": ssm_weights(*of("L2", "W_proj b_proj A_log D dt_bias W_out b_out")),
        "l3": ssm_weights(*of("L3", "W_proj b_proj A_log D dt_bias W_out b_out")),
    }
    nc = bacc.Bacc("TRN2", target_bir_lowering=False, num_devices=1)
    arrays = {}

    def dram(name, value):
        arrays[name] = value
        return nc.dram_tensor(name, value.shape, mybir.dt.from_np(value.dtype), kind="ExternalInput").ap()

    x = dram("x", a["x"])
    w = {layer: {k: dram(f"{layer}_{k}_in", v) for k, v in named.items()} for layer, named in weights.items()}
    consts = {k: dram(f"const_{k}", v) for k, v in shape_constants().items()}
    out = nc.dram_tensor("out", a["x"].shape, F32, kind="ExternalOutput").ap()
    program(nc, x, out, w, consts)
    return run_bass_kernel_spmd(nc, [arrays], core_ids=[0]).results[0]["out"]
```

```python
import numpy as np
from contextlib import ExitStack
import concourse.bass as bass
from concourse import mybir

F32 = mybir.dt.float32
BF16 = mybir.dt.bfloat16
ALU = mybir.AluOpType
ACT = mybir.ActivationFunctionType
AX = mybir.AxisListType


TAPS, STRIP, STRIPS, IMAGES = 13, 4, 8, 16
ROWS_PER_WINDOW, WINDOWS = 4, 4
J = 16
STEP, QUAD, QUADS = 12, 4, 3
GROUP_CH = 6
STEPS = 192 // STEP
T_FILLS, X_PER_FILL = 8, 4
KT = 116


class Step:

    def __init__(self, it, s):
        self.it, self.s = it, s
        self.first = isinstance(it, int) and it == 0 and s == 0

    def count(self, per_step, more):
        return self.it * (2 * per_step) + (self.s * per_step + more)

    def channel(self, more):
        return self.it * (2 * STEP) + (self.s * STEP + more)


def conv_layer(nc, tag, x_src, x_dst, w, consts):
    ctx = ExitStack()
    with ctx:
        sb = lambda name, shape, dt=F32: ctx.enter_context(nc.sbuf_tensor(f"{tag}_{name}", shape, dt))
        ps = lambda name, shape: ctx.enter_context(nc.psum_tensor(f"{tag}_{name}", shape, F32))
        sem = lambda name: ctx.enter_context(nc.semaphore(f"{tag}_{name}"))
        PIX = STRIP * 32
        TAP_ROWS = ROWS_PER_WINDOW * TAPS
        COLS = (STRIPS + 3) * IMAGES
        KERNEL = 192 * J

        x = sb("x", [128, 192, PIX])
        toeplitz = [sb(f"toeplitz{i}", [128, STEP, 32, J]) for i in range(2)]
        xn = sb("xn", [128, 2, STEP, PIX])
        strips_t = [sb(f"strips_t{i}", [128, QUAD, COLS]) for i in range(2)]
        w_hi_mid = sb("w_hi_mid", [KT, 192, J], BF16)
        w_low = sb("w_low", [KT, 192, J], BF16)
        select = sb("select", [KT, 32, 128], BF16)
        shift_all = sb("shift_all", [128, 192])
        ident = sb("ident", [128, 128])
        strip_avg = sb("strip_avg", [128, 128])
        stats = sb("stats", [128, 4, 2, 6])
        moments = sb("moments", [128, 4, 2])
        g_mom = sb("g_mom", [128, 4, 2])
        var_eps = sb("var_eps", [128, 4])
        rstd = sb("rstd", [128, 4])
        shift = sb("shift", [128, 4])
        minus_half = sb("minus_half", [128, 6])
        variances = sb("variances", [96, 6])
        factors_dram = nc.dram_tensor(f"{tag}_factors", [1, 3 * 192], F32).ap()
        room0 = toeplitz[1][:].rearrange("p c x j -> p (c x j)")
        room1 = xn[:].rearrange("p a c x -> p (a c x)")
        w_large = room0[0:TAP_ROWS, 0:KERNEL]
        scales = room0[:, KERNEL:KERNEL + 12 * 192]
        w_small = room1[0:TAP_ROWS, 0:6 * 192]
        centre = room1[0:TAP_ROWS, 6 * 192:2 * 6 * 192]
        toeplitz_rule = room1[0:KT, 2304:2304 + 4 * 63]
        high_f32 = room1[0:TAP_ROWS, 0:KERNEL]

        t_ps = ps("t_ps", [128, 2, X_PER_FILL, 256])
        tr_ps = ps("tr_ps", [128, 2, 512])
        out_ps = ps("out_ps", [128, 2, 512])

        consts_loaded, weights_step, power_made = sem("consts_loaded"), sem("weights_step"), sem("power_made")
        variances_loaded = sem("variances_loaded")
        factors_stored, factors_loaded = sem("factors_stored"), sem("factors_loaded")
        weights_made, x_loaded, stored = sem("weights_made"), sem("x_loaded"), sem("stored")
        norm_step, averaged, rstd_made, xn_made = sem("norm_step"), sem("averaged"), sem("rstd_made"), sem("xn_made")
        shifted = sem("shifted")
        stats_seen = sem("stats_seen")
        transposed, strips_made = sem("transposed"), sem("strips_made")
        t_filled, t_drained = sem("t_filled"), sem("t_drained")
        conv_done, added = sem("conv_done"), sem("added")

        PAIRS_OF_STEPS = STEPS // 2
        src = x_src.rearrange("b c h w -> b c (h w)")
        dst = x_dst.rearrange("b c h w -> b c (h w)")
        N_CONSTS = 13

        def schedule(eng, step):
            for s in range(2):
                step(Step(0, s))
            with eng.Fori(1, PAIRS_OF_STEPS - 1) as it:
                for s in range(2):
                    step(Step(it, s))
            for s in range(2):
                step(Step(PAIRS_OF_STEPS - 1, s))

        def is_step(k, number):
            return isinstance(k.it, int) and 2 * k.it + k.s == number

        def has_next(k):
            return not is_step(k, STEPS - 1)

        def has_next_pair(k):
            return not (isinstance(k.it, int) and k.it == PAIRS_OF_STEPS - 1)

        def channels(k, first, n):
            c0 = k.channel(first)
            return slice(c0, c0 + n) if isinstance(c0, int) else bass.ds(c0, n)

        with nc.Block() as block:
            @block.sync
            def _(sp):
                for r in range(ROWS_PER_WINDOW):
                    sp.dma_start(w_large[TAPS * r:TAPS * (r + 1), :].rearrange("p (j c) -> p j c", j=J),
                                 w["large"][3 - r:3 - r + J].rearrange("j x c -> x j c")).then_inc(consts_loaded, 16)
                    sp.dma_start(w_small[TAPS * r:TAPS * (r + 1), :].rearrange("p (j c) -> p j c", j=6),
                                 w["small"][8 - r:8 - r + 6].rearrange("j x c -> x j c")).then_inc(consts_loaded, 16)
                sp.dma_start(variances[:, :], w["variances"]).then_inc(variances_loaded, 16)
                for t, a in ((scales[:, 0:9 * 192], w["scales"]), (centre, consts["centre"]), (toeplitz_rule, consts["toeplitz_rule"]),
                             (ident[:], consts["ident"]), (strip_avg[:], consts["strip_avg"])):
                    sp.dma_start(t, a).then_inc(consts_loaded, 16)

                def load(first_pair):
                    for strip in range(STRIPS):
                        c0 = first_pair * (2 * STEP)
                        sl = slice(c0, c0 + 2 * STEP) if isinstance(c0, int) else bass.ds(c0, 2 * STEP)
                        sp.dma_start(x[IMAGES * strip:IMAGES * (strip + 1), sl, :],
                                     src[:, sl, PIX * strip:PIX * (strip + 1)]).then_inc(x_loaded, 16)

                def store(pair):
                    sp.wait_ge(added, pair * (2 * QUADS) + 2 * QUADS)
                    c0 = pair * (2 * STEP)
                    sl = slice(c0, c0 + 2 * STEP) if isinstance(c0, int) else bass.ds(c0, 2 * STEP)
                    for strip in range(STRIPS):
                        sp.dma_start(dst[:, sl, PIX * strip:PIX * (strip + 1)],
                                     x[IMAGES * strip:IMAGES * (strip + 1), sl, :]).then_inc(stored, 16)

                sp.wait_ge(power_made, 2)
                sp.dma_start(factors_dram[0, :].rearrange("(p k) -> p k", k=6), variances[:, :]).then_inc(factors_stored, 16)
                sp.wait_ge(factors_stored, 16)
                sp.dma_start(scales[:, 9 * 192:12 * 192], factors_dram[:, :].to_broadcast([128, 3 * 192])).then_inc(factors_loaded, 16)
                load(0)
                with sp.Fori(1, PAIRS_OF_STEPS) as pair:
                    sp.wait_ge(x_loaded, pair * (16 * STRIPS))
                    load(pair)
                with sp.Fori(0, PAIRS_OF_STEPS) as pair:
                    store(pair)
                sp.wait_ge(stored, 16 * STRIPS * PAIRS_OF_STEPS)

            @block.tensor
            def _(pe):
                def average(pair):
                    pe.wait_ge(norm_step, pair * 8 + 4)
                    nc.tensor.matmul(out_ps[:, 1, 0:8], strip_avg[:, :], moments[:].rearrange("p a b -> p (a b)"),
                                     start=True, stop=True).then_inc(averaged, 1)

                def transposes(k, q):
                    half, quad = (k.s, q) if q < QUADS else (1 - k.s, 0)
                    slot = (QUADS * k.s + q) % 2
                    if quad == 0:
                        pe.wait_ge(xn_made, k.count(1, 1 if q == 0 else 2))
                    if not (isinstance(k.it, int) and k.it == 0 and QUADS * k.s + q < 2):
                        pe.wait_ge(strips_made, k.count(QUADS, q - 1))
                    for i in range(QUAD):
                        last = nc.tensor.transpose(tr_ps[:, slot, PIX * i:PIX * (i + 1)],
                                                   xn[:, half, QUAD * quad + i, :], ident[:, :])
                    last.then_inc(transposed, 1)

                def build(k, fills):
                    for i in fills:
                        unit = i % 2
                        if k is None:
                            if i >= 2:
                                pe.wait_ge(t_drained, i - 1)
                            cs = slice(0, STEP)
                        else:
                            pe.wait_ge(t_drained, k.count(T_FILLS, T_FILLS + i - 1))
                            cs = channels(k, STEP, STEP)
                        for xi in range(X_PER_FILL):
                            for part, t in enumerate((w_hi_mid, w_low)):
                                last = nc.tensor.matmul(t_ps[:, unit, xi, 0:192],
                                                        select[:, X_PER_FILL * i + xi, :], t[:, cs, :],
                                                        start=(part == 0), stop=(part == 1))
                        last.then_inc(t_filled, 1)

                def convolve(k, q):
                    slot = (QUADS * k.s + q) % 2
                    if q == 0:
                        pe.wait_ge(t_drained, k.count(T_FILLS, T_FILLS))
                    pe.wait_ge(strips_made, k.count(QUADS, q + 1))
                    if not (isinstance(k.it, int) and k.it == 0 and QUADS * k.s + q < 2):
                        pe.wait_ge(added, k.count(QUADS, q - 1))
                    for i in range(QUAD):
                        for o in range(WINDOWS):
                            first = 4 * (WINDOWS - 1 - o)
                            last = nc.tensor.matmul(out_ps[:, slot, PIX * i:PIX * (i + 1)],
                                                    strips_t[slot][:, i, IMAGES * o:IMAGES * o + 128],
                                                    toeplitz[k.s][:, QUAD * q + i, :, first:first + 4],
                                                    start=(o == 0), stop=(o == WINDOWS - 1))
                    last.then_inc(conv_done, 1)

                def step(k):
                    for q in range(QUADS):
                        if q + 1 < QUADS or has_next(k):
                            transposes(k, q + 1)
                        if has_next(k):
                            build(k, range(3 * q, min(3 * q + 3, T_FILLS)))
                        if k.s == 0 and q == 1 and has_next_pair(k):
                            if not k.first:
                                pe.wait_ge(added, k.count(QUADS, 0))
                            average(k.it + 1)
                            pe.wait_ge(norm_step, k.it * 8 + 13)
                        convolve(k, q)

                pe.wait_ge(consts_loaded, 16 * N_CONSTS)
                average(0)
                pe.wait_ge(weights_made, 1)
                build(None, range(T_FILLS))
                transposes(Step(0, 0), 0)
                schedule(pe, step)

            @block.scalar
            def _(act):
                def evacuate(k, i):
                    buf = 0 if k is None else 1 - k.s
                    act.wait_ge(t_filled, i + 1 if k is None else k.count(T_FILLS, T_FILLS + i + 1))
                    if k is not None and i == 0 and not k.first:
                        act.wait_ge(conv_done, k.count(QUADS, 0))
                    nc.scalar.activation(
                        toeplitz[buf][:, :, X_PER_FILL * i:X_PER_FILL * (i + 1), :].rearrange("p c x j -> p x c j"),
                        t_ps[:, i % 2, :, 0:192].rearrange("p x (c j) -> p x c j", j=J),
                        ACT.Copy).then_inc(t_drained, 1)

                def step(k):
                    if has_next(k):
                        for i in range(T_FILLS):
                            evacuate(k, i)

                for i in range(T_FILLS):
                    evacuate(None, i)
                schedule(act, step)

            @block.vector
            def _(dve):
                def norm_stats(pair, cs):
                    dve.wait_ge(x_loaded, pair * (16 * STRIPS) + 16 * STRIPS)
                    for g in range(4):
                        for half in range(2):
                            last = nc.vector.bn_stats(stats[:, g, half, :],
                                                      x[:, cs(GROUP_CH * g + 3 * half, 3), :].rearrange("p c x -> p (c x)"))
                    last.then_inc(norm_step, 1)
                    dve.wait_ge(norm_step, pair * 8 + 1)
                    dve.sem_inc(stats_seen, 1)
                    for g in range(4):
                        last = nc.vector.bn_aggr(moments[:, g, :], stats[:, g, :, :].rearrange("p a b -> p (a b)"))
                    last.then_inc(norm_step, 1)
                    dve.wait_ge(norm_step, pair * 8 + 2)
                    nc.vector.tensor_tensor(g_mom[:, :, 0], moments[:, :, 0], moments[:, :, 0], ALU.mult).then_inc(norm_step, 1)
                    dve.wait_ge(norm_step, pair * 8 + 3)
                    nc.vector.tensor_tensor(moments[:, :, 1], moments[:, :, 1], g_mom[:, :, 0], ALU.add).then_inc(norm_step, 1)

                def norm_finish(pair):
                    dve.wait_ge(averaged, pair + 1)
                    nc.vector.tensor_copy(g_mom[:].rearrange("p a b -> p (a b)"), out_ps[:, 1, 0:8]).then_inc(norm_step, 1)
                    dve.wait_ge(norm_step, pair * 8 + 5)
                    nc.vector.tensor_tensor(var_eps[:, :], g_mom[:, :, 0], g_mom[:, :, 0], ALU.mult).then_inc(norm_step, 1)
                    dve.wait_ge(norm_step, pair * 8 + 6)
                    nc.vector.scalar_tensor_tensor(var_eps[:, :], g_mom[:, :, 1], 1e-5, var_eps[:, :],
                                                   ALU.add, ALU.subtract).then_inc(norm_step, 1)
                    dve.wait_ge(rstd_made, pair + 1)
                    nc.vector.scalar_tensor_tensor(shift[:, :], g_mom[:, :, 0], -1.0, rstd[:, :],
                                                   ALU.mult, ALU.mult).then_inc(norm_step, 1)
                    dve.wait_ge(norm_step, pair * 8 + 8)

                def normalise(pair, half, cs):
                    for g in range(2):
                        gg = 2 * half + g
                        last = nc.vector.tensor_scalar(
                            xn[:, half, GROUP_CH * g:GROUP_CH * (g + 1), :].rearrange("p c x -> p (c x)"),
                            x[:, cs(GROUP_CH * gg, GROUP_CH), :].rearrange("p c x -> p (c x)"),
                            rstd[:, gg:gg + 1], shift[:, gg:gg + 1], ALU.mult, ALU.add)
                    last.then_inc(xn_made, 1)

                def strips(k, q):
                    slot = (QUADS * k.s + q) % 2
                    dve.wait_ge(transposed, k.count(QUADS, q + 1))
                    if not (isinstance(k.it, int) and k.it == 0 and QUADS * k.s + q < 2):
                        dve.wait_ge(conv_done, k.count(QUADS, q - 1))
                    t = tr_ps[:, slot, :].rearrange("p (c m) -> p c m", c=QUAD)
                    nc.vector.tensor_copy(strips_t[slot][0:64, :, 2 * IMAGES:2 * IMAGES + 128], t[64:128, :, :])
                    nc.vector.tensor_copy(strips_t[slot][64:128, :, IMAGES:IMAGES + 128], t[0:64, :, :]).then_inc(strips_made, 1)

                def add(k, q):
                    slot = (QUADS * k.s + q) % 2
                    dve.wait_ge(conv_done, k.count(QUADS, q + 1))
                    if q == 0:
                        dve.wait_ge(shifted, k.count(1, 1))
                    view = x[:, channels(k, QUAD * q, QUAD), :].rearrange("p c (y x) -> p c y x", y=STRIP)
                    nc.vector.tensor_tensor(view, out_ps[:, slot, :].rearrange("p (c x y) -> p c y x", c=QUAD, y=STRIP),
                                            view, ALU.add).then_inc(added, 1)

                def in_pair(k, pairs_on):
                    c0 = k.it * (2 * STEP) + 2 * STEP * pairs_on
                    return lambda a, n: slice(c0 + a, c0 + a + n) if isinstance(c0, int) else bass.ds(c0 + a, n)

                def step(k):
                    nxt = in_pair(k, 1)
                    for q in range(QUADS):
                        if q + 1 < QUADS or has_next(k):
                            strips(k, q + 1)
                        if not (k.first and q == 0):
                            add(k, q - 1)
                        if not has_next_pair(k):
                            continue
                        if k.s == 0 and q == 0:
                            norm_stats(k.it + 1, nxt)
                        if k.s == 0 and q == 1:
                            norm_finish(k.it + 1)
                        if k.s == 1 and q == 0:
                            normalise(k.it + 1, 0, nxt)
                        if k.s == 1 and q == 2:
                            normalise(k.it + 1, 1, nxt)

                def prepare():
                    kinds = scales.rearrange("p (k b c) -> p k b c", k=4, b=3)
                    g, m, b, factor = (kinds[:, i] for i in range(4))
                    nc.vector.memset(minus_half[:, :], -0.5)
                    nc.vector.memset(w_hi_mid[:, :, :], 0.0)
                    nc.vector.memset(w_low[:, :, :], 0.0)
                    for t in strips_t:
                        nc.vector.memset(t[:, :, :], 0.0)
                    dve.wait_ge(variances_loaded, 16)
                    nc.vector.tensor_scalar(variances[:, :], variances[:, :], 1e-5, None, ALU.add).then_inc(power_made, 1)
                    dve.wait_ge(consts_loaded, 16 * N_CONSTS)
                    for xo in range(32):
                        nc.vector.tensor_copy(select[:, xo, :].rearrange("p (r x) -> p r x", r=4),
                                              toeplitz_rule.rearrange("p (r u) -> p r u", r=4)[:, :, 31 - xo:63 - xo])
                    dve.wait_ge(factors_loaded, 16)
                    nc.vector.tensor_tensor(g, g, factor, ALU.mult).then_inc(weights_step, 1)
                    dve.wait_ge(weights_step, 1)
                    scale = lambda branch, js: g[0:TAP_ROWS, branch, None, :].to_broadcast([TAP_ROWS, js, 192])
                    by_j = lambda t, js: t.rearrange("p (j c) -> p j c", j=js)
                    nc.vector.tensor_tensor(m, m, g, ALU.mult)
                    nc.vector.tensor_tensor(by_j(w_small, 6), by_j(w_small, 6), scale(1, 6), ALU.mult)
                    nc.vector.tensor_tensor(by_j(centre, 6), by_j(centre, 6), scale(2, 6), ALU.mult)
                    nc.vector.tensor_tensor(by_j(w_large, J), by_j(w_large, J), scale(0, J), ALU.mult).then_inc(weights_step, 1)
                    dve.wait_ge(weights_step, 2)
                    nc.vector.tensor_tensor(b, b, m, ALU.subtract)
                    nc.vector.tensor_tensor(w_small, w_small, centre, ALU.add).then_inc(weights_step, 1)
                    dve.wait_ge(weights_step, 3)
                    nc.vector.tensor_tensor(shift_all[:, :], b[:, 0, :], b[:, 1, :], ALU.add)
                    some = w_large[:, 5 * 192:11 * 192]
                    nc.vector.tensor_tensor(some, some, w_small, ALU.add).then_inc(weights_step, 1)
                    dve.wait_ge(weights_step, 4)
                    nc.vector.tensor_tensor(shift_all[:, :], shift_all[:, :], b[:, 2, :], ALU.add)
                    full = w_large.rearrange("p (j c) -> p c j", j=J)
                    rest = high_f32.rearrange("p (c j) -> p c j", j=J)
                    nc.vector.tensor_copy(w_hi_mid[0:TAP_ROWS], full).then_inc(weights_step, 1)
                    dve.wait_ge(weights_step, 5)
                    nc.vector.tensor_tensor(rest, full, w_hi_mid[0:TAP_ROWS], ALU.subtract).then_inc(weights_step, 1)
                    dve.wait_ge(weights_step, 6)
                    nc.vector.tensor_copy(w_hi_mid[64:64 + TAP_ROWS], rest)
                    nc.vector.tensor_copy(w_low[0:TAP_ROWS], rest).then_inc(weights_step, 1)
                    dve.wait_ge(weights_step, 7)
                    nc.vector.tensor_tensor(w_low[0:TAP_ROWS], rest, w_low[0:TAP_ROWS], ALU.subtract).then_inc(weights_step, 1)
                    dve.wait_ge(weights_step, 8)
                    dve.sem_inc(weights_made, 1)

                prepare()
                cs0 = lambda a, n: slice(a, a + n)
                norm_stats(0, cs0)
                norm_finish(0)
                normalise(0, 0, cs0)
                normalise(0, 1, cs0)
                strips(Step(0, 0), 0)
                schedule(dve, step)
                add(Step(PAIRS_OF_STEPS - 1, 1), 2)

            @block.gpsimd
            def _(pool):
                def power(pair):
                    pool.wait_ge(norm_step, pair * 8 + 7)
                    nc.gpsimd.tensor_tensor(rstd[:, :], var_eps[:, :], minus_half[:, 0:4], ALU.pow).then_inc(rstd_made, 1)

                def add_shift(k):
                    pool.wait_ge(xn_made, k.count(1, 1))
                    cs = channels(k, 0, STEP)
                    view = x[:, cs, :]
                    nc.gpsimd.tensor_tensor(view, view, shift_all[:, cs, None].to_broadcast([128, STEP, PIX]),
                                            ALU.add).then_inc(shifted, 1)

                def step(k):
                    add_shift(k)
                    if k.s == 0 and has_next_pair(k):
                        power(k.it + 1)

                pool.wait_ge(power_made, 1)
                nc.gpsimd.tensor_tensor(variances[:, :], variances[:, :], minus_half[0:96, :], ALU.pow).then_inc(power_made, 1)
                power(0)
                schedule(pool, step)


CHUNK = 96
BLOCK = 32
STATES = 16
TILE_STATES = 128 // BLOCK
PAIRS = 12
RING = 8
FILLS = 29
NORM, DELTA_P, X_P, B_REP = 0, 1, 5, 9


class Batch:

    def __init__(self, it, s):
        self.it, self.s = it, s
        self.first = isinstance(it, int) and it == 0 and s == 0

    def count(self, per_batch, more):
        return self.it * (2 * per_batch) + (self.s * per_batch + more)


class Fill:

    def __init__(self, n, offset):
        self.bank = (FILLS * n.s + offset) % 2
        self.number = n.it * (2 * FILLS) + (FILLS * n.s + offset)
        self.before = n.it * FILLS + (FILLS * n.s + offset) // 2
        self.static_first = isinstance(self.before, int) and self.before == 0


def ssm_layer(nc, tag, x_src, x_dst, w, consts, batches):
    L = 1024
    HALF = 512
    ctx = ExitStack()
    with ctx:
        sb = lambda name, shape, dt=F32: ctx.enter_context(nc.sbuf_tensor(f"{tag}_{name}", shape, dt))
        ps = lambda name, shape: ctx.enter_context(nc.psum_tensor(f"{tag}_{name}", shape, F32))
        sem = lambda name: ctx.enter_context(nc.semaphore(f"{tag}_{name}"))

        x = sb("x", [CHUNK, 2, L])
        x_res = sb("x_res", [CHUNK, 2, L])
        xn = sb("xn", [CHUNK, 2, L])
        x_in = [sb(f"x_in{i}", [CHUNK, 2, L]) for i in range(2)]
        relu_t = sb("relu_t", [128, 2, L])
        log_t = sb("log_t", [CHUNK, 2, L])
        delta = sb("delta", [CHUNK, 2, L])
        dx = sb("dx", [CHUNK, 2, L])
        b_rep = sb("b_rep", [128, 4, L])
        c_rep = sb("c_rep", [128, 4, L])
        decay = sb("decay", [128, 2, 2 * L])
        h = sb("h", [128, RING, 2 * L])
        y_sb = sb("y_sb", [CHUNK, 2, L])
        bc_parts = sb("bc_parts", [128, L], BF16)
        mid_t = sb("mid_t", [128, L], BF16)
        w_proj = sb("w_proj", [CHUNK, 2, 416])
        w_out = sb("w_out", [CHUNK, 2, 192])
        a_neg = sb("a_neg", [128, 24])
        vecs = sb("vecs", [CHUNK, 10])
        bc_bias = sb("bc_bias", [128, 1])
        rep_sel = sb("rep_sel", [CHUNK, 3, 128])
        state_sum = sb("state_sum", [128, BLOCK])
        group_avg = sb("group_avg", [CHUNK, CHUNK])
        bc_sel = sb("bc_sel", [128, 8, 128], BF16)
        stats = sb("stats", [CHUNK, 4, 6])
        moments = sb("moments", [CHUNK, 2, 2])
        g_mom = sb("g_mom", [CHUNK, 2, 2])
        var_eps = sb("var_eps", [CHUNK, 2])
        rstd = sb("rstd", [CHUNK, 2])
        shift = sb("shift", [CHUNK, 2])
        minus_half = sb("minus_half", [CHUNK, 2])

        delta_rep = ps("delta_rep", [128, L])
        dx_rep = ps("dx_rep", [128, L])
        y_ps = ps("y_ps", [128, L])
        scratch = ps("scratch", [128, 2, HALF])

        consts_loaded = sem("consts_loaded")
        consts_made = sem("consts_made")
        x_loaded = sem("x_loaded")
        res_loaded = sem("res_loaded")
        out_stored = sem("out_stored")
        filled = sem("filled")
        out_added = sem("out_added")
        stats_seen = sem("stats_seen")
        drained = [sem(f"drained{i}") for i in range(2)]
        norm_step = sem("norm_step")
        rstd_made = sem("rstd_made")
        xn_made = sem("xn_made")
        soft_step = sem("soft_step")
        bc_high = sem("bc_high")
        bc_step = sem("bc_step")
        bc_mid = sem("bc_mid")
        delta_made = [sem(f"delta_made{c}") for c in range(2)]
        dx_made = [sem(f"dx_made{c}") for c in range(2)]
        delta_replicated = sem("delta_replicated")
        dx_replicated = sem("dx_replicated")
        decay_made = sem("decay_made")
        u_made = sem("u_made")
        scanned = sem("scanned")
        c_applied = sem("c_applied")
        y_summed = sem("y_summed")
        y_kept = sem("y_kept")

        bx, bdl, dtb, d_skip, b_out = (vecs[:, 2 * i:2 * i + 2] for i in range(5))

        def prologue_fill(m_of, j):
            if m_of is None:
                return Fill(Batch(0, 0), j)
            return Fill(m_of, (21 if m_of.first else 17) if j == NORM else 25 + j)

        def c_fill(n, i):
            no_norm = isinstance(n.it, int) and 2 * n.it + n.s == batches - 1
            return Fill(n, (17 if n.first else 13) + i + (1 if i >= 4 and not no_norm else 0))

        def tail_fill(n_next, i):
            number = 2 * n_next.it + n_next.s if isinstance(n_next.it, int) else None
            if number == batches:
                return Fill(n_next, -4 + i)
            return Fill(n_next, (21 if number == batches - 1 else 22) + i)

        def await_bank(pe, f):
            if not f.static_first:
                pe.wait_ge(drained[f.bank], f.before)

        def await_fill(eng, f):
            eng.wait_ge(filled, f.number + 1)

        def await_drained(eng, f):
            eng.wait_ge(drained[f.bank], f.before + 1)

        def following(n):
            return Batch(0, 0) if n is None else (Batch(n.it, 1) if n.s == 0 else Batch(n.it + 1, 0))

        def schedule(eng, prologue, main, tail):
            prologue(None)
            main(Batch(0, 0), False)
            main(Batch(0, 1), False)
            last = batches // 2 - 1
            if last > 1:
                with eng.Fori(1, last) as it:
                    main(Batch(it, 0), False)
                    main(Batch(it, 1), False)
            main(Batch(last, 0), False)
            main(Batch(last, 1), True)
            tail(Batch(last + 1, 0))

        src = x_src.rearrange("b (c p) h w -> b p c (h w)", p=CHUNK)
        dst = x_dst.rearrange("b (c p) h w -> b p c (h w)", p=CHUNK)
        N_CONSTS = 9

        with nc.Block() as block:
            @block.sync
            def _(sp):
                sp.dma_start(x[:, :, :], src[0]).then_inc(x_loaded, 16)
                for t, a in ((group_avg, consts["group_avg"]), (w_proj, w["w_proj"]), (vecs, w["vecs"]), (a_neg, w["a_log"]),
                             (rep_sel, consts["rep_sel"]), (w_out, w["w_out"]), (state_sum, consts["state_sum"])):
                    sp.dma_start(t[:], a).then_inc(consts_loaded, 16)
                sp.dma_start(bc_bias[96:128, :], w["bc_bias"]).then_inc(consts_loaded, 16)
                sp.dma_start(h[:, 0, 0:1024].rearrange("p (t m) -> p t m", t=8), consts["bc_sel"]).then_inc(consts_loaded, 16)

                def load(n):
                    sp.dma_start(x[:, :, :], src[n.count(1, 0)]).then_inc(x_loaded, 16)

                def load_residual(n):
                    sp.dma_start(x_res[:, :, :], src[n.count(1, 0)]).then_inc(res_loaded, 16)

                def store(n_next):
                    sp.wait_ge(out_added, n_next.count(1, 0))
                    sp.dma_start(dst[n_next.count(1, -1)], x_res[:, :, :]).then_inc(out_stored, 16)
                    sp.wait_ge(out_stored, n_next.count(16, 0))

                def main(n, last):
                    if not n.first:
                        store(n)
                        load_residual(n)
                    if not (isinstance(n.it, int) and n.it == batches // 2 - 1):
                        sp.wait_ge(xn_made, n.count(1, 2))
                        load(Batch(n.it + 1, n.s))

                load_residual(Batch(0, 0))
                sp.wait_ge(xn_made, 1)
                load(Batch(0, 1))
                schedule(sp, lambda n: None, main, store)

            @block.tensor
            def _(pe):
                def replicate_dx(n, d):
                    if d % 3 == 0:
                        pe.wait_ge(dx_made[d // 3], n.count(1, 1))
                    if not (n.first and d == 0):
                        pe.wait_ge(u_made, n.count(PAIRS, 2 * d))
                    for half in range(2):
                        t = slice(half * HALF, (half + 1) * HALF)
                        last = nc.tensor.matmul(dx_rep[:, t], rep_sel[:, d % 3, :], dx[:, d // 3, t],
                                                start=True, stop=True)
                    last.then_inc(dx_replicated, 1)

                def replicate_delta(n, d):
                    if d % 3 == 0:
                        pe.wait_ge(delta_made[d // 3], n.count(1, 1))
                    if not (n.first and d == 0):
                        pe.wait_ge(decay_made, n.count(PAIRS, 2 * d))
                    for half in range(2):
                        t = slice(half * HALF, (half + 1) * HALF)
                        last = nc.tensor.matmul(delta_rep[:, t], rep_sel[:, d % 3, :], delta[:, d // 3, t],
                                                start=True, stop=True)
                    last.then_inc(delta_replicated, 1)

                def sum_states(n, g, np_):
                    if np_ == 0 and not (n.first and g == 0):
                        pe.wait_ge(y_kept, n.count(2, g))
                    pe.wait_ge(c_applied, n.count(PAIRS, 6 * g + 5 + np_))
                    for sub in range(2):
                        for half in range(2):
                            for dd in range(3):
                                p = 6 * g + 2 * dd + np_
                                slot = (PAIRS * n.s + p) % RING
                                at = sub * L + half * HALF
                                last = nc.tensor.matmul(
                                    y_ps[BLOCK * dd:BLOCK * (dd + 1), half * HALF:(half + 1) * HALF],
                                    state_sum[:, :], h[:, slot, at:at + HALF],
                                    start=(np_ == 0 and sub == 0), stop=(np_ == 1 and sub == 1))
                    last.then_inc(y_summed, 1)

                def project_out(n_next, i):
                    if i == 0:
                        pe.wait_ge(y_kept, n_next.count(2, 0))
                    co, half = divmod(i, 2)
                    f = tail_fill(n_next, i)
                    await_bank(pe, f)
                    for ci in range(2):
                        last = nc.tensor.matmul(scratch[0:CHUNK, f.bank, :],
                                                w_out[:, ci, co * CHUNK:(co + 1) * CHUNK],
                                                y_sb[:, ci, half * HALF:(half + 1) * HALF],
                                                start=(ci == 0), stop=(ci == 1))
                    last.then_inc(filled, 1)

                def norm(m_of):
                    f = prologue_fill(m_of, NORM)
                    await_bank(pe, f)
                    pe.wait_ge(norm_step, following(m_of).count(7, 3))
                    nc.tensor.matmul(scratch[0:CHUNK, f.bank, 0:4], group_avg[:, :],
                                     moments[:, :, :].rearrange("p a b -> p (a b)"), start=True,
                                     stop=True).then_inc(filled, 1)

                def project(m_of, f, half, m0, m1):
                    pe.wait_ge(xn_made, following(m_of).count(1, 1))
                    await_bank(pe, f)
                    for ci in range(2):
                        last = nc.tensor.matmul(scratch[0:m1 - m0, f.bank, :], w_proj[:, ci, m0:m1],
                                                xn[:, ci, half * HALF:(half + 1) * HALF],
                                                start=(ci == 0), stop=(ci == 1))
                    last.then_inc(filled, 1)

                def project_delta(m_of, i):
                    c, half = divmod(i, 2)
                    project(m_of, prologue_fill(m_of, DELTA_P + i), half, 224 + CHUNK * c, 320 + CHUNK * c)

                def project_x(m_of, i):
                    c, half = divmod(i, 2)
                    project(m_of, prologue_fill(m_of, X_P + i), half, *((0, 128), (128, 224))[c])

                def replicate_bc(f, tile, half):
                    await_bank(pe, f)
                    nc.tensor.matmul(scratch[:, f.bank, :], bc_sel[:, tile, :],
                                     bc_parts[:, half * HALF:(half + 1) * HALF],
                                     start=True, stop=True).then_inc(filled, 1)

                def b_tile(m_of, i):
                    m = following(m_of)
                    if i == 0:
                        pe.wait_ge(bc_mid, m.count(1, 1))
                        pe.wait_ge(bc_step, m.count(3, 3))
                    replicate_bc(prologue_fill(m_of, B_REP + i), i // 2, i % 2)

                def c_tile(n, i):
                    replicate_bc(c_fill(n, i), 4 + i // 2, i % 2)

                def prologue(m_of):
                    norm(m_of)
                    for i in range(4):
                        project_delta(m_of, i)
                    for i in range(4):
                        project_x(m_of, i)
                    for i in range(8):
                        b_tile(m_of, i)
                    replicate_dx(following(m_of), 0)
                    replicate_delta(following(m_of), 0)

                def main(n, last):
                    c_tile(n, 0)
                    if not n.first:
                        sum_states(before(n), 1, 0)
                    c_tile(n, 1)
                    c_tile(n, 2)
                    replicate_delta(n, 1)
                    c_tile(n, 3)
                    if not last:
                        norm(n)
                    replicate_dx(n, 1)
                    c_tile(n, 4)
                    if not n.first:
                        sum_states(before(n), 1, 1)
                    c_tile(n, 5)
                    c_tile(n, 6)
                    replicate_delta(n, 2)
                    c_tile(n, 7)
                    replicate_dx(n, 2)
                    if not n.first:
                        project_out(n, 0)
                        project_out(n, 1)
                        project_out(n, 2)
                        project_out(n, 3)
                    if not last:
                        project_delta(n, 0)
                        project_delta(n, 1)
                    replicate_delta(n, 3)
                    replicate_dx(n, 3)
                    if not last:
                        project_delta(n, 2)
                        project_delta(n, 3)
                    sum_states(n, 0, 0)
                    replicate_dx(n, 4)
                    replicate_delta(n, 4)
                    sum_states(n, 0, 1)
                    if not last:
                        project_x(n, 0)
                        project_x(n, 1)
                        project_x(n, 2)
                    replicate_delta(n, 5)
                    replicate_dx(n, 5)
                    if not last:
                        project_x(n, 3)
                        b_tile(n, 0)
                        b_tile(n, 1)
                        b_tile(n, 2)
                        b_tile(n, 3)
                        b_tile(n, 4)
                        b_tile(n, 5)
                        b_tile(n, 6)
                        replicate_delta(following(n), 0)
                        b_tile(n, 7)
                        replicate_dx(following(n), 0)

                def before(n):
                    return Batch(n.it, 0) if n.s else Batch(n.it - 1, 1)

                def tail(n):
                    sum_states(before(n), 1, 0)
                    sum_states(before(n), 1, 1)
                    for i in range(4):
                        project_out(n, i)

                pe.wait_ge(consts_loaded, 16 * N_CONSTS)
                pe.wait_ge(consts_made, 5)
                schedule(pe, prologue, main, tail)

            @block.scalar
            def _(act):
                def exp_pair(n, p):
                    d, np_ = divmod(p, 2)
                    if np_ == 0:
                        act.wait_ge(delta_replicated, n.count(6, d + 1))
                    if not (n.first and p < 2):
                        act.wait_ge(scanned, n.count(PAIRS, p - 1))
                    for sub in range(2):
                        col = 4 * d + 2 * np_ + sub
                        last = nc.scalar.activation(decay[:, p % 2, sub * L + 1:(sub + 1) * L], delta_rep[:, 1:L],
                                                    ACT.Exp, scale=a_neg[:, col:col + 1])
                    last.then_inc(decay_made, 1)

                def drain_rep(f, out):
                    await_fill(act, f)
                    nc.scalar.activation(out, scratch[:, f.bank, :], ACT.Copy).then_inc(drained[f.bank], 1)

                def take_c(n, i):
                    if not n.first and i % 4 == 0:
                        act.wait_ge(c_applied, n.count(PAIRS, i // 4 - 1))
                    drain_rep(c_fill(n, i), c_rep[:, i // 2, (i % 2) * HALF:(i % 2 + 1) * HALF])

                def take_b(m_of, i):
                    if m_of is not None and i % 4 == 0:
                        act.wait_ge(u_made, m_of.count(PAIRS, 11 + i // 4))
                    drain_rep(prologue_fill(m_of, B_REP + i), b_rep[:, i // 2, (i % 2) * HALF:(i % 2 + 1) * HALF])

                def normalise(m_of):
                    m = following(m_of)
                    act.wait_ge(norm_step, m.count(7, 7))
                    for c in range(2):
                        last = nc.scalar.activation(xn[:, c, :], x[:, c, :], ACT.Identity,
                                                    scale=rstd[:, c:c + 1], bias=shift[:, c:c + 1])
                    last.then_inc(xn_made, 1)

                def take_delta(m_of, i):
                    m = following(m_of)
                    if m_of is not None and i == 0:
                        for c in range(2):
                            act.wait_ge(delta_made[c], m.count(1, 0))
                        if not m_of.first:
                            act.wait_ge(out_added, m_of.count(1, 0))
                    c, half = divmod(i, 2)
                    t = slice(half * HALF, (half + 1) * HALF)
                    f = prologue_fill(m_of, DELTA_P + i)
                    await_fill(act, f)
                    nc.scalar.activation(log_t[:, c, t], scratch[0:CHUNK, f.bank, :], ACT.Abs, bias=bdl[:, c:c + 1])
                    nc.scalar.activation(relu_t[0:CHUNK, c, t], scratch[0:CHUNK, f.bank, :], ACT.Relu,
                                         bias=bdl[:, c:c + 1]).then_inc(drained[f.bank], 1)

                def small_exp(m_of):
                    for i in (2, 3):
                        await_drained(act, prologue_fill(m_of, DELTA_P + i))
                    nc.scalar.activation(log_t[:, :, :], log_t[:, :, :], ACT.Exp, scale=-1.0).then_inc(soft_step, 1)

                def small_log(m_of):
                    m = following(m_of)
                    act.wait_ge(soft_step, m.count(2, 1))
                    nc.scalar.activation(log_t[:, :, :], log_t[:, :, :], ACT.Ln, bias=1.0).then_inc(soft_step, 1)

                def take_x(m_of, i):
                    m = following(m_of)
                    if m_of is not None and i == 0:
                        act.wait_ge(bc_step, m.count(3, 0))
                        if not m_of.first:
                            act.wait_ge(y_kept, m_of.count(2, 0))
                    c, half = divmod(i, 2)
                    t = slice(half * HALF, (half + 1) * HALF)
                    f = prologue_fill(m_of, X_P + i)
                    await_fill(act, f)
                    if c == 0:
                        nc.scalar.activation(relu_t[CHUNK:128, 0, t], scratch[CHUNK:128, f.bank, :], ACT.Identity,
                                             bias=bc_bias[CHUNK:128, :])
                    nc.scalar.activation(x_in[m.s][:, c, t], scratch[0:CHUNK, f.bank, :], ACT.Identity,
                                         bias=bx[:, c:c + 1]).then_inc(drained[f.bank], 1)

                def high_part(m_of):
                    for i in (0, 1):
                        await_drained(act, prologue_fill(m_of, X_P + i))
                    nc.scalar.activation(bc_parts[CHUNK:128, :], relu_t[CHUNK:128, 0, :], ACT.Copy).then_inc(bc_high, 1)

                def middle_part(m_of):
                    m = following(m_of)
                    act.wait_ge(bc_step, m.count(3, 1))
                    nc.scalar.activation(bc_parts[0:32, :], relu_t[CHUNK:128, 1, :], ACT.Copy).then_inc(bc_mid, 1)

                def take_output(n_next, i):
                    if i == 0:
                        last_batch = isinstance(n_next.it, int) and 2 * n_next.it + n_next.s == batches
                        for c in range(2):
                            act.wait_ge(delta_made[c], n_next.count(1, 0 if last_batch else 1))
                    co, half = divmod(i, 2)
                    f = tail_fill(n_next, i)
                    await_fill(act, f)
                    nc.scalar.activation(log_t[:, co, half * HALF:(half + 1) * HALF], scratch[0:CHUNK, f.bank, :],
                                         ACT.Identity, bias=b_out[:, co:co + 1]).then_inc(drained[f.bank], 1)

                def prologue(m_of):
                    normalise(m_of)
                    for i in range(4):
                        take_delta(m_of, i)
                    small_exp(m_of)
                    for i in range(2):
                        take_x(m_of, i)
                    high_part(m_of)
                    small_log(m_of)
                    for i in range(2, 4):
                        take_x(m_of, i)
                    middle_part(m_of)
                    for i in range(8):
                        take_b(m_of, i)

                def tail(n_next):
                    for i in range(4):
                        take_output(n_next, i)

                def main(n, last):
                    exp_pair(n, 0)
                    take_c(n, 0)
                    exp_pair(n, 1)
                    take_c(n, 1)
                    take_c(n, 2)
                    take_c(n, 3)
                    exp_pair(n, 2)
                    take_c(n, 4)
                    exp_pair(n, 3)
                    take_c(n, 5)
                    take_c(n, 6)
                    take_c(n, 7)
                    if not last:
                        normalise(n)
                    if not n.first:
                        take_output(n, 0)
                        take_output(n, 1)
                    exp_pair(n, 4)
                    if not n.first:
                        take_output(n, 2)
                        take_output(n, 3)
                    exp_pair(n, 5)
                    if not last:
                        take_delta(n, 0)
                        take_delta(n, 1)
                    exp_pair(n, 6)
                    exp_pair(n, 7)
                    if not last:
                        take_delta(n, 2)
                        take_delta(n, 3)
                        small_exp(n)
                        small_log(n)
                    exp_pair(n, 8)
                    exp_pair(n, 9)
                    if not last:
                        take_x(n, 0)
                        take_x(n, 1)
                        high_part(n)
                        take_x(n, 2)
                    exp_pair(n, 10)
                    if not last:
                        middle_part(n)
                    exp_pair(n, 11)
                    if not last:
                        take_x(n, 3)
                        take_b(n, 0)
                        take_b(n, 1)
                        take_b(n, 2)
                        take_b(n, 3)
                        take_b(n, 4)
                        take_b(n, 5)
                        take_b(n, 6)
                        take_b(n, 7)

                act.wait_ge(consts_loaded, 16 * N_CONSTS)
                nc.scalar.activation(a_neg[:, :], a_neg[:, :], ACT.Exp).then_inc(consts_made, 1)
                act.wait_ge(consts_made, 5)
                schedule(act, prologue, main, tail)

            @block.vector
            def _(dve):
                def make_u(n, p):
                    d, np_ = divmod(p, 2)
                    if np_ == 0:
                        dve.wait_ge(dx_replicated, n.count(6, d + 1))
                    if p < 2:
                        m_of = None if n.first else before(n)
                        for i in (2, 3):
                            await_drained(dve, prologue_fill(m_of, B_REP + 4 * np_ + i))
                    if p >= RING:
                        dve.wait_ge(y_summed, n.count(4, np_ + 1))
                    elif not n.first:
                        dve.wait_ge(y_summed, n.count(4, -4 + 2 * ((p + 4) // 6) + np_ + 1))
                    slot = (PAIRS * n.s + p) % RING
                    nc.vector.tensor_tensor(h[:, slot, :].rearrange("p (s t) -> p s t", s=2),
                                            dx_rep[:, None, :].to_broadcast([128, 2, L]),
                                            b_rep[:, 2 * np_:2 * np_ + 2, :], ALU.mult).then_inc(u_made, 1)

                def before(n):
                    return Batch(n.it, 0) if n.s else Batch(n.it - 1, 1)

                def scan(n, p):
                    dve.wait_ge(decay_made, n.count(PAIRS, p + 1))
                    dve.wait_ge(u_made, n.count(PAIRS, p + 1))
                    slot = (PAIRS * n.s + p) % RING
                    nc.vector.tensor_tensor_scan(h[:, slot, :], decay[:, p % 2, :], h[:, slot, :], 0.0,
                                                 ALU.mult, ALU.add).then_inc(scanned, 1)

                def keep_y(n, g):
                    dve.wait_ge(y_summed, n.count(4, 2 * g + 2))
                    if g == 0 and not n.first:
                        await_fill(dve, tail_fill(n, 3))
                    nc.vector.scalar_tensor_tensor(y_sb[:, g, :], x_in[n.s][:, g, :], d_skip[:, g:g + 1],
                                                   y_ps[0:CHUNK, :], ALU.mult, ALU.add).then_inc(y_kept, 1)

                def add_output(n_next):
                    dve.wait_ge(res_loaded, n_next.count(16, 0))
                    for i in (2, 3):
                        await_drained(dve, tail_fill(n_next, i))
                    nc.vector.tensor_tensor(x_res[:, :, :], x_res[:, :, :], log_t[:, :, :], ALU.add).then_inc(out_added, 1)

                def norm_stats(m_of):
                    m = following(m_of)
                    k = m.count(7, 0)
                    dve.wait_ge(x_loaded, m.count(16, 16))
                    for i in range(4):
                        c, half = divmod(i, 2)
                        last = nc.vector.bn_stats(stats[:, i, :], x[:, c, half * HALF:(half + 1) * HALF])
                    last.then_inc(norm_step, 1)
                    dve.wait_ge(norm_step, k + 1)
                    if m_of is not None:
                        await_fill(dve, prologue_fill_before(m_of))
                    dve.sem_inc(stats_seen, 1)
                    for c in range(2):
                        last = nc.vector.bn_aggr(moments[:, c, :], stats[:, 2 * c:2 * c + 2, :].rearrange("p a b -> p (a b)"))
                    last.then_inc(norm_step, 1)
                    dve.wait_ge(norm_step, k + 2)
                    for c in range(2):
                        last = nc.vector.scalar_tensor_tensor(moments[:, c, 1:2], moments[:, c, 0:1],
                                                              moments[:, c, 0:1], moments[:, c, 1:2], ALU.mult, ALU.add)
                    last.then_inc(norm_step, 1)

                def prologue_fill_before(m_of):
                    return prologue_fill(None if m_of.first else before(m_of), NORM)

                def norm_finish(m_of):
                    m = following(m_of)
                    k = m.count(7, 0)
                    f = prologue_fill(m_of, NORM)
                    await_fill(dve, f)
                    nc.vector.tensor_copy(g_mom[:, :, :].rearrange("p a b -> p (a b)"),
                                          scratch[0:CHUNK, f.bank, 0:4]).then_inc(drained[f.bank], 1)
                    await_drained(dve, f)
                    for c in range(2):
                        last = nc.vector.scalar_tensor_tensor(var_eps[:, c:c + 1], g_mom[:, c, 0:1], g_mom[:, c, 0:1],
                                                              g_mom[:, c, 1:2], ALU.mult, ALU.subtract)
                    last.then_inc(norm_step, 1)
                    dve.wait_ge(norm_step, k + 4)
                    nc.vector.tensor_scalar(var_eps[:, :], var_eps[:, :], -1.0, 1e-5, ALU.mult, ALU.add).then_inc(norm_step, 1)

                def norm_shift(m_of):
                    m = following(m_of)
                    k = m.count(7, 0)
                    dve.wait_ge(rstd_made, m.count(1, 1))
                    nc.vector.scalar_tensor_tensor(shift[:, :], g_mom[:, :, 0], -1.0, rstd[:, :],
                                                   ALU.mult, ALU.mult).then_inc(norm_step, 2)

                q = slice(CHUNK, 128)

                def bc_remainder(m_of):
                    m = following(m_of)
                    dve.wait_ge(bc_high, m.count(1, 1))
                    nc.vector.tensor_tensor(relu_t[q, 1, :], relu_t[q, 0, :], bc_parts[q, :], ALU.subtract).then_inc(bc_step, 1)

                def bc_low(m_of):
                    k = following(m_of).count(3, 0)
                    dve.wait_ge(bc_step, k + 1)
                    nc.vector.tensor_copy(mid_t[q, :], relu_t[q, 1, :]).then_inc(bc_step, 1)
                    dve.wait_ge(bc_step, k + 2)
                    nc.vector.tensor_tensor(bc_parts[32:64, :], relu_t[q, 1, :], mid_t[q, :], ALU.subtract).then_inc(bc_step, 1)

                def finish_delta(m_of, c):
                    m = following(m_of)
                    dve.wait_ge(soft_step, m.count(2, 2))
                    if m_of is not None:
                        dve.wait_ge(delta_replicated, m_of.count(6, 3 + 3 * c))
                    nc.vector.tensor_tensor(delta[:, c, :], relu_t[0:CHUNK, c, :], log_t[:, c, :], ALU.add).then_inc(delta_made[c], 1)

                def finish_dx(m_of, c):
                    m = following(m_of)
                    dve.wait_ge(delta_made[c], m.count(1, 1))
                    if m_of is not None:
                        dve.wait_ge(dx_replicated, m_of.count(6, 3 + 3 * c))
                    for i in (2 * c, 2 * c + 1):
                        await_drained(dve, prologue_fill(m_of, X_P + i))
                    nc.vector.tensor_tensor(dx[:, c, :], delta[:, c, :], x_in[m.s][:, c, :], ALU.mult).then_inc(dx_made[c], 1)

                def prepare_consts():
                    dve.wait_ge(consts_loaded, 16 * N_CONSTS)
                    nc.vector.tensor_tensor(bdl, bdl, dtb, ALU.add)
                    nc.vector.tensor_copy(bc_sel[:, :, :], h[:, 0, 0:1024].rearrange("p (t m) -> p t m", t=8)).then_inc(consts_made, 1)
                    dve.wait_ge(consts_made, 4)
                    nc.vector.tensor_scalar(a_neg[:, :], a_neg[:, :], -1.0, None, ALU.mult).then_inc(consts_made, 1)
                    dve.wait_ge(consts_made, 5)

                def prologue(m_of):
                    norm_stats(m_of)
                    prepare_consts()
                    norm_finish(m_of)
                    norm_shift(m_of)
                    bc_remainder(m_of)
                    bc_low(m_of)
                    finish_delta(m_of, 0)
                    finish_dx(m_of, 0)

                def main(n, last):
                    if not last:
                        norm_stats(n)
                    make_u(n, 0)
                    make_u(n, 1)
                    scan(n, 0)
                    if not last:
                        norm_finish(n)
                    scan(n, 1)
                    make_u(n, 2)
                    make_u(n, 3)
                    if not n.first:
                        keep_y(before(n), 1)
                    if not last:
                        norm_shift(n)
                    scan(n, 2)
                    scan(n, 3)
                    make_u(n, 4)
                    make_u(n, 5)
                    if not n.first:
                        add_output(n)
                    scan(n, 4)
                    scan(n, 5)
                    make_u(n, 6)
                    make_u(n, 7)
                    scan(n, 6)
                    scan(n, 7)
                    make_u(n, 8)
                    if not last:
                        finish_delta(n, 0)
                    scan(n, 8)
                    make_u(n, 9)
                    keep_y(n, 0)
                    scan(n, 9)
                    if not last:
                        bc_remainder(n)
                        bc_low(n)
                    make_u(n, 10)
                    make_u(n, 11)
                    if not last:
                        finish_dx(n, 0)
                    scan(n, 10)
                    scan(n, 11)

                def tail(n):
                    keep_y(before(n), 1)
                    add_output(n)

                nc.vector.memset(decay[:, :, 0:1], 0.0).then_inc(consts_made, 1)
                nc.vector.memset(decay[:, :, L:L + 1], 0.0)
                nc.vector.memset(minus_half[:, :], -0.5)
                nc.vector.memset(bc_parts[64:96, :], 0.0).then_inc(consts_made, 1)
                schedule(dve, prologue, main, tail)

            @block.gpsimd
            def _(pool):
                def before(n):
                    return Batch(n.it, 0) if n.s else Batch(n.it - 1, 1)

                def apply_c(n, p):
                    np_ = p % 2
                    if p < 2:
                        for i in (2, 3):
                            await_drained(pool, c_fill(n, 4 * np_ + i))
                    pool.wait_ge(scanned, n.count(PAIRS, p + 1))
                    slot = (PAIRS * n.s + p) % RING
                    view = h[:, slot, :].rearrange("p (s t) -> p s t", s=2)
                    nc.gpsimd.tensor_tensor(view, view, c_rep[:, 2 * np_:2 * np_ + 2, :], ALU.mult).then_inc(c_applied, 1)

                def finish_delta(m_of, c):
                    m = following(m_of)
                    pool.wait_ge(soft_step, m.count(2, 2))
                    if m_of is not None:
                        pool.wait_ge(delta_replicated, m_of.count(6, 3 + 3 * c))
                    nc.gpsimd.tensor_tensor(delta[:, c, :], relu_t[0:CHUNK, c, :], log_t[:, c, :], ALU.add).then_inc(delta_made[c], 1)

                def finish_dx(m_of, c):
                    m = following(m_of)
                    pool.wait_ge(delta_made[c], m.count(1, 1))
                    if m_of is not None:
                        pool.wait_ge(dx_replicated, m_of.count(6, 3 + 3 * c))
                    for i in (2 * c, 2 * c + 1):
                        await_drained(pool, prologue_fill(m_of, X_P + i))
                    nc.gpsimd.tensor_tensor(dx[:, c, :], delta[:, c, :], x_in[m.s][:, c, :], ALU.mult).then_inc(dx_made[c], 1)

                def power(m_of):
                    m = following(m_of)
                    pool.wait_ge(norm_step, m.count(7, 5))
                    nc.gpsimd.tensor_tensor(rstd[:, :], var_eps[:, :], minus_half[:, :], ALU.pow).then_inc(rstd_made, 1)

                def prologue(m_of):
                    power(m_of)
                    finish_delta(m_of, 1)
                    finish_dx(m_of, 1)

                def main(n, last):
                    if not last:
                        power(n)
                    apply_c(n, 0)
                    apply_c(n, 1)
                    apply_c(n, 2)
                    apply_c(n, 3)
                    apply_c(n, 4)
                    apply_c(n, 5)
                    apply_c(n, 6)
                    apply_c(n, 7)
                    apply_c(n, 8)
                    apply_c(n, 9)
                    if not last:
                        finish_delta(n, 1)
                        finish_dx(n, 1)
                    apply_c(n, 10)
                    apply_c(n, 11)

                pool.wait_ge(consts_made, 5)
                schedule(pool, prologue, main, lambda n: None)


HEADS, HEAD = 6, 32
WIN, PAD, SIDE = 7, 3, 32
TILE_H, TILE_W = 8, 16
TILES = [(ty, tx) for ty in (0, 3, 1, 2) for tx in (0, 1)]
GROUP = 3
UNIT_PAIRS = 12
MASK_ROWS = slice(64, 112)
A_FILLS = 59


DEN_AT = (3, 2, 1)


def quadrant(i):
    return slice(HEAD * i, HEAD * (i + 1))


def halo(tile):
    ty, tx = tile
    y = TILE_H * ty
    r0, r1 = max(0, y - PAD), min(SIDE, y + TILE_H + PAD)
    return r0, r1, (r1 - r0) * TILE_W, (r1 - r0) * (TILE_W + PAD), (slice(0, PAD) if tx == 0 else slice(TILE_W - PAD, TILE_W))


def tile_at(tile):
    ty, tx = tile
    first = 512 * tx + 128 * ty
    return slice(first, first + 128)


def attention(nc, tag, x_src, x_dst, w, consts, batches):
    L, HALF = 1024, 512
    ctx = ExitStack()
    with ctx:
        sb = lambda name, shape, dt=F32: ctx.enter_context(nc.sbuf_tensor(f"{tag}_{name}", shape, dt))
        ps = lambda name, shape: ctx.enter_context(nc.psum_tensor(f"{tag}_{name}", shape, F32))
        sem = lambda name: ctx.enter_context(nc.semaphore(f"{tag}_{name}"))

        x = sb("x", [CHUNK, 2, L])
        x_res = sb("x_res", [CHUNK, 2, L])
        xn = sb("xn", [CHUNK, 2, L])
        qk = sb("qk", [128, 3, L])
        qk1 = sb("qk1", [128, 3, L], BF16)
        qk2 = sb("qk2", [128, 3, L], BF16)
        qk3 = sb("qk3", [128, 3, L], BF16)
        q_a = [sb(f"q_a{i}", [128, HEADS, L], BF16) for i in range(2)]
        k_a = [sb(f"k_a{i}", [128, HEADS, L], BF16) for i in range(2)]
        q_b = [sb(f"q_b{i}", [128, HEADS, L], BF16) for i in range(2)]
        k_b = [sb(f"k_b{i}", [128, HEADS, L], BF16) for i in range(2)]
        v = [sb(f"v{i}", [128, 8, 192]) for i in range(2)]
        P_SLOTS = 3
        probs = sb("probs", [128, P_SLOTS, 2, 266])
        att = sb("att", [CHUNK, 2, L])
        den = sb("den", [CHUNK, L])
        pad_rows = sb("pad_rows", [18, L], BF16)
        w_qk = sb("w_qk", [CHUNK, 2, 384])
        w_v = sb("w_v", [CHUNK, 2, 192])
        w_o = sb("w_o", [CHUNK, 2, 192])
        b_v = sb("b_v", [128, 192])
        qk_scale = sb("qk_scale", [128, 3])
        qk_bias = sb("qk_bias", [128, 3])
        b_o = sb("b_o", [CHUNK, 2])
        group_avg = sb("group_avg", [CHUNK, CHUNK])
        ident = sb("ident", [128, 128])
        ones = sb("ones", [128, HEAD])
        den_sel = sb("den_sel", [18, 3, 128], BF16)
        floor = sb("floor", [128, HEADS, 2, 4])
        ln_pad = sb("ln_pad", [128, HEADS, 2, 4])
        m_raw = sb("m_raw", [128, 48])
        m_max = sb("m_max", [128, HEADS, 2, 4])
        m_hi = sb("m_hi", [128, HEADS, 2, 4], BF16)
        m_lo = sb("m_lo", [128, HEADS, 2, 4], BF16)
        pad_arg = sb("pad_arg", [128, HEADS, 2, 4])
        pad_exp = sb("pad_exp", [128, HEADS, 2, 4])
        pad_hi = sb("pad_hi", [128, HEADS, 2, 4], BF16)
        to_rows = sb("to_rows", [128, 2, 5, GROUP * 8])
        rows_bf = sb("rows_bf", [120, 2, 128], BF16)
        stats = sb("stats", [CHUNK, 4, 6])
        moments = sb("moments", [CHUNK, 2, 2])
        g_mom = sb("g_mom", [CHUNK, 2, 2])
        var_eps = sb("var_eps", [CHUNK, 2])
        rstd = sb("rstd", [CHUNK, 2])
        shift = sb("shift", [CHUNK, 2])
        minus_half = sb("minus_half", [CHUNK, 2])
        qk_dram = nc.dram_tensor(f"{tag}_qk_parts", [3, 384, L], BF16).ap()
        row_dram = nc.dram_tensor(f"{tag}_max_rows", [30, L], BF16).ap()

        work = ps("work", [128, 2, 2, HALF])
        acc = ps("acc", [128, L])
        acc_den = ps("acc_den", [128, L])

        consts_loaded, consts_made = sem("consts_loaded"), sem("consts_made")
        masks_loaded, masks_made = sem("masks_loaded"), sem("masks_made")
        x_loaded, res_loaded, out_stored = sem("x_loaded"), sem("res_loaded"), sem("out_stored")
        filled = sem("filled")
        wait_passed = sem("wait_passed")
        stats_seen = sem("stats_seen")
        drained = [sem(f"drained{i}") for i in range(2)]
        norm_step, rstd_made, xn_made = sem("norm_step"), sem("rstd_made"), sem("xn_made")
        high_made, rest_made, mid_made, low_made = sem("high_made"), sem("rest_made"), sem("mid_made"), sem("low_made")
        part_stored, part_loaded = ([sem(f"{what}{i}") for i in range(3)] for what in ("part_stored", "part_loaded"))
        stacks_copied = sem("stacks_copied")
        max_step, pad_made, small_step = sem("max_step"), sem("pad_made"), sem("small_step")
        rows_made, rows_stored, rows_loaded = sem("rows_made"), sem("rows_stored"), sem("rows_loaded")
        probs_made, probs_used = sem("probs_made"), sem("probs_used")
        group_done, acc_kept = sem("group_done"), sem("acc_kept")
        den_inverted, att_made = sem("den_inverted"), sem("att_made")

        last_pair = batches // 2 - 1

        def is_static(n, v):
            return isinstance(n.it, int) and 2 * n.it + n.s == v

        def has(n, k):
            return not isinstance(n.it, int) or 2 * n.it + n.s + k < batches

        class Use:
            def __init__(self, n, offset):
                self.unit = (A_FILLS * n.s + offset) % 2
                self.number = n.it * (2 * A_FILLS) + (A_FILLS * n.s + offset)
                self.before = n.it * A_FILLS + (A_FILLS * n.s + offset) // 2
                self.none_before = isinstance(self.before, int) and self.before == 0

        ZERO = Batch(0, 0)

        def project_use(n, j):
            return Use(ZERO, 1 + j) if n is None else Use(n, (34 if n.first else 32) + j)

        def a_use(n, i):
            return Use(ZERO, 8 + i) if n is None else Use(n, 53 + i)

        def norm_use(n):
            return Use(ZERO, 0) if n == "start" else Use(ZERO, 32) if n is None else Use(n, 77)

        def rows_use(n):
            return Use(ZERO, 33) if n is None else Use(n, 90 if has(n, 2) else 89)

        def out_use(n_next, i):
            if is_static(n_next, batches):
                return Use(n_next, -2 + i)
            return Use(n_next, (39 if has(n_next, 1) else 31) + i)

        def b_use(n, g, i):
            if not has(n, 1):
                return Use(n, (33, 45)[g] + i)
            return Use(n, (41, 78 if has(n, 2) else 77)[g] + i)

        def await_unit(pe, f):
            if not f.none_before:
                pe.wait_ge(drained[f.unit], f.before)

        def await_all(eng, waits):
            for semaphore, value in waits:
                eng.wait_ge(semaphore, value)
                eng.sem_inc(wait_passed, 1)

        def await_fill(eng, f):
            eng.wait_ge(filled, f.number + 1)

        def await_drained(eng, f):
            eng.wait_ge(drained[f.unit], f.before + 1)

        def after(n):
            return ZERO if n is None else (Batch(n.it, 1) if n.s == 0 else Batch(n.it + 1, 0))

        def before(n):
            return Batch(n.it, 0) if n.s else Batch(n.it - 1, 1)

        def schedule(eng, prologue, main, tail):
            prologue()
            main(Batch(0, 0))
            main(Batch(0, 1))
            if last_pair > 1:
                with eng.Fori(1, last_pair) as it:
                    main(Batch(it, 0))
                    main(Batch(it, 1))
            main(Batch(last_pair, 0))
            main(Batch(last_pair, 1))
            tail(Batch(last_pair + 1, 0))

        def units(i):
            return [divmod(2 * i + k, GROUP) for k in range(2)]

        def image(ap):
            return ap.rearrange("p (s y x) -> p s y x", s=2, x=TILE_W)

        src = x_src.rearrange("b (c p) h w -> b p c (h w)", p=CHUNK)
        dst = x_dst.rearrange("b (c p) h w -> b p c (h w)", p=CHUNK)
        N_CONSTS = 11
        mask_room = (v[1][64:128, :, :].rearrange("p a b -> p (a b)")[:, 0:L],
                     probs[64:128, :, :, :].rearrange("p a b c -> p (a b c)")[:, 0:L])
        den_sel_room = v[1][0:18, 0:2, :].rearrange("p a b -> p (a b)")

        with nc.Block() as block:
            @block.sync
            def _(sp):
                sp.dma_start(x[:, :, :], src[0]).then_inc(x_loaded, 16)
                for t, a in ((w_qk, w["w_qk"]), (w_v, w["w_v"]), (w_o, w["w_o"]), (b_v, w["b_v"]),
                             (qk_bias, w["b_qk"]), (b_o, w["b_o"]), (qk_scale, consts["qk_scale"]),
                             (group_avg, consts["group_avg"]), (ident, consts["ident"]),
                             (floor, consts["floor"]), (ln_pad, consts["ln_pad"])):
                    sp.dma_start(t[:], a).then_inc(consts_loaded, 16)
                sp.dma_start(mask_room[0], consts["masks"][:, 0, :]).then_inc(masks_loaded, 16)
                sp.dma_start(mask_room[1], consts["masks"][:, 1, :]).then_inc(masks_loaded, 16)
                sp.dma_start(den_sel_room, consts["den_sel"]).then_inc(masks_loaded, 16)

                def load(n):
                    sp.dma_start(x[:, :, :], src[n.count(1, 0)]).then_inc(x_loaded, 16)

                def load_residual(n):
                    sp.dma_start(x_res[:, :, :], src[n.count(1, 0)]).then_inc(res_loaded, 16)

                def move_parts(n):
                    m = after(n)
                    q, k = 0, 1
                    for part, (t, made, k_made, places) in enumerate((
                            (qk1, high_made, 3, ((0, q_a, q), (0, k_a, k))),
                            (qk2, mid_made, 1, ((64, q_a, q), (32, k_a, k))),
                            (qk3, low_made, 3, ((32, q_b, q), (0, k_b, k))))):
                        if n is not None:
                            sp.wait_ge(part_loaded[part], m.count(64, 0))
                        sp.wait_ge(made, m.count(k_made, k_made))
                        sp.dma_start(qk_dram[part].rearrange("(t p) c -> p t c", p=128), t[:, :, :]).then_inc(part_stored[part], 16)
                        sp.wait_ge(part_stored[part], m.count(16, 16))
                        if part == 0 and n is not None and not n.first:
                            sp.wait_ge(group_done, before(n).count(2, 2))
                        for base, out, side in places:
                            for first_row, h0, h1 in ((0 + 128 * side, 0, 4), (256 + 64 * side, 4, 6)):
                                rows = qk_dram[part, first_row:first_row + (h1 - h0) * HEAD, :].rearrange("(h d) t -> d h t", d=HEAD)
                                sp.dma_start(out[m.s][base:base + 32, h0:h1, :], rows).then_inc(part_loaded[part], 16)

                def move_rows(n):
                    m = after(n)
                    await_all(sp, [(rows_made, m.count(1, 1))] + ([(rows_loaded, m.count(32, 0)), (group_done, m.count(2, 0))]
                                                                  if n is not None else []))
                    for g in range(2):
                        sp.dma_start(row_dram[:, :].rearrange("(a h) (t c) -> h a t c", h=HEADS, c=128)[GROUP * g:GROUP * (g + 1)]
                                     .rearrange("h a t c -> a h t c"),
                                     rows_bf[:, g, :]).then_inc(rows_stored, 16)
                    sp.wait_ge(rows_stored, m.count(32, 32))
                    sp.dma_start(q_b[m.s][112:114, :, :], row_dram[0:12, :].rearrange("(a h) t -> a h t", a=2)).then_inc(rows_loaded, 16)
                    sp.dma_start(pad_rows[:, :], row_dram[12:30, :]).then_inc(rows_loaded, 16)

                def store(n_next):
                    await_all(sp, [(drained[f.unit], f.before + 1) for f in (out_use(n_next, 0), out_use(n_next, 1))])
                    sp.dma_start(dst[n_next.count(1, -1)], x_res[:, :, :]).then_inc(out_stored, 16)
                    sp.wait_ge(out_stored, n_next.count(16, 0))

                def prologue():
                    load_residual(ZERO)
                    sp.wait_ge(xn_made, 1)
                    load(Batch(0, 1))
                    move_parts(None)
                    move_rows(None)

                def main(n):
                    if has(n, 2):
                        sp.wait_ge(xn_made, n.count(1, 2))
                        load(Batch(n.it + 1, n.s))
                    if has(n, 1):
                        move_parts(n)
                    if not n.first:
                        store(n)
                        load_residual(n)
                    if has(n, 1):
                        move_rows(n)

                schedule(sp, prologue, main, store)

            @block.tensor
            def _(pe):
                def norm(n):
                    f = norm_use(n)
                    await_unit(pe, f)
                    pe.wait_ge(norm_step, (ZERO if n == "start" else Batch(0, 1) if n is None else Batch(n.it + 1, n.s)).count(7, 3))
                    nc.tensor.matmul(work[0:CHUNK, f.unit, 0, 0:4], group_avg[:, :],
                                     moments[:, :, :].rearrange("p a b -> p (a b)"), start=True,
                                     stop=True).then_inc(filled, 1)

                def project(n):
                    m = after(n)
                    pe.wait_ge(xn_made, m.count(1, 1))
                    for j in range(3):
                        f = project_use(n, j)
                        await_unit(pe, f)
                        for half in range(2):
                            for c in range(2):
                                last = nc.tensor.matmul(work[:, f.unit, half, :], w_qk[:, c, 128 * j:128 * (j + 1)],
                                                        xn[:, c, half * HALF:(half + 1) * HALF],
                                                        start=(c == 0), stop=(c == 1))
                        last.then_inc(filled, 1)
                    for j in range(4):
                        f = project_use(n, 3 + j)
                        await_unit(pe, f)
                        for i in range(2):
                            for c in range(2):
                                last = nc.tensor.matmul(work[:, f.unit, i, 0:192], xn[:, c, tile_at(TILES[2 * j + i])], w_v[:, c, :],
                                                        start=(c == 0), stop=(c == 1))
                        last.then_inc(filled, 1)

                def scores(f, m, g, i, on_a, on_b, off_a, off_b, rows):
                    await_unit(pe, f)
                    for k, (ti, hh) in enumerate(units(i)):
                        tx = TILES[ti][1]
                        head = GROUP * g + hh
                        r0, r1, own, size, cols = halo(TILES[ti])
                        out = work[:, f.unit, k, :]
                        for part in range(2):
                            for on, off, r, first in ((on_a, off_a, 128, True), (on_b, off_b, rows, False)):
                                tokens = image(off[m.s][0:r, head, :])
                                last = nc.tensor.matmul(
                                    out[:, 0:own] if part == 0 else out[:, own:size], on[m.s][0:r, head, tile_at(TILES[ti])],
                                    off[m.s][0:r, head, 512 * tx + TILE_W * r0:512 * tx + TILE_W * r1] if part == 0
                                    else tokens[:, 1 - tx, r0:r1, cols], start=first, stop=not first)
                    last.then_inc(filled, 1)

                def pass_a(n):
                    m = after(n)
                    if n is None or n.first:
                        pe.wait_ge(masks_made, 1 if n is None else 2)
                    pe.wait_ge(stacks_copied, m.count(2, 2))
                    pe.wait_ge(part_loaded[2], m.count(64, 64))
                    for i in range(2 * UNIT_PAIRS):
                        scores(a_use(n, i), m, i // UNIT_PAIRS, i % UNIT_PAIRS, q_a, q_b, k_a, k_b, 112)

                def values(n, g, i):
                    slot = i % P_SLOTS
                    pe.wait_ge(probs_made, n.count(24, UNIT_PAIRS * g + i + 1))
                    for part in range(2):
                        for k, (ti, hh) in enumerate(units(i)):
                            tx = TILES[ti][1]
                            r0, r1, own, size, cols = halo(TILES[ti])
                            head = GROUP * g + hh
                            p = probs[:, slot, k, 0:own] if part == 0 else \
                                probs[:, slot, k, own:size].rearrange("p (y x) -> p y x", x=PAD)
                            for to, rows, by in ((acc, quadrant(hh), v[n.s][:, ti, HEAD * head:HEAD * (head + 1)]),
                                                 (acc_den, quadrant(DEN_AT[hh]), ones[:, :])):
                                out = to[rows, 512 * tx + TILE_W * r0:512 * tx + TILE_W * r1] if part == 0 else \
                                    image(to[rows, :])[:, 1 - tx, r0:r1, cols]
                                last = nc.tensor.matmul(out, by, p, start=False, stop=(i == UNIT_PAIRS - 1),
                                                        skip_group_check=True)
                    last.then_inc(probs_used, 1)

                def pass_b(n, g):
                    if not (n.first and g == 0):
                        pe.wait_ge(acc_kept, n.count(2, g))
                    if g == 0:
                        pe.wait_ge(rows_loaded, n.count(32, 32))
                        pe.wait_ge(v_made(n)[0], v_made(n)[1])
                    for half in range(2):
                        t = slice(half * HALF, (half + 1) * HALF)
                        nc.tensor.matmul(acc[0:CHUNK, t], den_sel[:, 2, 0:CHUNK], pad_rows[:, t], start=True, stop=False,
                                         skip_group_check=True)
                        nc.tensor.matmul(acc_den[:, t], den_sel[:, g, :], pad_rows[:, t], start=True, stop=False,
                                         skip_group_check=True)
                    for i in range(UNIT_PAIRS + 1):
                        if i < UNIT_PAIRS:
                            scores(b_use(n, g, i), n, g, i, k_a, k_b, q_a, q_b, 114)
                        if i:
                            values(n, g, i - 1)
                    nc.tensor.matmul(acc_den[:, 0:1], den_sel[:, 2, :], pad_rows[:, 0:1], start=False, stop=True,
                                     skip_group_check=True).then_inc(group_done, 1)

                def v_made(n):
                    f = project_use(None if n.first else before(n), 6)
                    return drained[f.unit], f.before + 1

                def project_out(n_next):
                    pe.wait_ge(att_made, n_next.count(2, 0))
                    for co in range(2):
                        f = out_use(n_next, co)
                        await_unit(pe, f)
                        for half in range(2):
                            for ci in range(2):
                                last = nc.tensor.matmul(work[0:CHUNK, f.unit, half, :],
                                                        w_o[:, ci, co * CHUNK:(co + 1) * CHUNK],
                                                        att[:, ci, half * HALF:(half + 1) * HALF],
                                                        start=(ci == 0), stop=(ci == 1))
                        last.then_inc(filled, 1)

                def to_row_layout(n):
                    f = rows_use(n)
                    await_unit(pe, f)
                    pe.wait_ge(max_step, after(n).count(5, 5))
                    for g in range(2):
                        last = nc.tensor.transpose(work[0:120, f.unit, g, 0:128],
                                                   to_rows[:, g, :, :].rearrange("p a b -> p (a b)"), ident[:, :])
                    last.then_inc(filled, 1)

                def prologue():
                    norm("start")
                    project(None)
                    pass_a(None)
                    norm(None)
                    to_row_layout(None)

                def main(n):
                    if has(n, 1):
                        project(n)
                    if not n.first:
                        project_out(n)
                    pass_b(n, 0)
                    if has(n, 1):
                        pass_a(n)
                    if has(n, 2):
                        norm(n)
                    pass_b(n, 1)
                    if has(n, 1):
                        to_row_layout(n)

                pe.wait_ge(consts_loaded, 16 * N_CONSTS)
                pe.wait_ge(consts_made, 2)
                schedule(pe, prologue, main, project_out)

            @block.scalar
            def _(act):
                def normalise(m):
                    act.wait_ge(norm_step, m.count(7, 7))
                    if not m.first:
                        f = project_use(None if is_static(m, 1) else before(before(m)), 6)
                        await_fill(act, f)
                    for c in range(2):
                        last = nc.scalar.activation(image(xn[:, c, :]),
                                                    x[:, c, :].rearrange("p (y s x) -> p s y x", s=2, x=TILE_W), ACT.Identity,
                                                    scale=rstd[:, c:c + 1], bias=shift[:, c:c + 1])
                    last.then_inc(xn_made, 1)

                def take_qk(n):
                    m = after(n)
                    if n is not None:
                        act.wait_ge(low_made, m.count(3, 0))
                        act.wait_ge(part_stored[0], m.count(16, 0))
                        act.wait_ge(part_stored[1], m.count(16, 0))
                    for j in range(3):
                        f = project_use(n, j)
                        await_fill(act, f)
                        whole = work[:, f.unit, :, :].rearrange("p a b -> p (a b)")
                        nc.scalar.activation(qk1[:, j, :], whole, ACT.Identity, scale=qk_scale[:, j:j + 1],
                                             bias=qk_bias[:, j:j + 1]).then_inc(high_made, 1)
                        nc.scalar.activation(qk[:, j, :], whole, ACT.Identity, scale=qk_scale[:, j:j + 1],
                                             bias=qk_bias[:, j:j + 1]).then_inc(drained[f.unit], 1)

                def middle_part(n):
                    act.wait_ge(rest_made, after(n).count(3, 3))
                    nc.scalar.activation(qk2[:, :, :], qk[:, :, :], ACT.Copy).then_inc(mid_made, 1)

                def exps(n, g, i):
                    f = b_use(n, g, i)
                    await_fill(act, f)
                    k = UNIT_PAIRS * g + i
                    if not (n.first and k < P_SLOTS):
                        act.wait_ge(probs_used, n.count(24, k - P_SLOTS + 1))
                    size = halo(TILES[units(i)[0][0]])[3]
                    nc.scalar.activation(probs[:, i % P_SLOTS, :, 0:size], work[:, f.unit, :, 0:size],
                                         ACT.Exp).then_inc(probs_made, 1)
                    act.wait_ge(probs_made, n.count(24, k + 1))
                    act.sem_inc(drained[f.unit], 1)

                def keep_acc(n, g):
                    act.wait_ge(group_done, n.count(2, g + 1))
                    if g == 0 and not n.first:
                        await_fill(act, out_use(n, 1))
                    if not (n.first and g == 0):
                        act.wait_ge(att_made, n.count(2, g))
                    nc.scalar.activation(att[:, g, :], acc[0:CHUNK, :], ACT.Copy)
                    for hh in range(GROUP):
                        last = nc.scalar.activation(den[quadrant(hh), :], acc_den[quadrant(DEN_AT[hh]), :], ACT.Copy)
                    last.then_inc(acc_kept, 1)

                def padding_terms(n):
                    act.wait_ge(max_step, after(n).count(5, 3))
                    nc.scalar.activation(pad_exp[:, :, :, :], pad_arg[:, :, :, :], ACT.Exp).then_inc(pad_made, 1)

                def take_rows(n):
                    f = rows_use(n)
                    await_fill(act, f)
                    if n is not None:
                        act.wait_ge(rows_stored, after(n).count(32, 0))
                    nc.scalar.activation(rows_bf[:, :, :], work[0:120, f.unit, :, 0:128], ACT.Copy).then_inc(rows_made, 1)
                    act.wait_ge(rows_made, after(n).count(1, 1))
                    act.sem_inc(drained[f.unit], 1)

                def prologue():
                    normalise(ZERO)
                    take_qk(None)
                    middle_part(None)
                    padding_terms(None)
                    normalise(Batch(0, 1))
                    take_rows(None)

                def main(n):
                    if has(n, 1):
                        take_qk(n)
                        middle_part(n)
                    for i in range(UNIT_PAIRS):
                        exps(n, 0, i)
                    keep_acc(n, 0)
                    for i in range(UNIT_PAIRS):
                        exps(n, 1, i)
                        if i == 3 and has(n, 1):
                            padding_terms(n)
                        if i == 7 and has(n, 2):
                            normalise(Batch(n.it + 1, n.s))
                    keep_acc(n, 1)
                    if has(n, 1):
                        take_rows(n)

                act.wait_ge(consts_loaded, 16 * N_CONSTS)
                act.wait_ge(consts_made, 2)
                schedule(act, prologue, main, lambda n: None)

            @block.vector
            def _(dve):
                def norm_stats(m):
                    k = m.count(7, 0)
                    dve.wait_ge(x_loaded, m.count(16, 16))
                    for i in range(4):
                        c, half = divmod(i, 2)
                        last = nc.vector.bn_stats(stats[:, i, :], x[:, c, half * HALF:(half + 1) * HALF])
                    last.then_inc(norm_step, 1)
                    dve.wait_ge(norm_step, k + 1)
                    dve.sem_inc(stats_seen, 1)
                    for c in range(2):
                        last = nc.vector.bn_aggr(moments[:, c, :], stats[:, 2 * c:2 * c + 2, :].rearrange("p a b -> p (a b)"))
                    last.then_inc(norm_step, 1)
                    dve.wait_ge(norm_step, k + 2)
                    for c in range(2):
                        last = nc.vector.scalar_tensor_tensor(moments[:, c, 1:2], moments[:, c, 0:1],
                                                              moments[:, c, 0:1], moments[:, c, 1:2], ALU.mult, ALU.add)
                    last.then_inc(norm_step, 1)

                def norm_finish(f, m):
                    k = m.count(7, 0)
                    await_fill(dve, f)
                    nc.vector.tensor_copy(g_mom[:, :, :].rearrange("p a b -> p (a b)"),
                                          work[0:CHUNK, f.unit, 0, 0:4]).then_inc(drained[f.unit], 1)
                    await_drained(dve, f)
                    for c in range(2):
                        last = nc.vector.scalar_tensor_tensor(var_eps[:, c:c + 1], g_mom[:, c, 0:1], g_mom[:, c, 0:1],
                                                              g_mom[:, c, 1:2], ALU.mult, ALU.subtract)
                    last.then_inc(norm_step, 1)
                    dve.wait_ge(norm_step, k + 4)
                    nc.vector.tensor_scalar(var_eps[:, :], var_eps[:, :], -1.0, 1e-5, ALU.mult, ALU.add).then_inc(norm_step, 1)
                    dve.wait_ge(rstd_made, m.count(1, 1))
                    nc.vector.scalar_tensor_tensor(shift[:, :], g_mom[:, :, 0], -1.0, rstd[:, :],
                                                   ALU.mult, ALU.mult).then_inc(norm_step, 2)

                def take_v(n):
                    m = after(n)
                    if n is not None and not n.first:
                        dve.wait_ge(group_done, before(n).count(2, 2))
                    for j in range(4):
                        f = project_use(n, 3 + j)
                        await_fill(dve, f)
                        nc.vector.tensor_tensor(v[m.s][:, 2 * j:2 * j + 2, :], work[:, f.unit, :, 0:192],
                                                b_v[:, None, :].to_broadcast([128, 2, 192]), ALU.add).then_inc(drained[f.unit], 1)

                def copy_stacks(n, part):
                    m = after(n)
                    dve.wait_ge(part_loaded[part], m.count(64, 64))
                    a, b, c, d = (t[m.s] for t in (q_a, k_a, q_b, k_b))
                    for out, to, src_, at in (((a, 32, a, 0), (c, 0, a, 0), (b, 64, b, 0), (d, 32, b, 0)),
                                              ((a, 96, a, 64), (b, 96, b, 32)))[part]:
                        last = nc.vector.tensor_copy(out[to:to + 32, :, :], src_[at:at + 32, :, :])
                    last.then_inc(stacks_copied, 1)

                def maxima(n):
                    m = after(n)
                    for i in range(2 * UNIT_PAIRS):
                        f = a_use(n, i)
                        await_fill(dve, f)
                        size = halo(TILES[units(i % UNIT_PAIRS)[0][0]])[3]
                        nc.vector.tensor_reduce(m_raw[:, 2 * i:2 * i + 2], work[:, f.unit, :, 0:size],
                                                AX.X, ALU.max).then_inc(drained[f.unit], 1)
                    for i in (2 * UNIT_PAIRS - 2, 2 * UNIT_PAIRS - 1):
                        await_drained(dve, a_use(n, i))
                    for g in range(2):
                        for size, rows in ((0, slice(0, 4, 3)), (1, slice(1, 3, 1))):
                            view = lambda t: t[:, GROUP * g:GROUP * (g + 1), :, rows].rearrange("p h x y -> p y x h")
                            last = nc.vector.tensor_tensor(
                                view(m_max),
                                m_raw[:, 24 * g + 12 * size:24 * g + 12 * (size + 1)].rearrange("p (y x h) -> p y x h", y=2, x=2),
                                view(floor), ALU.max)
                    last.then_inc(max_step, 1)
                    dve.wait_ge(max_step, m.count(5, 1))
                    if n is not None:
                        await_fill(dve, rows_use(None if n.first else before(n)))
                    nc.vector.tensor_scalar(m_hi[:], m_max[:], -1.0, None, ALU.mult).then_inc(max_step, 1)
                    dve.wait_ge(max_step, m.count(5, 2))
                    nc.vector.scalar_tensor_tensor(flat(m_lo), flat(m_max), -1.0, flat(m_hi), ALU.mult, ALU.subtract)
                    nc.vector.tensor_tensor(pad_arg[:], m_hi[:], ln_pad[:], ALU.add)
                    nc.vector.tensor_copy(rows4(0), by_group(m_hi)).then_inc(small_step, 1)
                    dve.wait_ge(small_step, m.count(4, 1))
                    nc.vector.tensor_copy(rows4(1), by_group(m_lo))
                    nc.vector.tensor_tensor(pad_arg[:], pad_arg[:], m_lo[:], ALU.add).then_inc(max_step, 1)

                def rows4(part):
                    return to_rows[:, :, part, :]

                def by_group(t):
                    return t[:].rearrange("p (g h) x y -> p g (h x y)", g=2)

                def flat(t):
                    return t[:].rearrange("p a b c -> p (a b c)")

                def split_padding(n):
                    m = after(n)
                    dve.wait_ge(pad_made, m.count(1, 1))
                    nc.vector.tensor_copy(pad_hi[:], pad_exp[:]).then_inc(small_step, 1)
                    dve.wait_ge(small_step, m.count(4, 2))
                    nc.vector.tensor_copy(rows4(2), by_group(pad_hi))
                    nc.vector.tensor_tensor(pad_exp[:], pad_exp[:], pad_hi[:], ALU.subtract).then_inc(small_step, 1)
                    dve.wait_ge(small_step, m.count(4, 3))
                    nc.vector.tensor_copy(pad_hi[:], pad_exp[:]).then_inc(small_step, 1)
                    dve.wait_ge(small_step, m.count(4, 4))
                    nc.vector.tensor_copy(rows4(3), by_group(pad_hi))
                    nc.vector.tensor_tensor(rows4(4), by_group(pad_exp), by_group(pad_hi), ALU.subtract).then_inc(max_step, 2)

                def divide(n, g):
                    dve.wait_ge(acc_kept, n.count(2, g + 1))
                    nc.vector.reciprocal(den[:, :], den[:, :]).then_inc(den_inverted, 1)
                    dve.wait_ge(den_inverted, n.count(2, g + 1))
                    nc.vector.tensor_tensor(att[:, g, :], att[:, g, :], den[:, :], ALU.mult).then_inc(att_made, 1)

                def residual(n_next):
                    dve.wait_ge(res_loaded, n_next.count(16, 0))
                    for co in range(2):
                        f = out_use(n_next, co)
                        await_fill(dve, f)
                        for tx in range(2):
                            old = x_res[:, co, :].rearrange("p (y s x) -> p s y x", s=2, x=TILE_W)[:, tx]
                            last = nc.vector.scalar_tensor_tensor(
                                old, work[0:CHUNK, f.unit, tx, :].rearrange("p (y x) -> p y x", x=TILE_W),
                                b_o[:, co:co + 1], old, ALU.add, ALU.add)
                        last.then_inc(drained[f.unit], 1)

                def mask_rows(i):
                    for head in range(HEADS):
                        nc.vector.tensor_copy(q_b[i][64:128, head, :], mask_room[0])
                        last = nc.vector.tensor_copy(k_b[i][64:128, head, :], mask_room[1])
                    last.then_inc(masks_made, 1)

                def prologue():
                    norm_stats(ZERO)
                    dve.wait_ge(consts_loaded, 16 * N_CONSTS)
                    nc.vector.tensor_tensor(qk_bias[:, :], qk_bias[:, :], qk_scale[:, :], ALU.mult).then_inc(consts_made, 1)
                    norm_finish(norm_use("start"), ZERO)
                    dve.wait_ge(masks_loaded, 48)
                    nc.vector.tensor_copy(den_sel[:, :, :].rearrange("p a b -> p (a b)"), den_sel_room)
                    mask_rows(0)
                    take_v(None)
                    norm_stats(Batch(0, 1))
                    mask_rows(1)
                    copy_stacks(None, 0)
                    copy_stacks(None, 1)
                    maxima(None)
                    norm_finish(norm_use(None), Batch(0, 1))
                    split_padding(None)

                def main(n):
                    if not n.first:
                        divide(before(n), 1)
                    if has(n, 1):
                        take_v(n)
                    if not n.first:
                        residual(n)
                    if has(n, 1):
                        copy_stacks(n, 0)
                    if has(n, 2):
                        norm_stats(Batch(n.it + 1, n.s))
                    if has(n, 1):
                        copy_stacks(n, 1)
                        maxima(n)
                    if has(n, 2):
                        norm_finish(norm_use(n), Batch(n.it + 1, n.s))
                    divide(n, 0)
                    if has(n, 1):
                        split_padding(n)

                def tail(n_next):
                    divide(before(n_next), 1)
                    residual(n_next)

                nc.vector.memset(minus_half[:, :], -0.5)
                nc.vector.memset(ones[:, :], 1.0).then_inc(consts_made, 1)
                schedule(dve, prologue, main, tail)

            @block.gpsimd
            def _(pool):
                def split(n):
                    m = after(n)
                    for j in range(3):
                        await_drained(pool, project_use(n, j))
                        nc.gpsimd.tensor_tensor(qk[:, j, :], qk[:, j, :], qk1[:, j, :], ALU.subtract).then_inc(rest_made, 1)
                    pool.wait_ge(mid_made, m.count(1, 1))
                    if n is not None:
                        pool.wait_ge(part_stored[2], m.count(16, 0))
                    for j in range(3):
                        nc.gpsimd.tensor_tensor(qk3[:, j, :], qk[:, j, :], qk2[:, j, :], ALU.subtract).then_inc(low_made, 1)

                def power(m):
                    pool.wait_ge(norm_step, m.count(7, 5))
                    nc.gpsimd.tensor_tensor(rstd[:, :], var_eps[:, :], minus_half[:, :], ALU.pow).then_inc(rstd_made, 1)

                def prologue():
                    power(ZERO)
                    split(None)
                    power(Batch(0, 1))

                def main(n):
                    if has(n, 1):
                        split(n)
                    if has(n, 2):
                        power(Batch(n.it + 1, n.s))

                pool.wait_ge(consts_made, 1)
                schedule(pool, prologue, main, lambda n: None)


def shape_constants():
    p = np.arange(128)
    out = {}
    out["rep_sel"] = np.stack([(np.arange(96)[:, None] == 32 * j + p[None, :] % 32) for j in range(3)], 1).astype(np.float32)
    out["state_sum"] = (p[:, None] % 32 == np.arange(32)[None, :]).astype(np.float32)
    g = np.arange(96) // 6
    out["group_avg"] = ((g[:, None] == g[None, :]) / 6.0).astype(np.float32)
    row, quad = p % 32, p // 32
    out["bc_sel"] = np.stack([((row[:, None] == (t // 4) * 16 + (t % 4) * 4 + p[None, :] // 32) & (quad[:, None] != 2))
                              for t in range(8)], 1).astype(np.float32)
    BIG = 1e30
    yy, xx = np.divmod(np.arange(1024), 32)
    q_rows, k_rows = np.zeros((128, 1024), np.float32), np.zeros((128, 1024), np.float32)
    for r in range(16):
        q_rows[64 + r] = yy % 16 == r
        d = (yy - r) % 16
        k_rows[64 + r] = np.where(np.minimum(d, 16 - d) <= 3, 0.0, -BIG)
    for r in range(32):
        q_rows[80 + r] = xx == r
        k_rows[80 + r] = np.where(np.abs(xx - r) <= 3, 0.0, -BIG)
    k_rows[112:114] = 1.0
    halves = lambda a: a.reshape(128, 32, 2, 16).transpose(0, 2, 1, 3).reshape(128, 1024)
    out["masks"] = np.stack([halves(q_rows), halves(k_rows)], 1)[64:128]
    out["qk_scale"] = np.stack([np.full(128, 32 ** -0.5), np.ones(128), np.where(p < 64, 32 ** -0.5, 1.0)], 1).astype(np.float32)
    out["ident"] = np.eye(128, dtype=np.float32)
    inside = lambda c: np.minimum(31, c + 3) - np.maximum(0, c - 3) + 1
    y, x = p // 16, p % 16
    padded = np.stack([np.stack([49 - inside(8 * ty + y) * inside(16 * tx + x) for ty in range(4)], 1) for tx in range(2)], 1)
    padded = np.repeat(padded[:, None], 6, 1)
    out["floor"] = np.where(padded > 0, 0.0, -BIG).astype(np.float32)
    out["ln_pad"] = np.where(padded > 0, np.log(np.maximum(padded, 1)), -BIG).astype(np.float32)
    r18, head_at = np.arange(18), 3 - p // 32
    out["den_sel"] = np.concatenate([((r18[:, None] % 6 == 3 * g + head_at[None]) & (head_at[None] < 3)) for g in range(2)]
                                    + [np.zeros((18, 128))], 1).astype(np.float32)
    out["strip_avg"] = ((p[:, None] % 16 == p[None, :] % 16) / 8.0).astype(np.float32)
    r, dx = np.divmod(np.arange(52), 13)
    centre = (dx[:, None] == 6) & (5 + np.arange(6)[None, :] == 6 + r[:, None])
    out["centre"] = np.repeat(centre.astype(np.float32), 192, 1)
    rule = np.zeros((116, 4, 63), np.float32)
    for base in (0, 64):
        rule[base:base + 52] = (r[:, None, None] == np.arange(4)[None, :, None]) & (dx[:, None, None] == np.arange(63)[None, None] - 25)
    out["toeplitz_rule"] = rule.reshape(116, 252)
    return out


def conv_weights(w_large, w_small, *norms):
    def laid(w):
        k = w.shape[-1]
        padded = np.zeros((19, 13, w.shape[0]), w.dtype)
        y0, x0 = 3 + (13 - k) // 2, (13 - k) // 2
        padded[y0:y0 + k, x0:x0 + k] = w[:, 0].transpose(1, 2, 0)
        return np.ascontiguousarray(padded[::-1])
    g, b, m, v = (np.stack(norms[i::4]) for i in range(4))
    rows = np.stack([g, m, b]).reshape(1, -1)
    return {"large": laid(w_large), "small": laid(w_small), "variances": v.reshape(96, 6),
            "scales": np.ascontiguousarray(np.broadcast_to(rows, (128, rows.shape[1])))}


def ssm_weights(W_proj, b_proj, A_log, D, dt_bias, W_out, b_out):
    wt = W_proj.T
    wt = np.concatenate([wt[:, 0:96], wt[:, 384:416], wt[:, 96:192], wt[:, 192:384]], 1)
    return {
        "w_proj": np.ascontiguousarray(wt.reshape(2, 96, 416).transpose(1, 0, 2)),
        "w_out": np.ascontiguousarray(W_out.T.reshape(2, 96, 192).transpose(1, 0, 2)),
        "a_log": np.ascontiguousarray(A_log.reshape(6, 32, 4, 4).transpose(3, 1, 0, 2).reshape(128, 24)),
        "vecs": np.ascontiguousarray(np.concatenate([v.reshape(2, 96).T for v in (b_proj[0:192], b_proj[192:384], dt_bias, D, b_out)], 1)),
        "bc_bias": np.ascontiguousarray(b_proj[384:416].reshape(32, 1)),
    }


def attention_weights(w_qkv, b_qkv, w_proj, b_proj):
    chunks = lambda w: np.ascontiguousarray(w.T.reshape(2, 96, w.shape[0]).transpose(1, 0, 2))
    order = np.concatenate([np.arange(0, 128), np.arange(192, 320), np.arange(128, 192), np.arange(320, 384)])
    return {
        "w_qk": chunks(w_qkv[order]),
        "w_v": chunks(w_qkv[384:576]),
        "w_o": chunks(w_proj),
        "b_v": np.ascontiguousarray(np.broadcast_to(b_qkv[384:576], (128, 192))),
        "b_qk": np.ascontiguousarray(b_qkv[order].reshape(3, 128).T),
        "b_o": np.ascontiguousarray(b_proj.reshape(2, 96).T),
    }


def program(nc, x, out, weights, consts):
    between = [nc.dram_tensor(f"x_after_l{i}", list(x.shape), F32).ap() for i in range(3)]
    conv_layer(nc, "l0", x, between[0], weights["l0"], consts)
    attention(nc, "l1", between[0], between[1], weights["l1"], consts, x.shape[0])
    ssm_layer(nc, "l2", between[1], between[2], weights["l2"], consts, x.shape[0])
    ssm_layer(nc, "l3", between[2], out, weights["l3"], consts, x.shape[0])


def kernel(**inputs):
    import concourse.bacc as bacc
    from concourse.bass_utils import run_bass_kernel_spmd

    a = {name: np.ascontiguousarray(value) for name, value in inputs.items()}
    of = lambda layer, names: [a[f"{layer}_conv_{name}"] for name in names.split()]
    weights = {
        "l0": conv_weights(*of("L0", "w_large w_small g_l b_l m_l v_l g_s b_s m_s v_s g_i b_i m_i v_i")),
        "l1": attention_weights(*of("L1", "w_qkv b_qkv w_proj b_proj")),
        "l2": ssm_weights(*of("L2", "W_proj b_proj A_log D dt_bias W_out b_out")),
        "l3": ssm_weights(*of("L3", "W_proj b_proj A_log D dt_bias W_out b_out")),
    }
    nc = bacc.Bacc("TRN2", target_bir_lowering=False, num_devices=1)
    arrays = {}

    def dram(name, value):
        arrays[name] = value
        return nc.dram_tensor(name, value.shape, mybir.dt.from_np(value.dtype), kind="ExternalInput").ap()

    x = dram("x", a["x"])
    w = {layer: {k: dram(f"{layer}_{k}_in", v) for k, v in named.items()} for layer, named in weights.items()}
    consts = {k: dram(f"const_{k}", v) for k, v in shape_constants().items()}
    out = nc.dram_tensor("out", a["x"].shape, F32, kind="ExternalOutput").ap()
    program(nc, x, out, w, consts)
    return run_bass_kernel_spmd(nc, [arrays], core_ids=[0]).results[0]["out"]
```
